# Optimizing a Trainium2 kernel written in Bass

```python
import numpy as np
import jax
import jax.numpy as jnp

def _softmax(x, axis=-1):
    return jax.nn.softmax(x, axis=axis)

def _gelu(x):
    return jax.nn.gelu(x, approximate=True)

def _silu(x):
    return jax.nn.silu(x)

def _sigmoid(x):
    return jax.nn.sigmoid(x)

def _layernorm(x, axis=-1, eps=1e-05):
    m = jnp.mean(x, axis=axis, keepdims=True)
    v = jnp.var(x, axis=axis, keepdims=True)
    return (x - m) / jnp.sqrt(v + eps)

def _scatter_add(tgt, idx, src, axis=0):
    return tgt.at[idx].add(src)

def _segment_sum(src, seg, n):
    return jax.ops.segment_sum(src, seg, n)
kernel_name = 'mk_metaformer_d2_conv_nchw256_r2_dd0124'

def setup_inputs(seed: int=0):
    np.random.seed(seed)
    _w = jnp.asarray

    def _rec_inputs():
        import jax
        import jax.numpy as jnp
        _gk = jax.random.key(seed)
        x = -0.0002928 + 1 * jax.random.normal(jax.random.fold_in(_gk, 1), (4, 128, 32, 32), jnp.float32)
        return x
    x = _rec_inputs()

    def _L0_conv_setup():
        import jax, jax.numpy as jnp
        import numpy as np
        FS, STRIDE, PAD = (3, 1, 1)

        def _dcnv2(x, offset_w, offset_b, dcn_w):
            fs, stride, pad = (FS, STRIDE, PAD)
            N, C, H, W = x.shape
            out_C = dcn_w.shape[0]
            K2 = fs * fs
            om = jax.lax.conv_general_dilated(x, offset_w, (stride, stride), [(pad, pad), (pad, pad)], dimension_numbers=('NCHW', 'OIHW', 'NCHW')) + offset_b[None, :, None, None]
            Ho, Wo = (om.shape[2], om.shape[3])
            offset = om[:, :2 * K2].reshape(N, K2, 2, Ho, Wo)
            off_y, off_x = (offset[:, :, 0], offset[:, :, 1])
            mask = jax.nn.sigmoid(om[:, 2 * K2:])
            ky, kx = jnp.meshgrid(jnp.arange(fs), jnp.arange(fs), indexing='ij')
            ky = ky.reshape(K2).astype(jnp.float32)
            kx = kx.reshape(K2).astype(jnp.float32)
            base_y = (jnp.arange(Ho, dtype=jnp.float32) * stride - pad)[None, :, None] + ky[:, None, None]
            base_x = (jnp.arange(Wo, dtype=jnp.float32) * stride - pad)[None, None, :] + kx[:, None, None]
            h_im = base_y[None] + off_y
            w_im = base_x[None] + off_x
            y0 = jnp.floor(h_im)
            x0 = jnp.floor(w_im)
            lh, lw = (h_im - y0, w_im - x0)
            xf = x.reshape(N, C, H * W)

            def gather(yi, xi):
                valid = (yi >= 0) & (yi <= H - 1) & (xi >= 0) & (xi <= W - 1)
                yc = jnp.clip(yi, 0, H - 1).astype(jnp.int32)
                xc = jnp.clip(xi, 0, W - 1).astype(jnp.int32)
                idx = (yc * W + xc).reshape(N, -1)
                v = jax.vmap(lambda img, ind: img[:, ind])(xf, idx)
                v = v.reshape(N, C, K2, Ho, Wo)
                return v * valid[:, None].astype(x.dtype)
            hh, hw = (1.0 - lh, 1.0 - lw)
            sampled = (hh * hw)[:, None] * gather(y0, x0) + (hh * lw)[:, None] * gather(y0, x0 + 1) + (lh * hw)[:, None] * gather(y0 + 1, x0) + (lh * lw)[:, None] * gather(y0 + 1, x0 + 1)
            sampled = sampled * mask[:, None]
            wk = dcn_w.reshape(out_C, C, K2)
            return jnp.einsum('nckhw,ock->nohw', sampled, wk)
        key = jax.random.key(seed)
        k1, k2, k3 = jax.random.split(key, 3)
        N, C, H, W = (4, 128, 32, 32)
        out_C = 128
        x = jax.random.normal(k1, (N, C, H, W), jnp.float32)
        offset_w = jax.random.normal(k2, (FS * FS * 3, C, FS, FS), jnp.float32) * 0.01
        offset_b = jnp.zeros((FS * FS * 3,), jnp.float32)
        dcn_w = jax.random.normal(k3, (out_C, C, FS, FS), jnp.float32) * (1.0 / np.sqrt(C * FS * FS))
        return {'x': x, 'offset_w': offset_w, 'offset_b': offset_b, 'dcn_w': dcn_w}
    _L0_conv_all = _L0_conv_setup()
    _L0_conv_in = {k: v for k, v in _L0_conv_all.items() if k in ('offset_w', 'offset_b', 'dcn_w')}
    del _L0_conv_all

    def _L0_ffn_setup():
        import jax, jax.numpy as jnp
        import numpy as np
        B, S, D = (8, 2048, 128)
        H = 4 * D
        CAPACITY = 0.5
        key = jax.random.key(seed)
        ks = jax.random.split(key, 6)
        x = jax.random.normal(ks[0], (B, S, D), dtype=jnp.float32)
        attention_mask = jnp.zeros((B, 1, 1, S), dtype=jnp.float32)
        wr = jax.random.normal(ks[1], (D, 1), dtype=jnp.float32) * 0.02
        br = jnp.zeros((1,), dtype=jnp.float32)
        w1 = jax.random.normal(ks[2], (D, H), dtype=jnp.float32) * 0.02
        b1 = jnp.zeros((H,), dtype=jnp.float32)
        w2 = jax.random.normal(ks[3], (H, D), dtype=jnp.float32) * 0.02
        b2 = jnp.zeros((D,), dtype=jnp.float32)
        return {'x': x, 'attention_mask': attention_mask, 'wr': wr, 'br': br, 'w1': w1, 'b1': b1, 'w2': w2, 'b2': b2}
    _L0_ffn_all = _L0_ffn_setup()
    _L0_ffn_in = {k: v for k, v in _L0_ffn_all.items() if k in ('attention_mask', 'wr', 'br', 'w1', 'b1', 'w2', 'b2')}
    del _L0_ffn_all

    def _L1_conv_setup():
        import jax, jax.numpy as jnp
        import numpy as np
        B, CIN, COUT, H, W, K = (32, 128, 128, 56, 56, 3)
        STRIDE, PAD, DIL = (1, 1, 1)
        SPARSITY = 0.9
        key = jax.random.key(seed)
        kx, kw, km = jax.random.split(key, 3)
        x = jax.random.normal(kx, (B, CIN, H, W), dtype=jnp.float32)
        w = jax.random.normal(kw, (COUT, CIN, K, K), dtype=jnp.float32)
        mask = (jax.random.uniform(km, (COUT, CIN, K, K)) > SPARSITY).astype(jnp.float32)
        w = w * mask
        return {'x': x, 'weight': w}
    _L1_conv_all = _L1_conv_setup()
    _L1_conv_in = {k: v for k, v in _L1_conv_all.items() if k in ('weight',)}
    del _L1_conv_all

    def _L1_ffn_setup():
        import jax, jax.numpy as jnp
        import numpy as np
        B, N, D = (16, 2048, 128)
        NUM_EXPERTS, TOP_K, HEADS = (4, 2, 4)
        N_EDGES = 524288
        LN_EPS = 1e-05

        def _layernorm(x, g, b):
            mu = x.mean(-1, keepdims=True)
            var = ((x - mu) ** 2).mean(-1, keepdims=True)
            return (x - mu) * jax.lax.rsqrt(var + LN_EPS) * g + b

        def _forward(x, edge_index, W_gat, att_src, att_dst, b_gat, ln_gamma, ln_beta, W1, b1, W2, b2):
            Bc, Nc, Dc = x.shape
            M = Bc * Nc
            x_flat = x.reshape(M, Dc)
            h = (x_flat @ W_gat).reshape(M, HEADS, NUM_EXPERTS)
            loops = jnp.arange(M, dtype=edge_index.dtype)
            src = jnp.concatenate([edge_index[0], loops])
            dst = jnp.concatenate([edge_index[1], loops])
            a_src = (h * att_src).sum(-1)
            a_dst = (h * att_dst).sum(-1)
            e = jax.nn.leaky_relu(a_src[src] + a_dst[dst], negative_slope=0.2)
            e_max = jax.ops.segment_max(e, dst, num_segments=M)
            ee = jnp.exp(e - e_max[dst])
            denom = jax.ops.segment_sum(ee, dst, num_segments=M)
            alpha = ee / (denom[dst] + 1e-16)
            msg = h[src] * alpha[:, :, None]
            agg = jax.ops.segment_sum(msg, dst, num_segments=M).reshape(M, HEADS * NUM_EXPERTS) + b_gat
            scores = _layernorm(agg, ln_gamma, ln_beta).reshape(M, HEADS, NUM_EXPERTS).mean(1)
            scores = scores.reshape(Bc, Nc, NUM_EXPERTS)
            topk_s, topk_i = jax.lax.top_k(scores, TOP_K)
            w = jax.nn.softmax(topk_s, axis=-1)
            out = jnp.zeros_like(x)
            for ei in range(NUM_EXPERTS):
                g = jnp.where(topk_i == ei, w, 0.0).sum(-1)
                hh = jax.nn.gelu(x @ W1[ei] + b1[ei], approximate=False)
                out = out + g[..., None] * (hh @ W2[ei] + b2[ei])
            return out
        key = jax.random.key(seed)
        ks = jax.random.split(key, 8)
        s = 0.05
        return {'x': jax.random.normal(ks[0], (B, N, D), jnp.float32), 'W_gat': jax.random.normal(ks[1], (D, HEADS * NUM_EXPERTS), jnp.float32) * s, 'att_src': jax.random.normal(ks[2], (HEADS, NUM_EXPERTS), jnp.float32) * s, 'att_dst': jax.random.normal(ks[3], (HEADS, NUM_EXPERTS), jnp.float32) * s, 'b_gat': jnp.zeros((HEADS * NUM_EXPERTS,), jnp.float32), 'ln_gamma': jnp.ones((HEADS * NUM_EXPERTS,), jnp.float32), 'ln_beta': jnp.zeros((HEADS * NUM_EXPERTS,), jnp.float32), 'W1': jax.random.normal(ks[4], (NUM_EXPERTS, D, 2 * D), jnp.float32) * s, 'b1': jnp.zeros((NUM_EXPERTS, 2 * D), jnp.float32), 'W2': jax.random.normal(ks[5], (NUM_EXPERTS, 2 * D, D), jnp.float32) * s, 'b2': jnp.zeros((NUM_EXPERTS, D), jnp.float32), 'edge_index': jax.random.randint(ks[6], (2, N_EDGES), 0, B * N, jnp.int32)}
    _L1_ffn_all = _L1_ffn_setup()
    _L1_ffn_in = {k: v for k, v in _L1_ffn_all.items() if k in ('W_gat', 'att_src', 'att_dst', 'b_gat', 'ln_gamma', 'ln_beta', 'W1', 'b1', 'W2', 'b2', 'edge_index')}
    del _L1_ffn_all
    return {'x': x, 'L0_conv_offset_w': _L0_conv_in['offset_w'], 'L0_conv_offset_b': _L0_conv_in['offset_b'], 'L0_conv_dcn_w': _L0_conv_in['dcn_w'], 'L0_ffn_attention_mask': _L0_ffn_in['attention_mask'], 'L0_ffn_wr': _L0_ffn_in['wr'], 'L0_ffn_br': _L0_ffn_in['br'], 'L0_ffn_w1': _L0_ffn_in['w1'], 'L0_ffn_b1': _L0_ffn_in['b1'], 'L0_ffn_w2': _L0_ffn_in['w2'], 'L0_ffn_b2': _L0_ffn_in['b2'], 'L1_conv_weight': _L1_conv_in['weight'], 'L1_ffn_W_gat': _L1_ffn_in['W_gat'], 'L1_ffn_att_src': _L1_ffn_in['att_src'], 'L1_ffn_att_dst': _L1_ffn_in['att_dst'], 'L1_ffn_b_gat': _L1_ffn_in['b_gat'], 'L1_ffn_ln_gamma': _L1_ffn_in['ln_gamma'], 'L1_ffn_ln_beta': _L1_ffn_in['ln_beta'], 'L1_ffn_W1': _L1_ffn_in['W1'], 'L1_ffn_b1': _L1_ffn_in['b1'], 'L1_ffn_W2': _L1_ffn_in['W2'], 'L1_ffn_b2': _L1_ffn_in['b2'], 'L1_ffn_edge_index': _L1_ffn_in['edge_index']}

def reference(x, L0_conv_offset_w, L0_conv_offset_b, L0_conv_dcn_w, L0_ffn_attention_mask, L0_ffn_wr, L0_ffn_br, L0_ffn_w1, L0_ffn_b1, L0_ffn_w2, L0_ffn_b2, L1_conv_weight, L1_ffn_W_gat, L1_ffn_att_src, L1_ffn_att_dst, L1_ffn_b_gat, L1_ffn_ln_gamma, L1_ffn_ln_beta, L1_ffn_W1, L1_ffn_b1, L1_ffn_W2, L1_ffn_b2, L1_ffn_edge_index):
    import jax
    import jax.numpy as jnp

    def _L0_conv_ref(x, offset_w, offset_b, dcn_w):
        import jax, jax.numpy as jnp
        import numpy as np
        FS, STRIDE, PAD = (3, 1, 1)

        def _dcnv2(x, offset_w, offset_b, dcn_w):
            fs, stride, pad = (FS, STRIDE, PAD)
            N, C, H, W = x.shape
            out_C = dcn_w.shape[0]
            K2 = fs * fs
            om = jax.lax.conv_general_dilated(x, offset_w, (stride, stride), [(pad, pad), (pad, pad)], dimension_numbers=('NCHW', 'OIHW', 'NCHW')) + offset_b[None, :, None, None]
            Ho, Wo = (om.shape[2], om.shape[3])
            offset = om[:, :2 * K2].reshape(N, K2, 2, Ho, Wo)
            off_y, off_x = (offset[:, :, 0], offset[:, :, 1])
            mask = jax.nn.sigmoid(om[:, 2 * K2:])
            ky, kx = jnp.meshgrid(jnp.arange(fs), jnp.arange(fs), indexing='ij')
            ky = ky.reshape(K2).astype(jnp.float32)
            kx = kx.reshape(K2).astype(jnp.float32)
            base_y = (jnp.arange(Ho, dtype=jnp.float32) * stride - pad)[None, :, None] + ky[:, None, None]
            base_x = (jnp.arange(Wo, dtype=jnp.float32) * stride - pad)[None, None, :] + kx[:, None, None]
            h_im = base_y[None] + off_y
            w_im = base_x[None] + off_x
            y0 = jnp.floor(h_im)
            x0 = jnp.floor(w_im)
            lh, lw = (h_im - y0, w_im - x0)
            xf = x.reshape(N, C, H * W)

            def gather(yi, xi):
                valid = (yi >= 0) & (yi <= H - 1) & (xi >= 0) & (xi <= W - 1)
                yc = jnp.clip(yi, 0, H - 1).astype(jnp.int32)
                xc = jnp.clip(xi, 0, W - 1).astype(jnp.int32)
                idx = (yc * W + xc).reshape(N, -1)
                v = jax.vmap(lambda img, ind: img[:, ind])(xf, idx)
                v = v.reshape(N, C, K2, Ho, Wo)
                return v * valid[:, None].astype(x.dtype)
            hh, hw = (1.0 - lh, 1.0 - lw)
            sampled = (hh * hw)[:, None] * gather(y0, x0) + (hh * lw)[:, None] * gather(y0, x0 + 1) + (lh * hw)[:, None] * gather(y0 + 1, x0) + (lh * lw)[:, None] * gather(y0 + 1, x0 + 1)
            sampled = sampled * mask[:, None]
            wk = dcn_w.reshape(out_C, C, K2)
            return jnp.einsum('nckhw,ock->nohw', sampled, wk)
        return _dcnv2(x, offset_w, offset_b, dcn_w)

    def _L0_ffn_ref(x, attention_mask, wr, br, w1, b1, w2, b2):
        import jax, jax.numpy as jnp
        import numpy as np
        B, S, D = (8, 2048, 128)
        H = 4 * D
        CAPACITY = 0.5
        b, s, d = x.shape
        weights = (jnp.einsum('bsd,do->bso', x, wr) + br)[..., 0]
        k = max(1, int(CAPACITY * s))
        kk = k - 1 if k > 1 else 1
        _, idx = jax.lax.top_k(weights, k)
        sel_idx = idx[:, :kk]
        sel = jnp.take_along_axis(x, sel_idx[:, :, None], axis=1)
        h = jax.nn.gelu(jnp.einsum('bkd,dh->bkh', sel, w1) + b1)
        y = jnp.einsum('bkh,hd->bkd', h, w2) + b2
        w_sel = jnp.take_along_axis(weights, sel_idx, axis=1)
        y = y * w_sel[..., None]
        batch_idx = jnp.arange(b)[:, None]
        processed = jnp.zeros_like(x).at[batch_idx, sel_idx].set(y)
        return processed + x

    def _L1_conv_ref(x, weight):
        import jax, jax.numpy as jnp
        import numpy as np
        B, CIN, COUT, H, W, K = (32, 128, 128, 56, 56, 3)
        STRIDE, PAD, DIL = (1, 1, 1)
        SPARSITY = 0.9
        out = jax.lax.conv_general_dilated(x, weight, window_strides=(STRIDE, STRIDE), padding=[(PAD, PAD), (PAD, PAD)], rhs_dilation=(DIL, DIL), dimension_numbers=('NCHW', 'OIHW', 'NCHW'))
        return out

    def _L1_ffn_ref(x, W_gat, att_src, att_dst, b_gat, ln_gamma, ln_beta, W1, b1, W2, b2, edge_index):
        import jax, jax.numpy as jnp
        import numpy as np
        B, N, D = (16, 2048, 128)
        NUM_EXPERTS, TOP_K, HEADS = (4, 2, 4)
        N_EDGES = 524288
        LN_EPS = 1e-05

        def _layernorm(x, g, b):
            mu = x.mean(-1, keepdims=True)
            var = ((x - mu) ** 2).mean(-1, keepdims=True)
            return (x - mu) * jax.lax.rsqrt(var + LN_EPS) * g + b

        def _forward(x, edge_index, W_gat, att_src, att_dst, b_gat, ln_gamma, ln_beta, W1, b1, W2, b2):
            Bc, Nc, Dc = x.shape
            M = Bc * Nc
            x_flat = x.reshape(M, Dc)
            h = (x_flat @ W_gat).reshape(M, HEADS, NUM_EXPERTS)
            loops = jnp.arange(M, dtype=edge_index.dtype)
            src = jnp.concatenate([edge_index[0], loops])
            dst = jnp.concatenate([edge_index[1], loops])
            a_src = (h * att_src).sum(-1)
            a_dst = (h * att_dst).sum(-1)
            e = jax.nn.leaky_relu(a_src[src] + a_dst[dst], negative_slope=0.2)
            e_max = jax.ops.segment_max(e, dst, num_segments=M)
            ee = jnp.exp(e - e_max[dst])
            denom = jax.ops.segment_sum(ee, dst, num_segments=M)
            alpha = ee / (denom[dst] + 1e-16)
            msg = h[src] * alpha[:, :, None]
            agg = jax.ops.segment_sum(msg, dst, num_segments=M).reshape(M, HEADS * NUM_EXPERTS) + b_gat
            scores = _layernorm(agg, ln_gamma, ln_beta).reshape(M, HEADS, NUM_EXPERTS).mean(1)
            scores = scores.reshape(Bc, Nc, NUM_EXPERTS)
            topk_s, topk_i = jax.lax.top_k(scores, TOP_K)
            w = jax.nn.softmax(topk_s, axis=-1)
            out = jnp.zeros_like(x)
            for ei in range(NUM_EXPERTS):
                g = jnp.where(topk_i == ei, w, 0.0).sum(-1)
                hh = jax.nn.gelu(x @ W1[ei] + b1[ei], approximate=False)
                out = out + g[..., None] * (hh @ W2[ei] + b2[ei])
            return out
        return _forward(x, edge_index, W_gat, att_src, att_dst, b_gat, ln_gamma, ln_beta, W1, b1, W2, b2)

    def _gn(v, G=32, eps=1e-05):
        B_, C_, H_, W_ = v.shape
        g = v.reshape(B_, G, C_ // G, H_, W_)
        m = jnp.mean(g, axis=(2, 3, 4), keepdims=True)
        s = jnp.var(g, axis=(2, 3, 4), keepdims=True)
        return ((g - m) / jnp.sqrt(s + eps)).reshape(v.shape)

    def _ln_c(v, eps=1e-06):
        m = jnp.mean(v, axis=1, keepdims=True)
        s = jnp.var(v, axis=1, keepdims=True)
        return (v - m) / jnp.sqrt(s + eps)

    def _ln_t(v, eps=1e-05):
        m = jnp.mean(v, axis=-1, keepdims=True)
        s = jnp.var(v, axis=-1, keepdims=True)
        return (v - m) / jnp.sqrt(s + eps)

    def _to_tokens(v):
        B_, C_, H_, W_ = v.shape
        return v.reshape(B_, C_, H_ * W_).transpose(0, 2, 1)

    def _from_tokens(t, like):
        B_, C_, H_, W_ = like.shape
        return t.transpose(0, 2, 1).reshape(B_, C_, H_, W_)
    x = x + _L0_conv_ref(_ln_c(x), L0_conv_offset_w, L0_conv_offset_b, L0_conv_dcn_w)
    t = _to_tokens(x)
    t = t + _L0_ffn_ref(_ln_t(t), L0_ffn_attention_mask, L0_ffn_wr, L0_ffn_br, L0_ffn_w1, L0_ffn_b1, L0_ffn_w2, L0_ffn_b2)
    x = _from_tokens(t, x)
    x = x + _L1_conv_ref(_ln_c(x), L1_conv_weight)
    t = _to_tokens(x)
    t = t + _L1_ffn_ref(_ln_t(t), L1_ffn_W_gat, L1_ffn_att_src, L1_ffn_att_dst, L1_ffn_b_gat, L1_ffn_ln_gamma, L1_ffn_ln_beta, L1_ffn_W1, L1_ffn_b1, L1_ffn_W2, L1_ffn_b2, L1_ffn_edge_index)
    x = _from_tokens(t, x)
    return x

_drawn_inputs = setup_inputs


def setup_inputs(seed=0):
    import zlib

    import numpy as np

    out = dict(_drawn_inputs(seed))
    spreads = {'L0_conv_offset_b': (0.0, 0.1),
     'L0_ffn_b1': (0.0, 0.8),
     'L0_ffn_b2': (0.0, 0.8),
     'L1_ffn_b_gat': (0.0, 0.756),
     'L1_ffn_ln_gamma': (1.0, 0.6),
     'L1_ffn_ln_beta': (0.0, 0.8),
     'L1_ffn_b1': (0.0, 0.8),
     'L1_ffn_b2': (0.0, 0.8)}
    factors = {'L0_ffn_wr': 8.0,
     'L0_ffn_w1': 8.0,
     'L0_ffn_w2': 8.0,
     'L1_ffn_W_gat': 4.275,
     'L1_ffn_att_src': 8.0,
     'L1_ffn_att_dst': 8.0,
     'L1_ffn_W1': 3.296,
     'L1_ffn_W2': 3.054}
    for name, (base, spread) in spreads.items():
        noise = np.random.default_rng([zlib.crc32(name.encode()), seed]).standard_normal(out[name].shape)
        drawn = base * np.exp(spread * noise) if base else spread * noise
        out[name] = jnp.asarray(drawn.astype(out[name].dtype))
    for name, factor in factors.items():
        out[name] = (out[name] * factor).astype(out[name].dtype)
    return out
```

```python
from collections import namedtuple
from contextlib import ExitStack

import numpy as np

import concourse.bass as bass
from concourse import mybir

F32 = mybir.dt.float32
BF16 = mybir.dt.bfloat16
I32 = mybir.dt.int32
ALU = mybir.AluOpType
ACT = mybir.ActivationFunctionType
AX_X = mybir.AxisListType.X

P = 128
IMGS = 4
SIDE = 32
POS = SIDE * SIDE
NODES = IMGS * POS
CHUNK = 512
CHUNKS = NODES // CHUNK
TILES = NODES // P
TAPS = 9
HROWS = SIDE // 2
SRC_T = POS // P
PAD = SIDE + 2
GROUP = 4
KEPT = POS // 2 - 1
HID = 4


EDGES = 524288
ECOLS = EDGES // P
FIRST = 32
KEPT1 = ECOLS // FIRST * 8
BATCH = 96
BCHUNKS = 64
KEPT2 = BCHUNKS * 8
ROUND = 16
HALFR = ROUND // 2
MAX_BATCHES = -(-ECOLS // BATCH)
MAX_ROUNDS = ECOLS * P // ROUND
LAST = NODES - 1
NONE = -8192.0
BIG = 1e30
HEADS = 4
EXPERTS = 4
HE = HEADS * EXPERTS
ROW = HE + HEADS
HIS = TILES
PIECE = 16
PIECES = KEPT1 // PIECE // IMGS

LayerNorm = namedtuple("LayerNorm", "eps mean_ready centred squared var_ready std_ready inv_ready spread normed")


def metaformer_kernel(nc, a, out):
    with ExitStack() as ctx:
        def sb(name, shape, dt=F32):
            return ctx.enter_context(nc.sbuf_tensor(name, shape, dt))

        def sem(name):
            return ctx.enter_context(nc.semaphore(name))

        ps = [ctx.enter_context(nc.psum_tensor(f"bank{i}", [P, CHUNK], F32)) for i in range(8)]

        X = sb("X", [P, CHUNKS, CHUNK])
        T = sb("T", [P, CHUNKS, CHUNK])
        wide_buf = sb("wide_buf", [P, SRC_T * TAPS * P + 4 * GROUP * CHUNK])
        scratch = wide_buf[:, 0:SRC_T * TAPS * P]
        RW = scratch[:, 0:NODES].rearrange("p (i c) -> p i c", c=CHUNK)
        YF = scratch[:, NODES:2 * NODES].rearrange("p (i c) -> p i c", c=CHUNK)
        XP = sb("XP", [P, IMGS, PAD, PAD])
        sq = sb("sq", [P, 2, CHUNK])
        dev = sb("dev", [P, TILES])
        inv = sb("inv", [P, TILES])
        ident = sb("ident", [P, P])
        mean_w = sb("mean_w", [P, P])
        eps = sb("eps", [P, 2])
        ones_b = sb("ones_b", [P, P], BF16)
        later = sb("later", [P, P])

        w_off = sb("w_off", [P, TAPS, 64])
        b_off = sb("b_off", [64, 1])
        w_dcn = sb("w_dcn", [P, TAPS * P])
        base = scratch[0:2 * TAPS, 0:POS]
        off_row = scratch[0:2 * TAPS, 1024:1536]
        off_rem = scratch[0:2 * TAPS, 1536:2048]
        off_mid = scratch[0:2 * TAPS, 2048:2304].bitcast(BF16)
        msk_row = scratch[0:TAPS, 2560:3072]
        msk_rem = scratch[0:TAPS, 3072:3584]
        msk_mid = scratch[0:TAPS, 3584:3840].bitcast(BF16)
        shared = sb("shared", [P, 4096])
        split = lambda t: t.bitcast(BF16).rearrange("p (i c) -> p i c", c=CHUNK)
        OFS = split(shared[0:96, 0:2048])
        MSK = split(shared[0:96, 2048:4096])
        sel = sb("sel", [96, 2 * TAPS, P], BF16)
        zero_b = sb("zero_b", [P, CHUNK], BF16)
        neg_x = sb("neg_x", [P, 1])
        neg_y = sb("neg_y", [P, SRC_T])
        YT = scratch[:, :].rearrange("p (t k) -> p t k", t=SRC_T)
        TEN = wide_buf[:, SRC_T * TAPS * P:].rearrange("p (a b c) -> p a b c", a=4, b=GROUP)
        small = sb("small", [P, 3072])
        txm = small[:, 0:1024].rearrange("p (h c) -> p h c", h=2)
        absx = small[:, 1024:2048].rearrange("p (h c) -> p h c", h=2)
        own_img = small[:, 2048:3072]

        wr = sb("wr", [P, 1])
        wr_b = sb("wr_b", [P, P])
        br_b = sb("br_b", [P, 1])
        f_w1 = sb("f_w1", [P, HID * P])
        f_b1 = sb("f_b1", [P, HID])
        f_w2 = sb("f_w2", [P, HID, P])
        f_b2 = sb("f_b2", [P, 1])
        w_col = sb("w_col", [P, IMGS, SRC_T])
        tie = sb("tie", [P, P])
        cmp_b = TEN[:, 0:2, :, :].rearrange("p a b c -> p (a b c)").bitcast(BF16).rearrange("p (t c) -> p t c", t=SRC_T)
        hid = [TEN[:, 2 + h, :, :] for h in range(2)]

        w_conv = sb("w_conv", [P, TAPS, P])

        src_i = TEN[:, 0:2, :, :].rearrange("p a b c -> p (a b c)").bitcast(I32)
        dst_i = TEN[:, 2:4, :, :].rearrange("p a b c -> p (a b c)").bitcast(I32)
        flags = TEN[:, 0:2, :, :].rearrange("p a b c -> p (a b c)")
        code_i = TEN[:, 2:4, :, :].rearrange("p a b c -> p (a b c)").bitcast(I32)
        routed = wide_buf[:, 0:BATCH * P]
        keys = scratch[:, 0:ECOLS]
        listed = scratch[:, ECOLS:2 * ECOLS]
        e_int = sq[:, :, :].bitcast(I32)
        generic = sb("generic", [P, MAX_BATCHES * BATCH])
        batch_k = sb("batch_k", [P, BATCH])
        kept2 = sb("kept2", [P, KEPT2])
        top8 = sb("top8", [P, 8])
        round_k = sb("round_k", [P, ROUND])
        neg_lo = sb("neg_lo", [P, 1])
        counts = sb("counts", [P, 2])
        rest_n = sb("rest_n", [P, BATCH * P // ECOLS])
        counts_max = sb("counts_max", [P, 2])
        num = sb("num", [P, 8], I32)
        N_LEFT, N_A, N_B, N_BATCH, N_EA, N_EB, N_BASE, N_ALL = range(8)
        lane = sb("lane", [P, P])
        lane_b = sb("lane_b", [P, P], BF16)
        lo_b = sb("lo_b", [P, KEPT1], BF16)
        hi_b = sb("hi_b", [P, KEPT1], BF16)
        left_i = sb("left_i", [P, 2, 8], I32)
        left_b = sb("left_b", [P, 2, 8], BF16)
        oh_lo = generic[:, 0:2048].bitcast(BF16).rearrange("p (h c l) -> p h c l", h=2, l=P)
        oh_hi = generic[:, 2048:2560].bitcast(BF16).rearrange("p (h c l) -> p h c l", h=2, l=HIS)
        to_last = sb("to_last", [P, HIS])
        rounds_d = nc.dram_tensor("rounds_d", (MAX_ROUNDS, P, ROUND), F32, kind="Internal").ap()
        table_d = nc.dram_tensor("table_d", (NODES, ROW), F32, kind="Internal").ap()

        w_gat = sb("w_gat", [P, HE])
        att = sb("att", [P, 2, HE])
        gat_v = sb("gat_v", [P, 3, HE])
        table = shared[:, 2048:2688].rearrange("p (t f) -> p t f", f=ROW)
        prod = shared[:, 2688:3200].rearrange("p (t f) -> p t f", f=HE)
        a_dst = sb("a_dst", [P, HIS, HEADS])
        last_row = sb("last_row", [P, ROW])
        s_max = sb("s_max", [P, HIS, HEADS])
        e_max = sb("e_max", [P, HIS, HEADS])
        pen = sb("pen", [P, HIS])
        cand = sb("cand", [P, HIS, HEADS])
        g_idx = sb("g_idx", [P, ROUND], I32)
        g_int = sb("g_int", [P, ROUND], I32)
        g_hi = sb("g_hi", [P, ROUND])
        rows_g = sb("rows_g", [P, 2, HALFR, ROW])
        oh = shared[:, 3200:3456].rearrange("p (k t) -> p k t", t=HIS)
        oh_t = shared[:, 3456:3712].rearrange("p (t k) -> p t k", t=HIS)
        sel_p = shared[:, 0:HALFR * 8 * HIS]
        per_hi = sb("per_hi", [P, 8, HIS])
        got = sb("got", [P, HALFR, 8])
        z = sb("z", [P, HALFR, HEADS])
        vals = sb("vals", [P, HALFR, ROW])
        spread_v = [t[:, 0:GROUP * HIS * ROW].rearrange("p (k f) -> p k f", k=GROUP) for t in (generic, small)]
        pads = XP[:, :, :, :].rearrange("p n r c -> p (n r c)")
        m_w1 = pads[:, 2048:3072].rearrange("p (e h) -> p e h", e=EXPERTS)
        m_b1 = sb("m_b1", [P, EXPERTS, 2])
        m_w2 = pads[:, 3072:4096].rearrange("p (e k d) -> p e k d", e=EXPERTS, k=2)
        m_b2 = sb("m_b2", [P, EXPERTS])
        below = sb("below", [P, EXPERTS, EXPERTS])
        stat = sb("stat", [P, 4, HIS])
        score = sb("score", [P, HIS, EXPERTS])
        gate = sb("gate", [P, HIS, EXPERTS])
        pair = shared[:, 0:1024].rearrange("p (a t f) -> p a t f", a=2, t=HIS)
        mid = pads[:, 0:4 * CHUNK].rearrange("p (a b c) -> p a b c", a=2, b=2)
        y_exp = [scratch[:, 0:NODES], scratch[:, NODES:2 * NODES],
                 TEN[:, 0:2, :, :].rearrange("p a b c -> p (a b c)"), TEN[:, 2:4, :, :].rearrange("p a b c -> p (a b c)")]
        y_exp = [y.rearrange("p (i c) -> p i c", c=CHUNK) for y in y_exp]

        def image(t):
            return t[:, :, :].rearrange("p (n h) c -> p n (h c)", n=IMGS)

        x_in, wa_in, wb_in = sem("x_in"), sem("wa_in"), sem("wb_in")
        made = sem("made")
        padded, pads_used = sem("padded"), sem("pads_used")

        def layer_norm(tag, e):
            return LayerNorm(e, *(sem(f"{tag}_{n}") for n in LayerNorm._fields[1:]))

        ln0, ln1, ln2, ln3 = (layer_norm(f"ln{i}", e) for i, e in enumerate((0, 1, 0, 1)))

        off_ready, off_a, off_hi, off_r, off_m, off_done = (sem(f"off_{n}") for n in ("ready", "row", "hi", "rem", "mid", "done"))
        msk_cp = sem("msk_cp")
        msk_row_s, msk_hi, msk_r, msk_m, msk_done = (sem(f"msk_{n}") for n in ("row_s", "hi", "rem_s", "mid_s", "done"))
        bc_ready, ax_done, rx_done, txm_done = sem("bc_ready"), sem("ax_done"), sem("rx_done"), sem("txm_done")
        abs_done, relu_done, ten_done, main_done = sem("abs_done"), sem("relu_done"), sem("ten_done"), sem("main_done")
        own_ready = sem("own_ready")
        yt_ready, yt_done, res1 = sem("yt_ready"), sem("yt_done"), sem("res1")
        wrb_done = sem("wrb_done")
        rw_ready, rw_done, diag_done, col_done = sem("rw_ready"), sem("rw_done"), sem("diag_done"), sem("col_done")
        cmp_part, cmp_done, rank_ready, kept_done = sem("cmp_part"), sem("cmp_done"), sem("rank_ready"), sem("kept_done")
        h_ready, gelu_done, y_ready, yf_done = sem("h_ready"), sem("gelu_done"), sem("y_ready"), sem("yf_done")
        fin_a, fin_b, res2 = sem("fin_a"), sem("fin_b"), sem("res2")
        cv_ready, res3 = sem("cv_ready"), sem("res3")
        stored = sem("stored")
        passed, pool_passed, sp_passed = sem("passed"), sem("pool_passed"), sem("sp_passed")
        edges_in, wc_in, wd_in = sem("edges_in"), sem("wc_in"), sem("wd_in")
        e_step, e_chain, counted, reduced, made2 = sem("e_step"), sem("e_chain"), sem("counted"), sem("reduced"), sem("made2")
        left_known, left_coded, left_added, piece_made, piece_added = (sem(n) for n in (
            "left_known", "left_coded", "left_added", "piece_made", "piece_added"))
        codes_made, left_read = sem("codes_made"), sem("left_read")
        batches_known, batch_ready, turned, turned_out, batch_known = (sem(n) for n in (
            "batches_known", "batch_ready", "turned", "turned_out", "batch_known"))
        round_ready, round_stored, rounds_known = sem("round_ready"), sem("round_stored"), sem("rounds_known")
        r2_chain, pieces_done, shares_added = sem("r2_chain"), sem("pieces_done"), sem("shares_added")
        r_chain, rb_chain, b_chain = sem("r_chain"), sem("rb_chain"), sem("b_chain")
        feat_ready, t_chain, table_ready, table_out, last_in = (sem(n) for n in (
            "feat_ready", "t_chain", "table_ready", "table_out", "last_in"))
        key1_in, idx1_ready, rows1_in, max1_done, m1_chain = (sem(n) for n in (
            "key1_in", "idx1_ready", "rows1_in", "max1_done", "m1_chain"))
        key2_in, idx2_ready, rows2_in, got2, exp2, spread2, summed2, m2_chain = (sem(n) for n in (
            "key2_in", "idx2_ready", "rows2_in", "got2", "exp2", "spread2", "summed2", "m2_chain"))
        rows1_b, rows2_b, used2 = sem("rows1_b"), sem("rows2_b"), sem("used2")
        sums_done, f_chain, f_exp, f_ask = sem("sums_done"), sem("f_chain"), sem("f_exp"), sem("f_ask")
        mid_ready, mid_done, my_ready, my_done = sem("mid_ready"), sem("mid_done"), sem("my_ready"), sem("my_done")
        gates_known, gates_ready, gated, gated_b, res4 = (sem(n) for n in ("gates_known", "gates_ready", "gated", "gated_b", "res4"))

        block = ctx.enter_context(nc.Block())

        WA, WB_, WC = 16 * 7, 16 * 8, 16 * 8

        @block.sync
        def _(sp):
            for n in range(IMGS):
                sp.dma_start(image(X)[:, n, :], a["x"][n].rearrange("c h w -> c (h w)")).then_inc(x_in, 16)
            sp.dma_start(w_dcn[:, :], a["w_dcn"]).then_inc(wb_in, 16)
            sp.dma_start(wr[:, :], a["wr"]).then_inc(wb_in, 16)
            sp.dma_start(br_b[:, :], a["br"].partition_broadcast(P)).then_inc(wb_in, 16)
            sp.dma_start(f_w1[:, :], a["f_w1"]).then_inc(wb_in, 16)
            sp.dma_start(f_b1[:, :], a["f_b1"]).then_inc(wb_in, 16)
            sp.dma_start(f_w2[:, :, :], a["f_w2"].rearrange("(c p) d -> p c d", p=P)).then_inc(wb_in, 16)
            sp.dma_start(f_b2[:, :], a["f_b2"].rearrange("(p c) -> p c", c=1)).then_inc(wb_in, 16)
            sp.dma_start(w_conv[:, :, :], a["w_conv"]).then_inc(wb_in, 16)
            sp.dma_start(src_i, a["edges"][0].rearrange("(p c) -> p c", p=P)).then_inc(edges_in, 16)
            sp.dma_start(dst_i, a["edges"][1].rearrange("(p c) -> p c", p=P)).then_inc(edges_in, 16)
            sp.dma_start(w_gat[:, :], a["w_gat"]).then_inc(wc_in, 16)
            for k, name in enumerate(("att_src", "att_dst")):
                sp.dma_start(att[:, k, :], a[name].partition_broadcast(P)).then_inc(wc_in, 16)
            for k, name in enumerate(("b_gat", "ln_gamma", "ln_beta")):
                sp.dma_start(gat_v[:, k, :], a[name].partition_broadcast(P)).then_inc(wc_in, 16)
            sp.dma_start(m_b1[:, :, :], a["m_b1"]).then_inc(wc_in, 16)
            sp.dma_start(m_b2[:, :], a["m_b2"]).then_inc(wc_in, 16)
            sp.wait_ge(batches_known, 1)
            batches = sp.value_load(num[0:1, N_BATCH:N_BATCH + 1], min_val=1, max_val=MAX_BATCHES)
            with sp.Fori(0, batches) as b:
                sp.wait_ge(batch_known, b + 1)
                sp.sem_inc(sp_passed, 1)
                ea = sp.value_load(num[0:1, N_EA:N_EA + 1], min_val=1, max_val=KEPT2 // ROUND)
                eb = sp.value_load(num[0:1, N_EB:N_EB + 1], min_val=0, max_val=(BATCH * P - KEPT2) // ROUND)
                first = sp.value_load(num[0:1, N_BASE:N_BASE + 1], min_val=0, max_val=MAX_ROUNDS - BATCH * P // ROUND)
                with sp.Fori(0, ea) as r:
                    sp.wait_ge(round_ready, first + r + 1)
                    sp.dma_start(rounds_d[bass.ds(first + r, 1)].rearrange("o p s -> (o p) s"), round_k[:, :]).then_inc(round_stored, 16)
                with sp.If(eb > 0):
                    with sp.Fori(0, eb) as r:
                        sp.wait_ge(round_ready, first + ea + r + 1)
                        sp.dma_start(rounds_d[bass.ds(first + ea + r, 1)].rearrange("o p s -> (o p) s"), round_k[:, :]).then_inc(round_stored, 16)
                    sp.nop()
                sp.nop()
            sp.wait_ge(rounds_known, 1)
            total = sp.value_load(num[0:1, N_ALL:N_ALL + 1], min_val=1, max_val=MAX_ROUNDS)
            sp.wait_ge(round_stored, total * 16 + 16)
            sp.wait_ge(cv_ready, CHUNKS)
            sp.dma_start(m_w1[:, :, :], a["m_w1"].rearrange("e c h -> c e h")).then_inc(wd_in, 16)
            sp.dma_start(m_w2[:, :, :, :], a["m_w2"].rearrange("e (k p) d -> p e k d", p=P)).then_inc(wd_in, 16)
            sp.wait_ge(table_ready, 1)
            sp.dma_start(table_d.rearrange("(t p) f -> p t f", p=P), table[:, :, :]).then_inc(table_out, 16)
            sp.wait_ge(table_out, 16)
            sp.dma_start(last_row[:, :], table_d[LAST].partition_broadcast(P)).then_inc(last_in, 16)
            with sp.Fori(0, total) as r:
                sp.wait_ge(idx1_ready, r + 1)
                sp.dma_start(round_k[:, :], rounds_d[bass.ds(r, 1)].rearrange("o p s -> (o p) s")).then_inc(key1_in, 16)
            with sp.Fori(0, total) as r:
                sp.wait_ge(idx2_ready, r + 1)
                sp.dma_start(round_k[:, :], rounds_d[bass.ds(r, 1)].rearrange("o p s -> (o p) s")).then_inc(key2_in, 16)
            sp.wait_ge(res4, CHUNKS)
            for n in range(IMGS):
                sp.dma_start(out[n].rearrange("c h w -> c (h w)"), image(X)[:, n, :]).then_inc(stored, 16)
            sp.wait_ge(stored, 16 * IMGS)

        @block.gpsimd
        def _(pool):
            nc.gpsimd.memset(mean_w[:, :], 1.0 / P).then_inc(made, 1)
            nc.gpsimd.memset(ident[:, :], 0.0).then_inc(made, 1)
            nc.gpsimd.memset(eps[:, 0:1], 1e-6).then_inc(made, 1)
            nc.gpsimd.memset(eps[:, 1:2], 1e-5).then_inc(made, 1)
            nc.gpsimd.memset(w_off[:, :, :], 0.0).then_inc(made, 1)
            pool.wait_ge(made, 5)
            pool.dma_start(w_off[:, :, 0:2 * TAPS], a["w_off"][:, :, 0:2 * TAPS]).then_inc(wa_in, 16)
            pool.dma_start(w_off[:, :, 32:32 + TAPS], a["w_off"][:, :, 2 * TAPS:3 * TAPS]).then_inc(wa_in, 16)
            pool.dma_start(b_off[0:2 * TAPS, :], a["b_off"][0:2 * TAPS].rearrange("(p c) -> p c", c=1)).then_inc(wa_in, 16)
            pool.dma_start(b_off[32:32 + TAPS, :], a["b_off"][2 * TAPS:3 * TAPS].rearrange("(p c) -> p c", c=1)).then_inc(wa_in, 16)
            pool.dma_start(base, a["base"]).then_inc(wa_in, 16)
            pool.dma_start(neg_y[:, :], a["neg_y"]).then_inc(wa_in, 16)
            pool.dma_start(neg_x[:, :], a["neg_x"]).then_inc(wa_in, 16)
            nc.gpsimd.memset(XP[:, :, :, :], 0.0).then_inc(made, 1)
            nc.gpsimd.memset(shared[0:96, 0:2048], 0.0).then_inc(made, 1)
            nc.gpsimd.memset(shared[0:96, 2048:4096], 0.0).then_inc(made, 1)
            nc.gpsimd.memset(sel[:, :, :], 0.0).then_inc(made, 1)
            nc.gpsimd.memset(zero_b[:, :], 0.0).then_inc(made, 1)
            nc.gpsimd.memset(ones_b[:, :], 1.0).then_inc(made, 1)
            nc.gpsimd.memset(later[:, :], 1.0).then_inc(made, 1)
            pool.wait_ge(made, 12)
            for b in range(3):
                nc.gpsimd.affine_select(out=sel[:, :, :], in_=sel[:, :, :], compare_op=ALU.not_equal, fill=1.0,
                                        base=-32 * b, pattern=[[-1, 2 * TAPS], [0, P]],
                                        channel_multiplier=1).then_inc(made, 1)
                pool.wait_ge(made, 13 + b)
            nc.gpsimd.affine_select(out=ident[:, :], in_=ident[:, :], compare_op=ALU.not_equal, fill=1.0, base=0,
                                    pattern=[[-1, P]], channel_multiplier=1).then_inc(made, 1)
            nc.gpsimd.affine_select(out=later[:, :], in_=later[:, :], compare_op=ALU.is_gt, fill=0.0, base=0,
                                    pattern=[[1, P]], channel_multiplier=-1).then_inc(made, 1)
            nc.gpsimd.iota(lane[:, :], [[1, P]], base=0, channel_multiplier=0,
                           allow_small_or_imprecise_dtypes=True).then_inc(made2, 1)
            nc.gpsimd.iota(neg_lo[:, :], [[0, 1]], base=0, channel_multiplier=-(1 << 17),
                           allow_small_or_imprecise_dtypes=True).then_inc(made2, 1)
            nc.gpsimd.memset(below[:, :, :], 1.0).then_inc(made2, 1)
            pool.wait_ge(made2, 3)
            nc.gpsimd.tensor_copy(lane_b[:, :], lane[:, :]).then_inc(made2, 1)
            nc.gpsimd.affine_select(out=below[:, :, :], in_=below[:, :, :], compare_op=ALU.is_gt, fill=0.0, base=0,
                                    pattern=[[1, EXPERTS], [-1, EXPERTS]], channel_multiplier=0).then_inc(made2, 1)
            pool.sem_inc(msk_done, 1)
            for n in range(IMGS):
                for h in range(2):
                    i = 2 * n + h
                    pool.wait_ge(ln0.normed, i + 3)
                    nc.gpsimd.tensor_copy(XP[:, n, 1 + HROWS * h:1 + HROWS * (h + 1), 1:1 + SIDE],
                                          T[:, i, :].rearrange("p (r c) -> p r c", c=SIDE)).then_inc(padded, 1)
            for i in range(CHUNKS):
                pool.wait_ge(msk_row_s, i + 3)
                nc.gpsimd.tensor_copy(MSK[0:TAPS, i, :], msk_row).then_inc(msk_hi, 1)
                pool.wait_ge(msk_hi, i + 1)
                nc.gpsimd.tensor_tensor(msk_rem, msk_row, MSK[0:TAPS, i, :], ALU.subtract).then_inc(msk_r, 1)
                pool.wait_ge(msk_r, i + 1)
                nc.gpsimd.tensor_copy(msk_mid, msk_rem).then_inc(msk_m, 1)
                pool.wait_ge(msk_m, i + 1)
                nc.gpsimd.tensor_copy(MSK[32:32 + TAPS, i, :], msk_mid).then_inc(msk_cp, 1)
                pool.wait_ge(msk_cp, i + 1)
                nc.gpsimd.tensor_tensor(MSK[64:64 + TAPS, i, :], msk_rem, msk_mid, ALU.subtract).then_inc(msk_done, 1)
            pool.wait_ge(msk_done, 1 + CHUNKS)
            pool.wait_ge(counted, 1)
            nc.gpsimd.partition_all_reduce(counts_max[:, :], counts[:, :], P, bass.bass_isa.ReduceOp.max).then_inc(reduced, 1)
            pool.wait_ge(counted, 2)
            nc.gpsimd.partition_all_reduce(counts_max[:, :], counts[:, :], P, bass.bass_isa.ReduceOp.max).then_inc(reduced, 1)
            pool.wait_ge(batches_known, 1)
            batches = pool.value_load(num[0:1, N_BATCH:N_BATCH + 1], min_val=1, max_val=MAX_BATCHES)
            with pool.Fori(0, batches) as b:
                for k in range(2):
                    pool.wait_ge(counted, 2 * b + 3 + k)
                    pool.sem_inc(pool_passed, 1)
                    nc.gpsimd.partition_all_reduce(counts_max[:, :], counts[:, :], P, bass.bass_isa.ReduceOp.max).then_inc(reduced, 1)
            pool.wait_ge(rounds_known, 1)
            pool.wait_ge(made2, 5)
            for n in range(IMGS):
                pool.wait_ge(yt_done, 3 * SRC_T * n + 2)
                nc.gpsimd.tensor_copy(own_img, image(T)[:, n, :]).then_inc(own_ready, 1)
            for n in range(IMGS):
                for h in range(2):
                    i = 2 * n + h
                    pool.wait_ge(ln2.normed, i + 3)
                    nc.gpsimd.tensor_copy(XP[:, n, 1 + HROWS * h:1 + HROWS * (h + 1), 1:1 + SIDE],
                                          T[:, i, :].rearrange("p (r c) -> p r c", c=SIDE)).then_inc(padded, 1)
            total = pool.value_load(num[0:1, N_ALL:N_ALL + 1], min_val=1, max_val=MAX_ROUNDS)
            pool.wait_ge(last_in, 16)
            for idx_ready, used, landed in ((idx1_ready, max1_done, (rows1_in, rows1_b)), (idx2_ready, used2, (rows2_in, rows2_b))):
                with pool.Fori(0, total) as r:
                    pool.wait_ge(idx_ready, r + 2)
                    pool.sem_inc(pool_passed, 1)
                    for half in range(2):
                        pool.wait_ge(used, 2 * r + half + 1)
                        pool.sem_inc(pool_passed, 1)
                        for k in range(HALFR):
                            c = half * HALFR + k
                            pool.indirect_dma_start(rows_g[:, half, k, :], None, table_d,
                                                    bass.IndirectOffsetOnAxis(ap=g_idx[:, c:c + 1], axis=0)).then_inc(landed[half], 16)

        @block.scalar
        def _(act):
            def norm(ln):
                with act.Fori(0, IMGS) as n:
                    for h in range(2):
                        i = 2 * n + h
                        act.wait_ge(ln.centred, i + 3)
                        act.wait_ge(ln.var_ready, i + 1)
                        nc.scalar.activation(sq[:, h, :], T[:, i, :], ACT.Square).then_inc(ln.squared, 1)
                act.wait_ge(ln.var_ready, CHUNKS + 2)
                nc.scalar.activation(dev[:, :], ps[2][:, 0:TILES], ACT.Sqrt, bias=eps[:, ln.eps:ln.eps + 1]).then_inc(ln.std_ready, 1)

            act.wait_ge(made, 5)
            norm(ln0)
            act.sem_inc(msk_row_s, 2)
            act.sem_inc(abs_done, 4)
            act.sem_inc(ax_done, 1)
            act.wait_ge(wa_in, WA)
            with act.Fori(0, IMGS) as n:
                for h in range(2):
                    i = 2 * n + h
                    act.wait_ge(off_ready, i + 1)
                    act.wait_ge(msk_done, i + 1)
                    nc.scalar.activation(msk_row, ps[4 + h][32:32 + TAPS, :], ACT.Sigmoid,
                                         bias=b_off[32:32 + TAPS, :]).then_inc(msk_row_s, 1)
            act.wait_ge(batches_known, 1)
            act.wait_ge(made2, 5)
            batches = act.value_load(num[0:1, N_BATCH:N_BATCH + 1], min_val=1, max_val=MAX_BATCHES)
            act.sem_inc(turned_out, 2)
            with act.Fori(0, batches) as b:
                act.wait_ge(batch_ready, b + 1)
                for q in range(BATCH // 4):
                    act.wait_ge(turned, b * (BATCH // 4) + q + 1)
                    nc.scalar.activation(routed[:, q * CHUNK:(q + 1) * CHUNK], ps[4 + q % 2][:, :], ACT.Relu,
                                         bias=neg_lo[:, :]).then_inc(turned_out, 1)
            act.wait_ge(rounds_known, 1)
            with act.Fori(0, IMGS) as n:
                with act.Fori(0, TAPS) as k:
                    for h in range(2):
                        u = (n * TAPS + k) * 2 + h
                        act.wait_ge(bc_ready, u + 1)
                        act.wait_ge(txm_done, u + 1)
                        nc.scalar.activation(absx[:, h, :], ps[2][:, :], ACT.Abs, bias=neg_x[:, :]).then_inc(ax_done, 1)
                        act.wait_ge(ax_done, u + 2)
                        nc.scalar.activation(absx[:, h, :], absx[:, h, :], ACT.Relu, bias=1.0, scale=-1.0).then_inc(rx_done, 1)
                        for g in range(2):
                            b, v = 2 * h + g, 2 * u + g
                            act.wait_ge(main_done, v + 1)
                            for j in range(GROUP):
                                t = GROUP * g + j
                                last = nc.scalar.activation(TEN[:, b, j, :], ps[h][:, :], ACT.Abs, bias=neg_y[:, t:t + 1])
                            last.then_inc(abs_done, 1)
                            act.wait_ge(abs_done, v + 5)
                            nc.scalar.activation(TEN[:, b, :, :], TEN[:, b, :, :], ACT.Relu, bias=1.0,
                                                 scale=-1.0).then_inc(relu_done, 1)
            norm(ln1)
            act.wait_ge(wb_in, WB_)
            act.sem_inc(gelu_done, 2)
            act.sem_inc(yf_done, 2)
            act.wait_ge(col_done, 1)
            with act.Fori(0, IMGS) as n:
                for h in range(2):
                    i = 2 * n + h
                    for c in range(HID):
                        act.wait_ge(h_ready, HID * i + c + 1)
                        nc.scalar.activation(hid[h][:, c, :], ps[4 + c % 2][:, :], ACT.Gelu_apprx_tanh,
                                             bias=f_b1[:, c:c + 1]).then_inc(gelu_done, 1)
                    act.wait_ge(y_ready, i + 1)
                    nc.scalar.activation(YF[:, i, :], ps[6 + h][:, :], ACT.Identity, bias=f_b2[:, :]).then_inc(yf_done, 1)
            norm(ln2)
            norm(ln3)
            act.wait_ge(wc_in, WC)
            act.sem_inc(mid_done, 2)
            act.sem_inc(my_done, 2)

            def hidden(i, e):
                v = EXPERTS * i + e
                act.wait_ge(my_ready, v + 1)
                for c in range(2):
                    act.wait_ge(mid_ready, 2 * v + c + 1)
                    nc.scalar.activation(mid[:, e % 2, c, :], ps[2 + c][:, :], ACT.Gelu, bias=m_b1[:, e, c:c + 1]).then_inc(mid_done, 1)

            def expert_out(i, e):
                v = EXPERTS * i + e
                act.wait_ge(my_ready, v + 3)
                nc.scalar.activation(y_exp[e][:, i, :], ps[4 + e % 2][:, :], ACT.Identity, bias=m_b2[:, e:e + 1]).then_inc(my_done, 1)

            with act.Fori(0, CHUNKS) as i:
                hidden(i, 0)
                for e in range(1, EXPERTS):
                    hidden(i, e)
                    expert_out(i, e - 1)
                expert_out(i, EXPERTS - 1)
            total = act.value_load(num[0:1, N_ALL:N_ALL + 1], min_val=1, max_val=MAX_ROUNDS)
            with act.Fori(0, total) as r:
                for half in range(2):
                    act.wait_ge(got2, 2 * r + half + 1)
                    nc.scalar.activation(vals[:, :, 0:HEADS], z[:, :, :], ACT.Exp).then_inc(exp2, 1)
            act.wait_ge(f_ask, 1)
            nc.scalar.activation(cand[:, :, :], cand[:, :, :], ACT.Exp).then_inc(f_exp, 1)
            act.wait_ge(f_ask, 2)
            nc.scalar.activation(s_max[:, :, :], s_max[:, :, :], ACT.Exp).then_inc(f_exp, 1)
            act.wait_ge(f_ask, 3)
            nc.scalar.activation(stat[:, 1, :], stat[:, 1, :], ACT.Sqrt, bias=eps[:, 1:2]).then_inc(f_exp, 1)
            act.wait_ge(f_ask, 4)
            nc.scalar.activation(gate[:, :, :], gate[:, :, :], ACT.Exp).then_inc(f_exp, 1)

        @block.vector
        def _(dve):
            def norm(ln, res, credit):
                dve.sem_inc(ln.centred, 2)
                with dve.Fori(0, IMGS) as n:
                    for h in range(2):
                        i = 2 * n + h
                        if res is not None:
                            dve.wait_ge(res, i + credit + 1)
                        dve.wait_ge(ln.mean_ready, i + 1)
                        nc.vector.tensor_tensor(T[:, i, :], X[:, i, :], ps[h][:, :], ALU.subtract).then_inc(ln.centred, 1)
                dve.wait_ge(ln.std_ready, 1)
                nc.vector.reciprocal(inv[:, :], dev[:, :]).then_inc(ln.inv_ready, 1)
                dve.sem_inc(ln.normed, 2)
                with dve.Fori(0, IMGS) as n:
                    for h in range(2):
                        i = 2 * n + h
                        dve.wait_ge(ln.spread, i + 1)
                        nc.vector.tensor_tensor(T[:, i, :], T[:, i, :], ps[6 + h][:, :], ALU.mult).then_inc(ln.normed, 1)

            dve.wait_ge(x_in, 16 * IMGS)
            norm(ln0, None, 0)
            dve.wait_ge(wa_in, WA)
            dve.sem_inc(off_done, 2)
            with dve.Fori(0, IMGS) as n:
                for h in range(2):
                    i = 2 * n + h
                    dve.wait_ge(off_ready, i + 1)
                    dve.wait_ge(off_done, i + 2)
                    nc.vector.scalar_tensor_tensor(off_row, ps[4 + h][0:2 * TAPS, :], b_off[0:2 * TAPS, :],
                                                   base[:, h * CHUNK:(h + 1) * CHUNK], ALU.add, ALU.add).then_inc(off_a, 1)
                    dve.wait_ge(off_a, i + 1)
                    nc.vector.tensor_copy(OFS[0:2 * TAPS, i, :], off_row).then_inc(off_hi, 1)
                    dve.wait_ge(off_hi, i + 1)
                    nc.vector.tensor_tensor(off_rem, off_row, OFS[0:2 * TAPS, i, :], ALU.subtract).then_inc(off_r, 1)
                    dve.wait_ge(off_r, i + 1)
                    nc.vector.tensor_copy(off_mid, off_rem).then_inc(off_m, 1)
                    dve.wait_ge(off_m, i + 1)
                    nc.vector.tensor_copy(OFS[32:32 + 2 * TAPS, i, :], off_mid)
                    nc.vector.tensor_tensor(OFS[64:64 + 2 * TAPS, i, :], off_rem, off_mid, ALU.subtract).then_inc(off_done, 1)
            def chained(s_, first=0, apart=False):
                n = [0]

                def run(ins):
                    n[0] += 1
                    ins.then_inc(s_, 1)
                    dve.wait_ge(s_, first + n[0])
                    if apart:
                        dve.sem_inc(passed, 1)
                return run, n

            dve.wait_ge(edges_in, 32)
            dve.wait_ge(msk_done, 1 + CHUNKS)
            dve.wait_ge(made2, 5)
            KEY_STEPS = 18
            with dve.Fori(0, ECOLS // CHUNK) as q:
                run, n = chained(e_step, q * KEY_STEPS)
                s_in, d_in, key = src_i[:, bass.ts(q, CHUNK)], dst_i[:, bass.ts(q, CHUNK)], keys[:, bass.ts(q, CHUNK)]
                tA, tB, tC, tD = txm[:, 0, :], txm[:, 1, :], absx[:, 0, :], absx[:, 1, :]
                iA, iB = e_int[:, 0, :], e_int[:, 1, :]
                run(nc.vector.tensor_scalar(tA, s_in, 0.0, float(NODES), ALU.is_lt, ALU.mult))
                run(nc.vector.tensor_tensor(tA, tA, s_in, ALU.add))
                run(nc.vector.tensor_scalar(tA, tA, 0.0, float(LAST), ALU.max, ALU.min))
                run(nc.vector.tensor_scalar(iA, d_in, 0.0, float(LAST), ALU.max, ALU.min))
                run(nc.vector.tensor_scalar(tD, iA, -1.0, -1.0, ALU.mult, ALU.add))
                run(nc.vector.tensor_scalar(iB, iA, P - 1, 17, ALU.bitwise_and, ALU.logical_shift_left))
                run(nc.vector.tensor_scalar(iA, iA, 7, 12, ALU.logical_shift_right, ALU.logical_shift_left))
                run(nc.vector.tensor_tensor(tB, iA, iB, ALU.add))
                run(nc.vector.scalar_tensor_tensor(tB, tA, 1.0, tB, ALU.add, ALU.add))
                run(nc.vector.tensor_scalar(tC, tA, float(LAST), None, ALU.is_lt))
                run(nc.vector.tensor_tensor(tB, tB, tC, ALU.mult))
                run(nc.vector.scalar_tensor_tensor(tD, tC, 0.5, tD, ALU.is_lt, ALU.mult))
                run(nc.vector.tensor_tensor(tB, tB, tD, ALU.add))
                run(nc.vector.tensor_scalar(tC, d_in, 0.0, None, ALU.is_ge))
                run(nc.vector.scalar_tensor_tensor(tC, d_in, float(LAST), tC, ALU.is_le, ALU.mult))
                run(nc.vector.tensor_tensor(tB, tB, tC, ALU.mult))
                run(nc.vector.tensor_scalar(tC, tC, 1.0, -NONE, ALU.subtract, ALU.mult))
                run(nc.vector.tensor_tensor(key, tB, tC, ALU.add))
                assert n[0] == KEY_STEPS
            run, _ = chained(e_chain)
            run(nc.vector.memset(listed, NONE))
            for c in range(ECOLS // FIRST):
                last = nc.vector.max(listed[:, 8 * c:8 * c + 8], keys[:, FIRST * c:FIRST * (c + 1)])
            run(last)
            for c in range(ECOLS // FIRST):
                part = keys[:, FIRST * c:FIRST * (c + 1)]
                last = nc.vector.match_replace(part, listed[:, 8 * c:8 * c + 8], part, NONE)
            run(last)
            run(nc.vector.memset(counts[:, :], 0.0))
            run(nc.vector.tensor_scalar(flags, keys, NONE + 1, None, ALU.is_gt))
            run(nc.vector.tensor_reduce(counts[:, 0:1], flags, AX_X, ALU.add))
            dve.sem_inc(counted, 1)
            dve.wait_ge(reduced, 1)
            run(nc.vector.tensor_scalar(num[:, N_LEFT:N_LEFT + 1], counts_max[:, 0:1], 7.0, None, ALU.add))
            run(nc.vector.tensor_scalar(num[:, N_LEFT:N_LEFT + 1], num[:, N_LEFT:N_LEFT + 1], 3, None, ALU.logical_shift_right))
            run(nc.vector.tensor_scalar(num[:, N_LEFT:N_LEFT + 1], num[:, N_LEFT:N_LEFT + 1], 1.0, None, ALU.max))
            lefts = dve.value_load(num[0:1, N_LEFT:N_LEFT + 1], min_val=1, max_val=(ECOLS - KEPT1) // 8)
            dve.sem_inc(left_known, 1)
            with dve.Fori(0, lefts) as r:
                step, _ = chained(r_chain, r * 3, True)
                step(nc.vector.max(top8[:, :], keys))
                step(nc.vector.tensor_copy(listed[:, bass.ds(KEPT1 + 8 * r, 8)], top8[:, :]))
                step(nc.vector.match_replace(keys, top8[:, :], keys, NONE))
            code = code_i[:, 0:KEPT1]
            run(nc.vector.tensor_scalar(code, listed[:, 0:KEPT1], -1.0, -1.0, ALU.mult, ALU.add))
            run(nc.vector.tensor_scalar(code_i[:, KEPT1:2 * KEPT1], code, P - 1, None, ALU.bitwise_and))
            run(nc.vector.tensor_copy(lo_b[:, :], code_i[:, KEPT1:2 * KEPT1]))
            run(nc.vector.tensor_scalar(code, code, 7, None, ALU.arith_shift_right))
            run(nc.vector.tensor_copy(hi_b[:, :], code))
            with dve.Fori(0, lefts) as r:
                step, _ = chained(left_coded, r * 7)
                step(nc.vector.tensor_scalar(left_i[:, 0, :], listed[:, bass.ds(KEPT1 + 8 * r, 8)], -1.0, -1.0, ALU.mult, ALU.add))
                step(nc.vector.tensor_scalar(left_i[:, 1, :], left_i[:, 0, :], P - 1, None, ALU.bitwise_and))
                step(nc.vector.tensor_scalar(left_i[:, 0, :], left_i[:, 0, :], 7, None, ALU.arith_shift_right))
                step(nc.vector.tensor_copy(left_b[:, 0, :], left_i[:, 0, :]))
                step(nc.vector.tensor_copy(left_b[:, 1, :], left_i[:, 1, :]))
                dve.wait_ge(left_added, r + 1)
                step(nc.vector.tensor_tensor(oh_lo[:, 0, 0:8, :], left_b[:, 1, :].unsqueeze(2).to_broadcast([P, 8, P]),
                                             lane_b[:, :].unsqueeze(1).to_broadcast([P, 8, P]), ALU.is_equal))
                step(nc.vector.tensor_tensor(oh_hi[:, 0, 0:8, :], left_b[:, 0, :].unsqueeze(2).to_broadcast([P, 8, HIS]),
                                             lane_b[:, 0:HIS].unsqueeze(1).to_broadcast([P, 8, HIS]), ALU.is_equal))
            dve.wait_ge(left_added, lefts + 1)
            run(nc.vector.tensor_copy(to_last[:, :], ps[7][:, 0:HIS]))
            run(nc.vector.memset(generic[:, :], 0.0))
            run(nc.vector.tensor_scalar(keys, listed, 0.0, None, ALU.max))
            run(nc.vector.tensor_scalar(flags, keys, 0.5, None, ALU.is_gt))
            run(nc.vector.tensor_reduce(counts[:, 0:1], flags[:, 0:KEPT1], AX_X, ALU.add))
            run(nc.vector.tensor_reduce(counts[:, 1:2], flags[:, KEPT1:ECOLS], AX_X, ALU.add))
            dve.sem_inc(counted, 1)
            dve.wait_ge(reduced, 2)
            ab = num[:, N_A:N_B + 1]
            run(nc.vector.tensor_scalar(ab, counts_max[:, :], 7.0, None, ALU.add))
            run(nc.vector.tensor_scalar(ab, ab, 3, None, ALU.logical_shift_right))
            run(nc.vector.tensor_scalar(num[:, N_A:N_A + 1], num[:, N_A:N_A + 1], 1.0, None, ALU.max))
            run(nc.vector.tensor_tensor(num[:, N_BATCH:N_BATCH + 1], num[:, N_A:N_A + 1], num[:, N_B:N_B + 1], ALU.add))
            run(nc.vector.tensor_scalar(num[:, N_BATCH:N_BATCH + 1], num[:, N_BATCH:N_BATCH + 1], float(BATCH // 8 - 1),
                                        float((1 << 18) // (BATCH // 8) + 1), ALU.add, ALU.mult))
            run(nc.vector.tensor_scalar(num[:, N_BATCH:N_BATCH + 1], num[:, N_BATCH:N_BATCH + 1], 18, None, ALU.logical_shift_right))
            run(nc.vector.memset(num[:, N_ALL:N_ALL + 1], 0))
            in_a = dve.value_load(num[0:1, N_A:N_A + 1], min_val=1, max_val=KEPT1 // 8)
            in_b = dve.value_load(num[0:1, N_B:N_B + 1], min_val=0, max_val=(ECOLS - KEPT1) // 8)
            batches = dve.value_load(num[0:1, N_BATCH:N_BATCH + 1], min_val=1, max_val=MAX_BATCHES)
            dve.sem_inc(batches_known, 1)
            with dve.Fori(0, in_a) as r:
                step, _ = chained(rb_chain, r * 3, True)
                part = keys[:, 0:KEPT1]
                step(nc.vector.max(top8[:, :], part))
                step(nc.vector.tensor_copy(generic[:, bass.ds(8 * r, 8)], top8[:, :]))
                step(nc.vector.match_replace(part, top8[:, :], part, 0.0))
            with dve.If(in_b > 0):
                with dve.Fori(0, in_b) as r:
                    step, _ = chained(rb_chain, (in_a + r) * 3, True)
                    part = keys[:, KEPT1:ECOLS]
                    step(nc.vector.max(top8[:, :], part))
                    step(nc.vector.tensor_copy(generic[:, bass.ds(8 * (in_a + r), 8)], top8[:, :]))
                    step(nc.vector.match_replace(part, top8[:, :], part, 0.0))
                dve.nop()
            BATCH_STEPS = 23
            dve.sem_inc(round_stored, 16)
            with dve.Fori(0, batches) as b:
                run, n = chained(b_chain, b * BATCH_STEPS, True)
                run(nc.vector.tensor_copy(batch_k[:, :], generic[:, bass.ds(b * BATCH, BATCH)]))
                dve.sem_inc(batch_ready, 1)
                dve.wait_ge(turned_out, (b + 1) * (BATCH // 4) + 2)
                run(nc.vector.scalar_tensor_tensor(routed, routed, float(1 << 17), routed, ALU.is_le, ALU.mult))
                parts = routed.rearrange("p (s c) -> p c s", c=BCHUNKS)
                for c in range(BCHUNKS):
                    last = nc.vector.max(kept2[:, 8 * c:8 * c + 8], parts[:, c, :])
                run(last)
                fl = wide_buf[:, BATCH * P:BATCH * P + ECOLS]
                run(nc.vector.tensor_scalar(fl[:, 0:KEPT2], kept2[:, :], 0.5, None, ALU.is_gt))
                run(nc.vector.tensor_reduce(counts[:, 0:1], fl[:, 0:KEPT2], AX_X, ALU.add))
                run(nc.vector.tensor_reduce(counts[:, 1:2], kept2[:, :].rearrange("p (c k) -> p c k", k=8)[:, :, 7], AX_X, ALU.max))
                dve.sem_inc(counted, 1)
                dve.wait_ge(reduced, 2 * b + 3)
                dve.sem_inc(passed, 1)
                before = dve.value_load(num[0:1, N_ALL:N_ALL + 1], min_val=0, max_val=MAX_ROUNDS)
                dve.wait_ge(round_stored, before * 16 + 16)
                dve.sem_inc(passed, 1)
                e_ab = num[:, N_EA:N_EB + 1]
                run(nc.vector.tensor_scalar(e_ab, counts_max[:, :], float(ROUND - 1), None, ALU.add))
                run(nc.vector.tensor_scalar(e_ab, e_ab, 4, None, ALU.logical_shift_right))
                run(nc.vector.memset(counts[:, 1:2], 0.0))
                full = dve.value_load(num[0:1, N_EB:N_EB + 1], min_val=0, max_val=(1 << 17) // ROUND)
                with dve.If(full > 0):
                    for c in range(BCHUNKS):
                        last = nc.vector.match_replace(parts[:, c, :], kept2[:, 8 * c:8 * c + 8], parts[:, c, :], 0.0)
                    run(last)
                    for c in range(BATCH * P // ECOLS):
                        run(nc.vector.tensor_scalar(fl, routed[:, c * ECOLS:(c + 1) * ECOLS], 0.5, None, ALU.is_gt))
                        run(nc.vector.tensor_reduce(rest_n[:, c:c + 1], fl, AX_X, ALU.add))
                    run(nc.vector.tensor_reduce(counts[:, 1:2], rest_n[:, :], AX_X, ALU.add))
                with dve.If(full < 1):
                    dve.sem_inc(b_chain, 2 * (BATCH * P // ECOLS) + 2)
                dve.sem_inc(counted, 1)
                dve.wait_ge(reduced, 2 * b + 4)
                dve.sem_inc(passed, 1)
                run(nc.vector.tensor_scalar(num[:, N_EB:N_EB + 1], counts_max[:, 1:2], float(ROUND - 1), None, ALU.add))
                run(nc.vector.tensor_scalar(num[:, N_EB:N_EB + 1], num[:, N_EB:N_EB + 1], 4, None, ALU.logical_shift_right))
                run(nc.vector.tensor_scalar(num[:, N_EA:N_EA + 1], num[:, N_EA:N_EA + 1], 1.0, None, ALU.max))
                run(nc.vector.tensor_copy(num[:, N_BASE:N_BASE + 1], num[:, N_ALL:N_ALL + 1]))
                run(nc.vector.tensor_tensor(num[:, N_ALL:N_ALL + 1], num[:, N_ALL:N_ALL + 1], num[:, N_EA:N_EA + 1], ALU.add))
                run(nc.vector.tensor_tensor(num[:, N_ALL:N_ALL + 1], num[:, N_ALL:N_ALL + 1], num[:, N_EB:N_EB + 1], ALU.add))
                ea = dve.value_load(num[0:1, N_EA:N_EA + 1], min_val=1, max_val=KEPT2 // ROUND)
                eb = dve.value_load(num[0:1, N_EB:N_EB + 1], min_val=0, max_val=(BATCH * P - KEPT2) // ROUND)
                first = dve.value_load(num[0:1, N_BASE:N_BASE + 1], min_val=0, max_val=MAX_ROUNDS - BATCH * P // ROUND)
                dve.sem_inc(batch_known, 1)

                def emit(at, part):
                    step, _ = chained(r2_chain, at * 4, True)
                    dve.wait_ge(round_stored, at * 16 + 16)
                    dve.sem_inc(passed, 1)
                    for k in range(2):
                        step(nc.vector.max(round_k[:, 8 * k:8 * k + 8], part))
                        step(nc.vector.match_replace(part, round_k[:, 8 * k:8 * k + 8], part, 0.0))
                    dve.sem_inc(round_ready, 1)

                with dve.Fori(0, ea) as r:
                    emit(first + r, kept2[:, :])
                with dve.If(eb > 0):
                    with dve.Fori(0, eb) as r:
                        emit(first + ea + r, routed)
                    dve.nop()
                assert n[0] == BATCH_STEPS
                dve.nop()
            dve.sem_inc(rounds_known, 1)
            def weights(n, k, h):
                u = (n * TAPS + k) * 2 + h
                dve.wait_ge(rx_done, u + 1)
                dve.wait_ge(ten_done, 2 * u + 2)
                nc.vector.tensor_tensor(txm[:, h, :], absx[:, h, :], ps[3][:, :], ALU.mult).then_inc(txm_done, 1)
                dve.wait_ge(txm_done, u + 3)
                for g in range(2):
                    b, v = 2 * h + g, 2 * u + g
                    dve.wait_ge(relu_done, v + 1)
                    nc.vector.tensor_tensor(TEN[:, b, :, :], TEN[:, b, :, :],
                                            txm[:, h:h + 1, :].to_broadcast([P, GROUP, CHUNK]), ALU.mult).then_inc(ten_done, 1)

            def one_hot(n, k, h):
                u = PIECES * n + 2 * k + h
                dve.wait_ge(piece_added, u + 1)
                cols = bass.ds(u * PIECE, PIECE)
                nc.vector.tensor_tensor(oh_lo[:, h, :, :], lo_b[:, cols].unsqueeze(2).to_broadcast([P, PIECE, P]),
                                        lane_b[:, :].unsqueeze(1).to_broadcast([P, PIECE, P]), ALU.is_equal)
                nc.vector.tensor_tensor(oh_hi[:, h, :, :], hi_b[:, cols].unsqueeze(2).to_broadcast([P, PIECE, HIS]),
                                        lane_b[:, 0:HIS].unsqueeze(1).to_broadcast([P, PIECE, HIS]), ALU.is_equal).then_inc(piece_made, 1)

            dve.sem_inc(txm_done, 2)
            dve.sem_inc(ten_done, 4)
            dve.sem_inc(shares_added, 1)
            dve.sem_inc(yt_done, 2)
            dve.sem_inc(res1, 2)
            with dve.Fori(0, IMGS) as n:
                dve.wait_ge(main_done, 4 + 4 * TAPS * n)
                for q in range(3 * SRC_T):
                    t, g = divmod(q, 3)
                    w = min(CHUNK, TAPS * P - g * CHUNK)
                    dve.wait_ge(yt_ready, 3 * SRC_T * n + q + 1)
                    nc.vector.tensor_copy(YT[:, t, g * CHUNK:g * CHUNK + w], ps[6 + q % 2][:, 0:w]).then_inc(yt_done, 1)
                with dve.Fori(0, PIECES // 2) as k:
                    for h in range(2):
                        weights(n, k, h)
                        one_hot(n, k, h)
                for k in range(PIECES // 2, TAPS):
                    for h in range(2):
                        weights(n, k, h)
                dve.wait_ge(main_done, 4 + 4 * TAPS * (n + 1))
                dve.wait_ge(piece_added, PIECES * (n + 1) + 2)
                nc.vector.tensor_tensor(to_last[:, :], to_last[:, :], ps[7][:, 0:HIS], ALU.add).then_inc(shares_added, 1)
                for h in range(2):
                    i = 2 * n + h
                    nc.vector.tensor_tensor(X[:, i, :], X[:, i, :], ps[4 + h][:, :], ALU.add).then_inc(res1, 1)
            dve.wait_ge(wb_in, WB_)
            nc.vector.tensor_copy(wr_b[:, :], wr[:, 0:1].to_broadcast([P, P])).then_inc(wrb_done, 1)
            norm(ln1, res1, 2)
            dve.wait_ge(wb_in, WB_)
            dve.sem_inc(rw_done, 2)
            with dve.Fori(0, IMGS) as n:
                for h in range(2):
                    i = 2 * n + h
                    dve.wait_ge(rw_ready, i + 1)
                    nc.vector.tensor_scalar(RW[:, i, :], ps[h][:, :], br_b[:, :], None, ALU.add).then_inc(rw_done, 1)
            dve.wait_ge(rw_done, 2 + CHUNKS)
            nc.vector.tensor_tensor(YF[:, :, :].rearrange("p a (b c) -> p (a b) c", c=P),
                                    RW[:, :, :].rearrange("p a (b c) -> p (a b) c", c=P),
                                    ident[:, :].unsqueeze(1).to_broadcast([P, TILES, P]), ALU.mult).then_inc(diag_done, 1)
            dve.wait_ge(diag_done, 1)
            nc.vector.tensor_reduce(w_col[:, :, :].rearrange("p n t -> p (n t)"),
                                    YF[:, :, :].rearrange("p a (b c) -> p (a b) c", c=P), AX_X, ALU.add).then_inc(col_done, 1)
            dve.wait_ge(col_done, 1)
            dve.sem_inc(rank_ready, 1)
            dve.sem_inc(kept_done, 2)
            with dve.Fori(0, IMGS) as n:
                dve.wait_ge(rank_ready, n + 1)
                rows = image(RW)
                for t in range(SRC_T):
                    own = w_col[:, n, t:t + 1]
                    e = (t + 1) * P
                    nc.vector.tensor_scalar(tie[:, :], rows[:, n, e - P:e], own, None, ALU.is_equal).then_inc(cmp_part, 1)
                    nc.vector.tensor_scalar(cmp_b[:, t, 0:e], rows[:, n, 0:e], own, None, ALU.is_lt).then_inc(cmp_part, 1)
                    if e < POS:
                        nc.vector.tensor_scalar(cmp_b[:, t, e:], rows[:, n, e:], own, None, ALU.is_le)
                    dve.wait_ge(cmp_part, (n * SRC_T + t) * 3 + 2)
                    nc.vector.tensor_tensor(tie[:, :], tie[:, :], later[:, :], ALU.mult).then_inc(cmp_part, 1)
                    dve.wait_ge(cmp_part, (n * SRC_T + t) * 3 + 3)
                    nc.vector.tensor_tensor(cmp_b[:, t, e - P:e], cmp_b[:, t, e - P:e], tie[:, :], ALU.add).then_inc(cmp_done, 1)
                    dve.wait_ge(cmp_done, n * SRC_T + t + 1)
                dve.wait_ge(rank_ready, n + 2)
                for h in range(2):
                    nc.vector.scalar_tensor_tensor(RW[:, 2 * n + h, :], ps[2 + h][:, :], float(KEPT), RW[:, 2 * n + h, :],
                                                   ALU.is_lt, ALU.mult).then_inc(kept_done, 1)
            with dve.Fori(0, CHUNKS) as i:
                dve.wait_ge(yf_done, i + 3)
                dve.wait_ge(kept_done, i + 3)
                nc.vector.tensor_tensor(YF[:, i, :], YF[:, i, :], RW[:, i, :], ALU.mult).then_inc(fin_a, 1)
                dve.wait_ge(fin_a, i + 1)
                nc.vector.tensor_tensor(YF[:, i, :], YF[:, i, :], T[:, i, :], ALU.add).then_inc(fin_b, 1)
                dve.wait_ge(fin_b, i + 1)
                nc.vector.tensor_tensor(X[:, i, :], X[:, i, :], YF[:, i, :], ALU.add).then_inc(res2, 1)
            norm(ln2, res2, 0)
            dve.sem_inc(res3, 2)
            with dve.Fori(0, IMGS) as n:
                for h in range(2):
                    i = 2 * n + h
                    dve.wait_ge(cv_ready, i + 1)
                    nc.vector.tensor_tensor(X[:, i, :], X[:, i, :], ps[4 + h][:, :], ALU.add).then_inc(res3, 1)
            norm(ln3, res3, 2)
            run, _ = chained(t_chain)
            dve.wait_ge(wc_in, WC)
            dve.wait_ge(feat_ready, 1)
            feats = table[:, :, 0:HE]
            run(nc.vector.tensor_copy(feats, ps[0][:, :].rearrange("p (t f) -> p t f", f=HE)))
            for k, o in ((0, table[:, :, HE:ROW]), (1, a_dst[:, :, :])):
                run(nc.vector.tensor_tensor(prod[:, :, :], feats, att[:, k:k + 1, :].to_broadcast([P, HIS, HE]), ALU.mult))
                run(nc.vector.tensor_reduce(o, prod[:, :, :].rearrange("p t (h e) -> p t h e", h=HEADS), AX_X, ALU.add))
                if k == 0:
                    dve.sem_inc(table_ready, 1)
            a_src = table[:, :, HE:ROW]
            run(nc.vector.tensor_scalar(pen[:, :], to_last[:, :], 0.5, -BIG, ALU.is_lt, ALU.mult))
            dve.wait_ge(last_in, 16)
            run(nc.vector.tensor_tensor(cand[:, :, :], pen[:, :].unsqueeze(2).to_broadcast([P, HIS, HEADS]),
                                        last_row[:, HE:ROW].unsqueeze(1).to_broadcast([P, HIS, HEADS]), ALU.add))
            run(nc.vector.tensor_tensor(s_max[:, :, :], cand[:, :, :], a_src, ALU.max))
            total = dve.value_load(num[0:1, N_ALL:N_ALL + 1], min_val=1, max_val=MAX_ROUNDS)

            def decode(step, idx_ready):
                step(nc.vector.tensor_scalar(g_int[:, :], round_k[:, :], -1.0, None, ALU.add))
                step(nc.vector.tensor_scalar(g_idx[:, :], g_int[:, :], LAST, None, ALU.bitwise_and))
                step(nc.vector.tensor_scalar(g_int[:, :], g_int[:, :], 12, None, ALU.arith_shift_right))
                step(nc.vector.tensor_copy(g_hi[:, :], g_int[:, :]))
                dve.sem_inc(idx_ready, 1)

            dve.sem_inc(idx1_ready, 1)
            dve.sem_inc(max1_done, 2)
            lanes = lane[:, 0:HIS]
            M1 = 4 + 2 * 5
            with dve.Fori(0, total) as r:
                step, n = chained(m1_chain, r * M1)
                dve.wait_ge(key1_in, r * 16 + 16)
                decode(step, idx1_ready)
                for half in range(2):
                    hs = g_hi[:, half * HALFR:(half + 1) * HALFR]
                    step(nc.vector.tensor_tensor(oh_t[:, :, :], hs.unsqueeze(1).to_broadcast([P, HIS, HALFR]),
                                                 lanes.unsqueeze(2).to_broadcast([P, HIS, HALFR]), ALU.not_equal))
                    step(nc.vector.tensor_scalar(oh_t[:, :, :], oh_t[:, :, :], -BIG, None, ALU.mult))
                    dve.wait_ge((rows1_in, rows1_b)[half], (r + 1) * 16 * HALFR)
                    grid = sel_p[:, 0:HIS * HEADS * HALFR].rearrange("p (t h k) -> p t h k", t=HIS, h=HEADS)
                    step(nc.vector.tensor_tensor(
                        grid, oh_t[:, :, :].unsqueeze(2).to_broadcast([P, HIS, HEADS, HALFR]),
                        rows_g[:, half, :, HE:ROW].rearrange("p k h -> p h k").unsqueeze(1).to_broadcast([P, HIS, HEADS, HALFR]), ALU.add))
                    dve.sem_inc(max1_done, 1)
                    step(nc.vector.tensor_reduce(cand[:, :, :], grid, AX_X, ALU.max))
                    step(nc.vector.tensor_tensor(s_max[:, :, :], s_max[:, :, :], cand[:, :, :], ALU.max))
                assert n[0] == M1
            run(nc.vector.tensor_tensor(cand[:, :, :], s_max[:, :, :], a_dst[:, :, :], ALU.add))
            run(nc.vector.scalar_tensor_tensor(e_max[:, :, :], cand[:, :, :], 0.2, cand[:, :, :], ALU.mult, ALU.max))
            run(nc.vector.tensor_copy(per_hi[:, 0:HEADS, :], a_dst[:, :, :].rearrange("p t h -> p h t")))
            run(nc.vector.tensor_copy(per_hi[:, HEADS:8, :], e_max[:, :, :].rearrange("p t h -> p h t")))
            dve.sem_inc(idx2_ready, 1)
            dve.sem_inc(used2, 2)
            M2 = 4 + 2 * 8
            with dve.Fori(0, total) as r:
                step, n = chained(m2_chain, r * M2)
                dve.wait_ge(key2_in, r * 16 + 16)
                decode(step, idx2_ready)
                for half in range(2):
                    v = 2 * r + half
                    hs = g_hi[:, half * HALFR:(half + 1) * HALFR]
                    step(nc.vector.tensor_tensor(oh[:, :, :], hs.unsqueeze(2).to_broadcast([P, HALFR, HIS]),
                                                 lanes.unsqueeze(1).to_broadcast([P, HALFR, HIS]), ALU.is_equal))
                    grid = sel_p[:, :].rearrange("p (k f t) -> p k f t", k=HALFR, f=8)
                    step(nc.vector.tensor_tensor(grid, oh[:, :, :].unsqueeze(2).to_broadcast([P, HALFR, 8, HIS]),
                                                 per_hi[:, :, :].unsqueeze(1).to_broadcast([P, HALFR, 8, HIS]), ALU.mult))
                    step(nc.vector.tensor_reduce(got[:, :, :], grid, AX_X, ALU.add))
                    dve.wait_ge((rows2_in, rows2_b)[half], (r + 1) * 16 * HALFR)
                    step(nc.vector.tensor_tensor(z[:, :, :], rows_g[:, half, :, HE:ROW], got[:, :, 0:HEADS], ALU.add))
                    step(nc.vector.scalar_tensor_tensor(z[:, :, :], z[:, :, :], 0.2, z[:, :, :], ALU.mult, ALU.max))
                    step(nc.vector.tensor_tensor(z[:, :, :], z[:, :, :], got[:, :, HEADS:8], ALU.subtract))
                    step(nc.vector.tensor_scalar(z[:, :, :], z[:, :, :], 0.0, None, ALU.min))
                    dve.sem_inc(got2, 1)
                    dve.wait_ge(exp2, v + 1)
                    step(nc.vector.tensor_tensor(
                        vals[:, :, HEADS:ROW].rearrange("p k (h e) -> p k h e", h=HEADS),
                        rows_g[:, half, :, 0:HE].rearrange("p k (h e) -> p k h e", h=HEADS),
                        vals[:, :, 0:HEADS].unsqueeze(3).to_broadcast([P, HALFR, HEADS, EXPERTS]), ALU.mult))
                    dve.sem_inc(used2, 1)
                    for g in range(2):
                        dve.wait_ge(summed2, 2 * v + g + 1)
                        ks = slice(GROUP * g, GROUP * (g + 1))
                        nc.vector.tensor_tensor(spread_v[g].rearrange("p k (t f) -> p k t f", f=ROW),
                                                oh[:, ks, :].unsqueeze(3).to_broadcast([P, GROUP, HIS, ROW]),
                                                vals[:, ks, :].unsqueeze(2).to_broadcast([P, GROUP, HIS, ROW]), ALU.mult).then_inc(spread2, 1)
                    dve.wait_ge(spread2, 2 * v + 2)
                assert n[0] == M2
            run(nc.vector.tensor_tensor(cand[:, :, :], a_src, a_dst[:, :, :], ALU.add))
            run(nc.vector.scalar_tensor_tensor(cand[:, :, :], cand[:, :, :], 0.2, cand[:, :, :], ALU.mult, ALU.max))
            run(nc.vector.tensor_tensor(cand[:, :, :], cand[:, :, :], e_max[:, :, :], ALU.subtract))
            dve.sem_inc(f_ask, 1)
            run(nc.vector.tensor_tensor(s_max[:, :, :], a_dst[:, :, :],
                                        last_row[:, HE:ROW].unsqueeze(1).to_broadcast([P, HIS, HEADS]), ALU.add))
            run(nc.vector.scalar_tensor_tensor(s_max[:, :, :], s_max[:, :, :], 0.2, s_max[:, :, :], ALU.mult, ALU.max))
            run(nc.vector.tensor_tensor(s_max[:, :, :], s_max[:, :, :], e_max[:, :, :], ALU.subtract))
            run(nc.vector.tensor_scalar(s_max[:, :, :], s_max[:, :, :], 0.0, None, ALU.min))
            dve.sem_inc(f_ask, 1)
            dve.wait_ge(f_exp, 2)
            run(nc.vector.tensor_tensor(s_max[:, :, :], s_max[:, :, :], to_last[:, :].unsqueeze(2).to_broadcast([P, HIS, HEADS]), ALU.mult))
            acc = spread_v[0][:, 0, :].rearrange("p (t f) -> p t f", f=ROW)
            dve.wait_ge(summed2, total * 4 + 2)
            for b in range(2):
                run(nc.vector.tensor_copy(acc[:, b * (HIS // 2):(b + 1) * (HIS // 2), :],
                                          ps[b][:, 0:HIS // 2 * ROW].rearrange("p (t f) -> p t f", f=ROW)))
            den, agg = acc[:, :, 0:HEADS], acc[:, :, HEADS:ROW]
            by_head = lambda t: t.rearrange("p t (h e) -> p t h e", h=HEADS)
            for w, f in ((cand, feats), (s_max, last_row[:, 0:HE].unsqueeze(1).to_broadcast([P, HIS, HE]))):
                run(nc.vector.tensor_tensor(den, den, w[:, :, :], ALU.add))
                run(nc.vector.tensor_tensor(by_head(prod[:, :, :]), by_head(f), w[:, :, :].unsqueeze(3).to_broadcast([P, HIS, HEADS, EXPERTS]), ALU.mult))
                run(nc.vector.tensor_tensor(agg, agg, prod[:, :, :], ALU.add))
            run(nc.vector.tensor_scalar(cand[:, :, :], den, 1e-16, None, ALU.add))
            run(nc.vector.reciprocal(cand[:, :, :], cand[:, :, :]))
            run(nc.vector.tensor_tensor(by_head(prod[:, :, :]), by_head(agg), cand[:, :, :].unsqueeze(3).to_broadcast([P, HIS, HEADS, EXPERTS]), ALU.mult))
            row = lambda k: gat_v[:, k:k + 1, :].to_broadcast([P, HIS, HE])
            wide = lambda k, w=HE: stat[:, k, :].unsqueeze(2).to_broadcast([P, HIS, w])
            run(nc.vector.tensor_tensor(prod[:, :, :], prod[:, :, :], row(0), ALU.add))
            run(nc.vector.tensor_reduce(stat[:, 0, :], prod[:, :, :], AX_X, ALU.add))
            run(nc.vector.tensor_scalar(stat[:, 0, :], stat[:, 0, :], 1.0 / HE, None, ALU.mult))
            run(nc.vector.tensor_tensor(prod[:, :, :], prod[:, :, :], wide(0), ALU.subtract))
            run(nc.vector.tensor_tensor(agg, prod[:, :, :], prod[:, :, :], ALU.mult))
            run(nc.vector.tensor_reduce(stat[:, 1, :], agg, AX_X, ALU.add))
            run(nc.vector.tensor_scalar(stat[:, 1, :], stat[:, 1, :], 1.0 / HE, None, ALU.mult))
            dve.sem_inc(f_ask, 1)
            dve.wait_ge(f_exp, 3)
            run(nc.vector.reciprocal(stat[:, 1, :], stat[:, 1, :]))
            run(nc.vector.tensor_tensor(prod[:, :, :], prod[:, :, :], wide(1), ALU.mult))
            run(nc.vector.tensor_tensor(prod[:, :, :], prod[:, :, :], row(1), ALU.mult))
            run(nc.vector.tensor_tensor(prod[:, :, :], prod[:, :, :], row(2), ALU.add))
            run(nc.vector.tensor_reduce(score[:, :, :], prod[:, :, :].rearrange("p t (h e) -> p t e h", h=HEADS), AX_X, ALU.add))
            run(nc.vector.tensor_scalar(score[:, :, :], score[:, :, :], 1.0 / HEADS, None, ALU.mult))
            square = lambda k: pair[:, k, :, :].rearrange("p t (i j) -> p t i j", i=EXPERTS)
            other = score[:, :, :].unsqueeze(2).to_broadcast([P, HIS, EXPERTS, EXPERTS])
            mine = score[:, :, :].unsqueeze(3).to_broadcast([P, HIS, EXPERTS, EXPERTS])
            run(nc.vector.tensor_tensor(square(0), other, mine, ALU.is_gt))
            run(nc.vector.tensor_tensor(square(1), other, mine, ALU.is_equal))
            run(nc.vector.tensor_tensor(pair[:, 1, :, :], pair[:, 1, :, :],
                                        below[:, :, :].rearrange("p i j -> p (i j)").unsqueeze(1).to_broadcast([P, HIS, EXPERTS * EXPERTS]), ALU.mult))
            run(nc.vector.tensor_tensor(pair[:, 0, :, :], pair[:, 0, :, :], pair[:, 1, :, :], ALU.add))
            run(nc.vector.tensor_reduce(cand[:, :, :], square(0), AX_X, ALU.add))
            run(nc.vector.tensor_reduce(stat[:, 2, :], score[:, :, :], AX_X, ALU.max))
            run(nc.vector.tensor_tensor(gate[:, :, :], score[:, :, :], wide(2, EXPERTS), ALU.subtract))
            dve.sem_inc(f_ask, 1)
            dve.wait_ge(f_exp, 4)
            run(nc.vector.scalar_tensor_tensor(gate[:, :, :], cand[:, :, :], 1.5, gate[:, :, :], ALU.is_lt, ALU.mult))
            run(nc.vector.tensor_reduce(stat[:, 3, :], gate[:, :, :], AX_X, ALU.add))
            run(nc.vector.reciprocal(stat[:, 3, :], stat[:, 3, :]))
            run(nc.vector.tensor_tensor(gate[:, :, :], gate[:, :, :], wide(3, EXPERTS), ALU.mult))
            dve.sem_inc(gates_known, 1)
            dve.wait_ge(my_done, 2 + CHUNKS * EXPERTS)
            dve.sem_inc(gated, 2)
            with dve.Fori(0, CHUNKS) as i:
                for e in range(EXPERTS):
                    v = EXPERTS * i + e
                    dve.wait_ge(gates_ready, v + 1)
                    nc.vector.tensor_tensor(y_exp[e][:, i, :], y_exp[e][:, i, :], ps[6 + e % 2][:, :], ALU.mult).then_inc(gated, 1)
                dve.wait_ge(gated, EXPERTS * (i + 1) + 2)
                for e in (0, 2):
                    nc.vector.tensor_tensor(y_exp[e][:, i, :], y_exp[e][:, i, :], y_exp[e + 1][:, i, :], ALU.add).then_inc(gated_b, 1)
                dve.wait_ge(gated_b, 3 * i + 2)
                nc.vector.tensor_tensor(y_exp[0][:, i, :], y_exp[0][:, i, :], y_exp[2][:, i, :], ALU.add).then_inc(gated_b, 1)
                dve.wait_ge(gated_b, 3 * i + 3)
                nc.vector.tensor_tensor(X[:, i, :], X[:, i, :], y_exp[0][:, i, :], ALU.add).then_inc(res4, 1)

        @block.tensor
        def _(pe):
            def mm(o, l, r, start, stop, **kw):
                return nc.tensor.matmul(o, l, r, start=start, stop=stop, **kw)

            def norm(ln, res, credit):
                pe.sem_inc(ln.var_ready, 2)
                with pe.Fori(0, IMGS) as n:
                    for h in range(2):
                        i = 2 * n + h
                        if res is not None:
                            pe.wait_ge(res, i + credit + 1)
                        pe.wait_ge(ln.centred, i + 1)
                        mm(ps[h][:, :], mean_w[:, :], X[:, i, :], True, True).then_inc(ln.mean_ready, 1)
                    for h in range(2):
                        i = 2 * n + h
                        pe.wait_ge(ln.squared, i + 1)
                        for j in range(CHUNK // P):
                            last = mm(ps[2][:, bass.ds(i * (CHUNK // P) + j, 1)], sq[:, h, j * P:(j + 1) * P], mean_w[:, 0:1],
                                      True, True)
                        last.then_inc(ln.var_ready, 1)
                pe.wait_ge(ln.inv_ready, 1)
                for i in range(CHUNKS):
                    pe.wait_ge(ln.normed, i + 1)
                    for j in range(CHUNK // P):
                        t = i * (CHUNK // P) + j
                        last = mm(ps[6 + i % 2][:, j * P:(j + 1) * P], inv[:, t:t + 1].to_broadcast([P, P]), ident[:, :], True, True)
                    last.then_inc(ln.spread, 1)

            pe.wait_ge(x_in, 16 * IMGS)
            pe.wait_ge(made, 16)
            norm(ln0, None, 0)
            pe.wait_ge(wa_in, WA)
            pe.wait_ge(padded, CHUNKS)
            pe.wait_ge(made, 16)

            def conv(w, m, done, frees):
                with pe.Fori(0, IMGS) as n:
                    for h in range(2):
                        for f in frees:
                            pe.wait_ge(f, 2 * n + h + 1)
                        for k in range(TAPS):
                            dy, dx = divmod(k, 3)
                            last = mm(ps[4 + h][0:m, :], w[:, k, :],
                                      XP[:, n, HROWS * h + dy:HROWS * h + dy + HROWS, dx:dx + SIDE], k == 0, k == TAPS - 1)
                        last.then_inc(done, 1)

            conv(w_off, 64, off_ready, (off_done, msk_row_s))
            pe.sem_inc(main_done, 4)

            def broadcast(n, k, h):
                u = (n * TAPS + k) * 2 + h
                pe.wait_ge(abs_done, 2 * u + 2)
                mm(ps[h][:, :], sel[:, 2 * k, :], OFS[:, 2 * n + h, :], True, True)
                pe.wait_ge(ax_done, u + 1)
                mm(ps[2][:, :], sel[:, 2 * k + 1, :], OFS[:, 2 * n + h, :], True, True)
                pe.wait_ge(txm_done, u + 2)
                mm(ps[3][:, :], sel[:, k, :], MSK[:, 2 * n + h, :], True, True).then_inc(bc_ready, 1)

            def sample(n, k, h):
                u = (n * TAPS + k) * 2 + h
                for g in range(2):
                    v = 2 * u + g
                    pe.wait_ge(ten_done, v + 5)
                    for j in range(GROUP):
                        last = mm(ps[4 + h][:, :], YT[:, GROUP * g + j, k * P:(k + 1) * P], TEN[:, 2 * h + g, j, :], False, False,
                                  skip_group_check=True)
                    last.then_inc(main_done, 1)

            pe.wait_ge(wb_in, WB_)
            pe.wait_ge(off_done, 2 + CHUNKS)
            pe.wait_ge(msk_done, 1 + CHUNKS)
            pe.wait_ge(left_known, 1)
            lefts = pe.value_load(num[0:1, N_LEFT:N_LEFT + 1], min_val=1, max_val=(ECOLS - KEPT1) // 8)
            mm(ps[7][:, 0:HIS], zero_b[:, 0:P], zero_b[:, 0:HIS], True, False, skip_group_check=True)
            pe.sem_inc(left_added, 1)
            with pe.Fori(0, lefts) as r:
                pe.wait_ge(left_coded, r * 7 + 7)
                for c in range(8):
                    last = mm(ps[7][:, 0:HIS], oh_lo[:, 0, c, :], oh_hi[:, 0, c, :], False, False, skip_group_check=True)
                last.then_inc(left_added, 1)
            pe.wait_ge(batches_known, 1)
            batches = pe.value_load(num[0:1, N_BATCH:N_BATCH + 1], min_val=1, max_val=MAX_BATCHES)
            with pe.Fori(0, batches) as b:
                pe.wait_ge(batch_ready, b + 1)
                for q in range(BATCH // 4):
                    pe.wait_ge(turned_out, b * (BATCH // 4) + q + 1)
                    for j in range(4):
                        last = nc.tensor.transpose(ps[4 + q % 2][:, j * P:(j + 1) * P],
                                                   batch_k[:, 4 * q + j:4 * q + j + 1].to_broadcast([P, P]), ident[:, :])
                    last.then_inc(turned, 1)
            pe.wait_ge(rounds_known, 1)
            pe.sem_inc(piece_added, 2)

            def add_piece(n, k, h):
                pe.wait_ge(piece_made, PIECES * n + 2 * k + h + 1)
                for c in range(PIECE):
                    last = mm(ps[7][:, 0:HIS], oh_lo[:, h, c, :], oh_hi[:, h, c, :], k + h + c == 0,
                              2 * k + h == PIECES - 1 and c == PIECE - 1)
                last.then_inc(piece_added, 1)

            with pe.Fori(0, IMGS) as n:
                broadcast(n, 0, 0)
                pe.wait_ge(res1, 2 * n + 2)
                for h in range(2):
                    mm(ps[4 + h][:, :], zero_b[:, 0:P], zero_b[:, :], True, False, skip_group_check=True)
                pe.wait_ge(own_ready, n + 1)
                pe.wait_ge(shares_added, n + 1)
                for q in range(3 * SRC_T):
                    t, g = divmod(q, 3)
                    w = min(CHUNK, TAPS * P - g * CHUNK)
                    pe.wait_ge(yt_done, 3 * SRC_T * n + q + 1)
                    mm(ps[6 + q % 2][:, 0:w], own_img[:, t * P:(t + 1) * P], w_dcn[:, g * CHUNK:g * CHUNK + w],
                       True, True).then_inc(yt_ready, 1)
                pe.wait_ge(yt_done, 3 * SRC_T * (n + 1) + 2)
                for k in range(TAPS):
                    broadcast(n, k, 1)
                    sample(n, k, 0)
                    if 2 * k < PIECES:
                        add_piece(n, k, 0)
                    if k + 1 < TAPS:
                        broadcast(n, k + 1, 0)
                    sample(n, k, 1)
                    if 2 * k < PIECES:
                        add_piece(n, k, 1)
            norm(ln1, res1, 2)
            pe.wait_ge(wrb_done, 1)
            with pe.Fori(0, IMGS) as n:
                for h in range(2):
                    i = 2 * n + h
                    pe.wait_ge(ln1.normed, i + 3)
                    pe.wait_ge(rw_done, i + 1)
                    mm(ps[h][:, :], wr_b[:, :], T[:, i, :], True, True).then_inc(rw_ready, 1)
            with pe.Fori(0, IMGS) as n:
                for h in range(2):
                    i = 2 * n + h
                    for c in range(HID):
                        pe.wait_ge(gelu_done, HID * i + c + 1)
                        mm(ps[4 + c % 2][:, :], f_w1[:, c * P:(c + 1) * P], T[:, i, :], True, True).then_inc(h_ready, 1)
                    pe.wait_ge(gelu_done, HID * (i + 1) + 2)
                    pe.wait_ge(yf_done, i + 1)
                    for c in range(HID):
                        last = mm(ps[6 + h][:, :], f_w2[:, c, :], hid[h][:, c, :], c == 0, c == HID - 1)
                    last.then_inc(y_ready, 1)
                pe.wait_ge(cmp_done, SRC_T * (n + 1))
                pe.wait_ge(kept_done, 2 * n + 2)
                for h in range(2):
                    for t in range(SRC_T):
                        last = mm(ps[2 + h][:, :], ones_b[:, :], cmp_b[:, t, h * CHUNK:(h + 1) * CHUNK],
                                  t == 0, t == SRC_T - 1)
                last.then_inc(rank_ready, 1)
            norm(ln2, res2, 0)
            pe.wait_ge(padded, 2 * CHUNKS)
            conv(w_conv, P, cv_ready, (res3,))
            norm(ln3, res3, 2)
            pe.wait_ge(wc_in, WC)
            pe.wait_ge(ln3.normed, 2 + CHUNKS)
            for t in range(TILES):
                i, j = divmod(t, CHUNK // P)
                last = mm(ps[0][:, t * HE:(t + 1) * HE], T[:, i, j * P:(j + 1) * P], w_gat[:, :], True, True)
            last.then_inc(feat_ready, 1)
            def hidden(i, e):
                v = EXPERTS * i + e
                for c in range(2):
                    pe.wait_ge(mid_done, 2 * v + c + 1)
                    mm(ps[2 + c][:, :], m_w1[:, e, c * P:(c + 1) * P], T[:, i, :], True, True).then_inc(mid_ready, 1)

            def expert_out(i, e):
                v = EXPERTS * i + e
                pe.wait_ge(mid_done, 2 * v + 4)
                pe.wait_ge(my_done, v + 1)
                for c in range(2):
                    last = mm(ps[4 + e % 2][:, :], m_w2[:, e, c, :], mid[:, e % 2, c, :], c == 0, c == 1)
                last.then_inc(my_ready, 1)

            pe.wait_ge(wd_in, 32)
            pe.sem_inc(my_ready, 2)
            with pe.Fori(0, CHUNKS) as i:
                hidden(i, 0)
                for e in range(1, EXPERTS):
                    hidden(i, e)
                    expert_out(i, e - 1)
                expert_out(i, EXPERTS - 1)
            pe.wait_ge(t_chain, 1)
            wide_hi = HIS // 2 * ROW
            for b in range(2):
                mm(ps[b][:, 0:wide_hi], zero_b[:, 0:P], zero_b[:, 0:wide_hi], True, False, skip_group_check=True)
            pe.sem_inc(summed2, 2)
            total = pe.value_load(num[0:1, N_ALL:N_ALL + 1], min_val=1, max_val=MAX_ROUNDS)
            with pe.Fori(0, total) as r:
                for half in range(2):
                    for g in range(2):
                        pe.wait_ge(spread2, 4 * r + 2 * half + g + 1)
                        for k in range(GROUP):
                            for b in range(2):
                                last = mm(ps[b][:, 0:wide_hi], ident[:, :], spread_v[g][:, k, b * wide_hi:(b + 1) * wide_hi],
                                          False, False, skip_group_check=True)
                        last.then_inc(summed2, 1)
            pe.wait_ge(gates_known, 1)
            for i in range(CHUNKS):
                for e in range(EXPERTS):
                    pe.wait_ge(gated, EXPERTS * i + e + 1)
                    for j in range(CHUNK // P):
                        t = i * (CHUNK // P) + j
                        last = nc.tensor.transpose(ps[6 + e % 2][:, j * P:(j + 1) * P],
                                                   gate[:, t, e:e + 1].to_broadcast([P, P]), ident[:, :])
                    last.then_inc(gates_ready, 1)

_WEIGHTS = {
    "w_off": ("L0_conv_offset_w", (P, TAPS, 3 * TAPS)), "b_off": ("L0_conv_offset_b", (3 * TAPS,)),
    "w_dcn": ("L0_conv_dcn_w", (P, TAPS * P)), "wr": ("L0_ffn_wr", (P, 1)), "br": ("L0_ffn_br", (1,)),
    "f_w1": ("L0_ffn_w1", (P, HID * P)), "f_b1": ("L0_ffn_b1", (P, HID)),
    "edges": ("L1_ffn_edge_index", (2, EDGES)), "w_gat": ("L1_ffn_W_gat", (P, HE)),
    "att_src": ("L1_ffn_att_src", (HE,)), "att_dst": ("L1_ffn_att_dst", (HE,)), "b_gat": ("L1_ffn_b_gat", (HE,)),
    "ln_gamma": ("L1_ffn_ln_gamma", (HE,)), "ln_beta": ("L1_ffn_ln_beta", (HE,)),
    "m_w1": ("L1_ffn_W1", (EXPERTS, P, 2 * P)), "m_b1": ("L1_ffn_b1", (P, EXPERTS, 2)),
    "m_w2": ("L1_ffn_W2", (EXPERTS, 2 * P, P)), "m_b2": ("L1_ffn_b2", (P, EXPERTS)),
    "f_w2": ("L0_ffn_w2", (HID * P, P)), "f_b2": ("L0_ffn_b2", (P,)), "w_conv": ("L1_conv_weight", (P, TAPS, P)),
}


def kernel(**inputs):
    import concourse.bacc as _bacc
    from concourse.bass_utils import run_bass_kernel_spmd as _run

    nc = _bacc.Bacc("TRN2", target_bir_lowering=False, num_devices=1)
    y, x = np.divmod(np.arange(POS), SIDE)
    ky, kx = np.divmod(np.arange(TAPS), 3)
    base = np.stack([y[None] - 1 + ky[:, None], x[None] - 1 + kx[:, None]], 1).reshape(2 * TAPS, POS)
    rows = np.arange(P)[:, None] // SIDE + np.arange(SRC_T)[None] * (P // SIDE)
    arrays = {"base": base.astype(np.float32), "neg_y": -rows.astype(np.float32),
              "neg_x": -(np.arange(P)[:, None] % SIDE).astype(np.float32), "x": np.asarray(inputs["x"])}
    for name, (source, shape) in _WEIGHTS.items():
        w = np.asarray(inputs[source])
        if w.ndim == 4:
            w = w.reshape(w.shape[0], P, TAPS).transpose(1, 2, 0)
        elif name == "f_b1":
            w = w.reshape(HID, P).T
        elif name == "m_b1":
            w = w.reshape(EXPERTS, 2, P).transpose(2, 0, 1)
        elif name == "m_b2":
            w = w.T
        arrays[name] = np.ascontiguousarray(w).reshape(shape)
    a = {k: nc.dram_tensor(f"in_{k}", v.shape, mybir.dt.from_np(v.dtype), kind="ExternalInput").ap()
         for k, v in arrays.items()}
    out = nc.dram_tensor("out_x", (IMGS, P, SIDE, SIDE), F32, kind="ExternalOutput").ap()
    metaformer_kernel(nc, a, out)
    r = _run(nc, [{f"in_{k}": v for k, v in arrays.items()}], core_ids=[0])
    return r.results[0]["out_x"]
```

```python
from collections import namedtuple
from contextlib import ExitStack

import numpy as np

import concourse.bass as bass
from concourse import mybir

F32 = mybir.dt.float32
BF16 = mybir.dt.bfloat16
I32 = mybir.dt.int32
ALU = mybir.AluOpType
ACT = mybir.ActivationFunctionType
AX_X = mybir.AxisListType.X

P = 128
IMGS = 4
SIDE = 32
POS = SIDE * SIDE
NODES = IMGS * POS
CHUNK = 512
CHUNKS = NODES // CHUNK
TILES = NODES // P
TAPS = 9
HROWS = SIDE // 2
SRC_T = POS // P
PAD = SIDE + 2
GROUP = 4
NEAR = 3
FAR = 2.9 * 2.9
RING = 3
KEPT = POS // 2 - 1
HID = 4


EDGES = 524288
ECOLS = EDGES // P
FIRST = 32
KEPT1 = ECOLS // FIRST * 8
BATCH = 96
BCHUNKS = 64
KEPT2 = BCHUNKS * 8
ROUND = 16
HALFR = ROUND // 2
MAX_BATCHES = -(-ECOLS // BATCH)
MAX_ROUNDS = ECOLS * P // ROUND
LAST = NODES - 1
NONE = -8192.0
KEY_PART = 1024
SURE = 2.0 ** 27
KEY_BIAS = (-1.0, -LAST / 2, (LAST / 2 + 0.25) * SURE, (LAST - 0.5) * SURE)
BIG = 1e30
HEADS = 4
EXPERTS = 4
HE = HEADS * EXPERTS
ROW = HE + HEADS
HIS = TILES
PIECE = 16
PIECES = KEPT1 // PIECE // IMGS

LayerNorm = namedtuple("LayerNorm", "eps mean_ready centred squared var_ready std_ready inv_ready spread normed")


def metaformer_kernel(nc, a, out):
    with ExitStack() as ctx:
        def sb(name, shape, dt=F32):
            return ctx.enter_context(nc.sbuf_tensor(name, shape, dt))

        def sem(name):
            return ctx.enter_context(nc.semaphore(name))

        banks = ctx.enter_context(nc.psum_tensor("banks", [P, 8, CHUNK], F32))
        ps = [banks[:, i, :] for i in range(8)]
        bank_of = lambda i, p=slice(0, P): banks[p, bass.ds(i, 1), :].rearrange("p o c -> p (o c)")

        X = sb("X", [P, CHUNKS, CHUNK])
        T = sb("T", [P, CHUNKS, CHUNK])
        wide_buf = sb("wide_buf", [P, SRC_T * TAPS * P + 4 * GROUP * CHUNK])
        scratch = wide_buf[:, 0:SRC_T * TAPS * P]
        RW = scratch[:, 0:NODES].rearrange("p (i c) -> p i c", c=CHUNK)
        YF = scratch[:, NODES:2 * NODES].rearrange("p (i c) -> p i c", c=CHUNK)
        XP = sb("XP", [P, IMGS, PAD, PAD])
        sq = sb("sq", [P, 2, CHUNK])
        dev = sb("dev", [P, TILES])
        inv = sb("inv", [P, TILES])
        ident = sb("ident", [P, P])
        mean_w = sb("mean_w", [P, P])
        eps = sb("eps", [P, 2])
        k_bias = sb("k_bias", [P, 4])
        ones_b = sb("ones_b", [P, P], BF16)
        later = sb("later", [P, P])

        w_off = sb("w_off", [P, TAPS, 64])
        b_off = sb("b_off", [64, 1])
        w_dcn = sb("w_dcn", [P, TAPS * P])
        shared = sb("shared", [P, 4096])
        split = lambda t: t.bitcast(BF16).rearrange("p (i c) -> p i c", c=CHUNK)
        OFS = split(shared[0:96, 0:2048])
        MSK = split(shared[0:96, 2048:4096])
        sel = sb("sel", [96, 2 * TAPS, P], BF16)
        zero_b = sb("zero_b", [P, CHUNK], BF16)
        neg_x = sb("neg_x", [P, 1])
        neg_y = sb("neg_y", [P, SRC_T])
        YT = scratch[:, :].rearrange("p (t k) -> p t k", t=SRC_T)
        TEN = wide_buf[:, SRC_T * TAPS * P:].rearrange("p (a b c) -> p a b c", a=4, b=GROUP)
        small = sb("small", [P, 3072])
        txm = small[:, 0:1024].rearrange("p (h c) -> p h c", h=2)
        absx = small[:, 1024:2048].rearrange("p (h c) -> p h c", h=2)
        own_img = small[:, 2048:3072]
        near_w = [TEN[:, b, :, :].rearrange("p g c -> p (g c)")[:, 0:4 * NEAR * P].rearrange("p (s c) -> p s c", c=P)
                  for b in range(RING)]
        YTN = scratch[:, 0:RING * POS].rearrange("p (r t k) -> p r t k", r=RING, t=SRC_T)
        far = sb("far", [2 * TAPS, CHUNKS])

        def near_tiles(h):
            for t in range(SRC_T):
                js = [j for j in range(4) if abs(4 * h + j - t) <= 1]
                if js:
                    yield t, js[0], len(js), NEAR * js[0] + t - (4 * h + js[0]) + 1

        def near_parts(h):
            for j in range(4):
                ts = [t for t in range(SRC_T) if abs(4 * h + j - t) <= 1]
                yield j, NEAR * j + ts[0] - (4 * h + j) + 1, len(ts)

        wr = sb("wr", [P, 1])
        wr_b = sb("wr_b", [P, P])
        br_b = sb("br_b", [P, 1])
        f_w1 = sb("f_w1", [P, HID * P])
        f_b1 = sb("f_b1", [P, HID])
        f_w2 = sb("f_w2", [P, HID, P])
        f_b2 = sb("f_b2", [P, 1])
        w_col = sb("w_col", [P, IMGS, SRC_T])
        tie = sb("tie", [P, P])
        cmp_b = TEN[:, 0:2, :, :].rearrange("p a b c -> p (a b c)").bitcast(BF16).rearrange("p (t c) -> p t c", t=SRC_T)
        hid = [TEN[:, 2 + h, :, :] for h in range(2)]

        w_conv = sb("w_conv", [P, TAPS, P])

        src_i = TEN[:, 0:2, :, :].rearrange("p a b c -> p (a b c)").bitcast(I32)
        dst_i = TEN[:, 2:4, :, :].rearrange("p a b c -> p (a b c)").bitcast(I32)
        flags = TEN[:, 0:2, :, :].rearrange("p a b c -> p (a b c)")
        code_i = TEN[:, 2:4, :, :].rearrange("p a b c -> p (a b c)").bitcast(I32)
        routed = wide_buf[:, 0:BATCH * P]
        keys = scratch[:, 0:ECOLS]
        listed = scratch[:, ECOLS:2 * ECOLS]
        generic = sb("generic", [P, MAX_BATCHES * BATCH])
        base = scratch[0:2 * TAPS, 2 * ECOLS:2 * ECOLS + POS]
        off_row, off_rem, off_sq = (generic[0:2 * TAPS, k * CHUNK:(k + 1) * CHUNK] for k in range(3))
        off_mid = generic[0:2 * TAPS, 3 * CHUNK:3 * CHUNK + CHUNK // 2].bitcast(BF16)
        msk_row, msk_rem = (generic[0:TAPS, k * CHUNK:(k + 1) * CHUNK] for k in (4, 5))
        msk_mid = generic[0:TAPS, 6 * CHUNK:6 * CHUNK + CHUNK // 2].bitcast(BF16)
        k_src, k_last, k_gen, k_node = (generic[:, k * KEY_PART:(k + 1) * KEY_PART] for k in range(4))
        k_lo, k_hi = (small[:, k * KEY_PART:(k + 1) * KEY_PART].bitcast(I32) for k in range(2))
        k_key = small[:, 2 * KEY_PART:3 * KEY_PART]
        batch_k = sb("batch_k", [P, BATCH])
        kept2 = sb("kept2", [P, KEPT2])
        top8 = sb("top8", [P, 8])
        round_k = sb("round_k", [P, ROUND])
        neg_lo = sb("neg_lo", [P, 1])
        counts = sb("counts", [P, 2])
        rest_n = sb("rest_n", [P, BATCH * P // ECOLS])
        counts_max = sb("counts_max", [P, 2])
        num = sb("num", [P, 9], I32)
        N_LEFT, N_A, N_B, N_BATCH, N_EA, N_EB, N_BASE, N_ALL, N_FAR = range(9)
        lane = sb("lane", [P, P])
        lane_b = sb("lane_b", [P, P], BF16)
        lo_b = sb("lo_b", [P, KEPT1], BF16)
        hi_b = sb("hi_b", [P, KEPT1], BF16)
        left_i = sb("left_i", [P, 2, 8], I32)
        left_b = sb("left_b", [P, 2, 8], BF16)
        oh_lo = generic[:, 0:2048].bitcast(BF16).rearrange("p (h c l) -> p h c l", h=2, l=P)
        oh_hi = generic[:, 2048:2560].bitcast(BF16).rearrange("p (h c l) -> p h c l", h=2, l=HIS)
        to_last = sb("to_last", [P, HIS])
        rounds_d = nc.dram_tensor("rounds_d", (MAX_ROUNDS, P, ROUND), F32, kind="Internal").ap()
        generic_d = nc.dram_tensor("generic_d", (P, MAX_BATCHES * BATCH), F32, kind="Internal").ap()
        table_d = nc.dram_tensor("table_d", (NODES, ROW), F32, kind="Internal").ap()

        w_gat = sb("w_gat", [P, HE])
        att = sb("att", [P, 2, HE])
        gat_v = sb("gat_v", [P, 3, HE])
        table = shared[:, 2048:2688].rearrange("p (t f) -> p t f", f=ROW)
        prod = shared[:, 2688:3200].rearrange("p (t f) -> p t f", f=HE)
        a_dst = sb("a_dst", [P, HIS, HEADS])
        last_row = sb("last_row", [P, ROW])
        s_max = sb("s_max", [P, HIS, HEADS])
        e_max = sb("e_max", [P, HIS, HEADS])
        pen = sb("pen", [P, HIS])
        cand = sb("cand", [P, HIS, HEADS])
        g_idx = sb("g_idx", [P, ROUND], I32)
        g_int = sb("g_int", [P, ROUND], I32)
        g_hi = sb("g_hi", [P, ROUND])
        rows_g = sb("rows_g", [P, 2, HALFR, ROW])
        oh = shared[:, 3200:3456].rearrange("p (k t) -> p k t", t=HIS)
        oh_t = shared[:, 3456:3712].rearrange("p (t k) -> p t k", t=HIS)
        sel_p = shared[:, 0:HALFR * 8 * HIS]
        per_hi = sb("per_hi", [P, 8, HIS])
        got = sb("got", [P, HALFR, 8])
        z = sb("z", [P, HALFR, HEADS])
        vals = sb("vals", [P, HALFR, ROW])
        spread_v = [t[:, 0:GROUP * HIS * ROW].rearrange("p (k f) -> p k f", k=GROUP) for t in (generic, small)]
        pads = XP[:, :, :, :].rearrange("p n r c -> p (n r c)")
        m_w1 = pads[:, 2048:3072].rearrange("p (e h) -> p e h", e=EXPERTS)
        m_b1 = sb("m_b1", [P, EXPERTS, 2])
        m_w2 = pads[:, 3072:4096].rearrange("p (e k d) -> p e k d", e=EXPERTS, k=2)
        m_b2 = sb("m_b2", [P, EXPERTS])
        below = sb("below", [P, EXPERTS, EXPERTS])
        stat = sb("stat", [P, 4, HIS])
        score = sb("score", [P, HIS, EXPERTS])
        gate = sb("gate", [P, HIS, EXPERTS])
        pair = shared[:, 0:1024].rearrange("p (a t f) -> p a t f", a=2, t=HIS)
        mid = pads[:, 0:4 * CHUNK].rearrange("p (a b c) -> p a b c", a=2, b=2)
        y_exp = [scratch[:, 0:NODES], scratch[:, NODES:2 * NODES],
                 TEN[:, 0:2, :, :].rearrange("p a b c -> p (a b c)"), TEN[:, 2:4, :, :].rearrange("p a b c -> p (a b c)")]
        y_exp = [y.rearrange("p (i c) -> p i c", c=CHUNK) for y in y_exp]

        def image(t):
            return t[:, :, :].rearrange("p (n h) c -> p n (h c)", n=IMGS)

        x_in, wa_in, wb_in = sem("x_in"), sem("wa_in"), sem("wb_in")
        made = sem("made")
        padded, pads_used = sem("padded"), sem("pads_used")

        def layer_norm(tag, e):
            return LayerNorm(e, *(sem(f"{tag}_{n}") for n in LayerNorm._fields[1:]))

        ln0, ln1, ln2, ln3 = (layer_norm(f"ln{i}", e) for i, e in enumerate((0, 1, 0, 1)))

        off_ready, off_a, off_hi, off_r, off_m, off_done = (sem(f"off_{n}") for n in ("ready", "row", "hi", "rem", "mid", "done"))
        msk_cp = sem("msk_cp")
        msk_row_s, msk_hi, msk_r, msk_m, msk_done = (sem(f"msk_{n}") for n in ("row_s", "hi", "rem_s", "mid_s", "done"))
        bc_ready, ax_done, rx_done, txm_done = sem("bc_ready"), sem("ax_done"), sem("rx_done"), sem("txm_done")
        abs_done, relu_done, ten_done, main_done = sem("abs_done"), sem("relu_done"), sem("ten_done"), sem("main_done")
        own_ready, far_chain, ten_pool = sem("own_ready"), sem("far_chain"), sem("ten_pool")
        yt_ready, yt_done, res1 = sem("yt_ready"), sem("yt_done"), sem("res1")
        wrb_done = sem("wrb_done")
        rw_ready, rw_done, diag_done, col_done = sem("rw_ready"), sem("rw_done"), sem("diag_done"), sem("col_done")
        cmp_part, cmp_done, rank_ready, kept_done = sem("cmp_part"), sem("cmp_done"), sem("rank_ready"), sem("kept_done")
        h_ready, gelu_done, y_ready, yf_done = sem("h_ready"), sem("gelu_done"), sem("y_ready"), sem("yf_done")
        fin_a, fin_b, res2 = sem("fin_a"), sem("fin_b"), sem("res2")
        cv_ready, res3 = sem("cv_ready"), sem("res3")
        stored = sem("stored")
        passed, pool_passed, sp_passed, pe_passed, act_passed = (sem(n) for n in (
            "passed", "pool_passed", "sp_passed", "pe_passed", "act_passed"))
        edges_in, wc_in, wd_in = sem("edges_in"), sem("wc_in"), sem("wd_in")
        k_front, k_tests, k_gens, e_step, e_chain, counted, reduced, made2 = sem("k_front"), sem("k_tests"), sem("k_gens"), sem("e_step"), sem("e_chain"), sem("counted"), sem("reduced"), sem("made2")
        left_known, left_coded, left_added, piece_made, piece_added = (sem(n) for n in (
            "left_known", "left_coded", "left_added", "piece_made", "piece_added"))
        codes_made, left_read = sem("codes_made"), sem("left_read")
        batches_known, batch_ready, turned, turned_out, batch_known = (sem(n) for n in (
            "batches_known", "batch_ready", "turned", "turned_out", "batch_known"))
        batch_in, generic_made, generic_out = sem("batch_in"), sem("generic_made"), sem("generic_out")
        round_ready, round_stored, rounds_known = sem("round_ready"), sem("round_stored"), sem("rounds_known")
        r2_chain, pieces_done, shares_added = sem("r2_chain"), sem("pieces_done"), sem("shares_added")
        r_chain, rb_chain, b_chain = sem("r_chain"), sem("rb_chain"), sem("b_chain")
        feat_ready, t_chain, table_ready, table_out, last_in = (sem(n) for n in (
            "feat_ready", "t_chain", "table_ready", "table_out", "last_in"))
        key1_in, idx1_ready, rows1_in, max1_done, m1_chain = (sem(n) for n in (
            "key1_in", "idx1_ready", "rows1_in", "max1_done", "m1_chain"))
        key2_in, idx2_ready, rows2_in, got2, exp2, spread2, summed2, m2_chain = (sem(n) for n in (
            "key2_in", "idx2_ready", "rows2_in", "got2", "exp2", "spread2", "summed2", "m2_chain"))
        rows1_b, rows2_b, used2 = sem("rows1_b"), sem("rows2_b"), sem("used2")
        sums_done, f_chain, f_exp, f_ask = sem("sums_done"), sem("f_chain"), sem("f_exp"), sem("f_ask")
        mid_ready, mid_done, my_ready, my_done = sem("mid_ready"), sem("mid_done"), sem("my_ready"), sem("my_done")
        gates_known, gates_ready, gated, gated_b, res4 = (sem(n) for n in ("gates_known", "gates_ready", "gated", "gated_b", "res4"))

        POOL_BLOCKS, DVE_BLOCKS = ((0, 1), (2, 3)), ((2, 3), (0, 1))

        def near_mult(engine, b, h, blocks):
            parts = {}
            for j, s, c in near_parts(h):
                if j in blocks:
                    parts.setdefault(c, []).append((j, s))
            for c, js in parts.items():
                (j, s), k = js[0], len(js)
                t = near_w[b][:, s:s + NEAR * (k - 1) + c, :]
                m = txm[:, h, j * P:(j + k) * P].rearrange("p (k c) -> p k c", k=k).unsqueeze(2).to_broadcast([P, k, c, P])
                t = t.rearrange("p (k s) c -> p k s c", k=k)
                last = engine.tensor_tensor(t, t, m, ALU.mult)
            return last

        block = ctx.enter_context(nc.Block())

        WA, WB_, WC = 16 * 7, 16 * 8, 16 * 8

        @block.sync
        def _(sp):
            for n in range(IMGS):
                sp.dma_start(image(X)[:, n, :], a["x"][n].rearrange("c h w -> c (h w)")).then_inc(x_in, 16)
            sp.dma_start(src_i, a["edges"][0].rearrange("(p c) -> p c", p=P)).then_inc(edges_in, 16)
            sp.dma_start(dst_i, a["edges"][1].rearrange("(p c) -> p c", p=P)).then_inc(edges_in, 16)
            sp.dma_start(w_dcn[:, :], a["w_dcn"]).then_inc(wb_in, 16)
            sp.dma_start(wr[:, :], a["wr"]).then_inc(wb_in, 16)
            sp.dma_start(br_b[:, :], a["br"].partition_broadcast(P)).then_inc(wb_in, 16)
            sp.dma_start(f_w1[:, :], a["f_w1"]).then_inc(wb_in, 16)
            sp.dma_start(f_b1[:, :], a["f_b1"]).then_inc(wb_in, 16)
            sp.dma_start(f_w2[:, :, :], a["f_w2"].rearrange("(c p) d -> p c d", p=P)).then_inc(wb_in, 16)
            sp.dma_start(f_b2[:, :], a["f_b2"].rearrange("(p c) -> p c", c=1)).then_inc(wb_in, 16)
            sp.dma_start(w_conv[:, :, :], a["w_conv"]).then_inc(wb_in, 16)
            sp.dma_start(w_gat[:, :], a["w_gat"]).then_inc(wc_in, 16)
            for k, name in enumerate(("att_src", "att_dst")):
                sp.dma_start(att[:, k, :], a[name].partition_broadcast(P)).then_inc(wc_in, 16)
            for k, name in enumerate(("b_gat", "ln_gamma", "ln_beta")):
                sp.dma_start(gat_v[:, k, :], a[name].partition_broadcast(P)).then_inc(wc_in, 16)
            sp.dma_start(m_b1[:, :, :], a["m_b1"]).then_inc(wc_in, 16)
            sp.dma_start(m_b2[:, :], a["m_b2"]).then_inc(wc_in, 16)
            sp.wait_ge(generic_made, 1)
            sp.dma_start(generic_d, generic[:, :]).then_inc(generic_out, 16)
            sp.wait_ge(generic_out, 16)
            sp.wait_ge(batches_known, 1)
            batches = sp.value_load(num[0:1, N_BATCH:N_BATCH + 1], min_val=1, max_val=MAX_BATCHES)
            with sp.Fori(0, batches) as b:
                sp.wait_ge(turned, b * (BATCH // 4) + 1)
                sp.dma_start(batch_k[:, :], generic_d[:, bass.ds(b * BATCH, BATCH)]).then_inc(batch_in, 16)
                sp.wait_ge(batch_known, b + 1)
                sp.sem_inc(sp_passed, 1)
                ea = sp.value_load(num[0:1, N_EA:N_EA + 1], min_val=1, max_val=KEPT2 // ROUND)
                eb = sp.value_load(num[0:1, N_EB:N_EB + 1], min_val=0, max_val=(BATCH * P - KEPT2) // ROUND)
                first = sp.value_load(num[0:1, N_BASE:N_BASE + 1], min_val=0, max_val=MAX_ROUNDS - BATCH * P // ROUND)
                with sp.Fori(0, ea) as r:
                    sp.wait_ge(round_ready, first + r + 1)
                    sp.dma_start(rounds_d[bass.ds(first + r, 1)].rearrange("o p s -> (o p) s"), round_k[:, :]).then_inc(round_stored, 16)
                with sp.If(eb > 0):
                    with sp.Fori(0, eb) as r:
                        sp.wait_ge(round_ready, first + ea + r + 1)
                        sp.dma_start(rounds_d[bass.ds(first + ea + r, 1)].rearrange("o p s -> (o p) s"), round_k[:, :]).then_inc(round_stored, 16)
                    sp.nop()
                sp.nop()
            sp.wait_ge(rounds_known, 1)
            total = sp.value_load(num[0:1, N_ALL:N_ALL + 1], min_val=1, max_val=MAX_ROUNDS)
            sp.wait_ge(round_stored, total * 16 + 16)
            sp.wait_ge(cv_ready, CHUNKS)
            sp.dma_start(m_w1[:, :, :], a["m_w1"].rearrange("e c h -> c e h")).then_inc(wd_in, 16)
            sp.dma_start(m_w2[:, :, :, :], a["m_w2"].rearrange("e (k p) d -> p e k d", p=P)).then_inc(wd_in, 16)
            sp.wait_ge(table_ready, 1)
            sp.dma_start(table_d.rearrange("(t p) f -> p t f", p=P), table[:, :, :]).then_inc(table_out, 16)
            sp.wait_ge(table_out, 16)
            sp.dma_start(last_row[:, :], table_d[LAST].partition_broadcast(P)).then_inc(last_in, 16)
            with sp.Fori(0, total) as r:
                sp.wait_ge(idx1_ready, r + 1)
                sp.dma_start(round_k[:, :], rounds_d[bass.ds(r, 1)].rearrange("o p s -> (o p) s")).then_inc(key1_in, 16)
            with sp.Fori(0, total) as r:
                sp.wait_ge(idx2_ready, r + 1)
                sp.dma_start(round_k[:, :], rounds_d[bass.ds(r, 1)].rearrange("o p s -> (o p) s")).then_inc(key2_in, 16)
            sp.wait_ge(res4, CHUNKS)
            for n in range(IMGS):
                sp.dma_start(out[n].rearrange("c h w -> c (h w)"), image(X)[:, n, :]).then_inc(stored, 16)
            sp.wait_ge(stored, 16 * IMGS)

        @block.gpsimd
        def _(pool):
            nc.gpsimd.memset(mean_w[:, :], 1.0 / P).then_inc(made, 1)
            nc.gpsimd.memset(ident[:, :], 0.0).then_inc(made, 1)
            nc.gpsimd.memset(eps[:, 0:1], 1e-6).then_inc(made, 1)
            nc.gpsimd.memset(eps[:, 1:2], 1e-5).then_inc(made, 1)
            for k, v in enumerate(KEY_BIAS):
                nc.gpsimd.memset(k_bias[:, k:k + 1], v).then_inc(made, 1)
            nc.gpsimd.memset(w_off[:, :, :], 0.0).then_inc(made, 1)
            pool.wait_ge(made, 9)
            nc.gpsimd.affine_select(out=ident[:, :], in_=ident[:, :], compare_op=ALU.not_equal, fill=1.0, base=0,
                                    pattern=[[-1, P]], channel_multiplier=1).then_inc(made, 1)
            pool.dma_start(w_off[:, :, 0:2 * TAPS], a["w_off"][:, :, 0:2 * TAPS]).then_inc(wa_in, 16)
            pool.dma_start(w_off[:, :, 32:32 + TAPS], a["w_off"][:, :, 2 * TAPS:3 * TAPS]).then_inc(wa_in, 16)
            pool.dma_start(b_off[0:2 * TAPS, :], a["b_off"][0:2 * TAPS].rearrange("(p c) -> p c", c=1)).then_inc(wa_in, 16)
            pool.dma_start(b_off[32:32 + TAPS, :], a["b_off"][2 * TAPS:3 * TAPS].rearrange("(p c) -> p c", c=1)).then_inc(wa_in, 16)
            pool.dma_start(base, a["base"]).then_inc(wa_in, 16)
            pool.dma_start(neg_y[:, :], a["neg_y"]).then_inc(wa_in, 16)
            pool.dma_start(neg_x[:, :], a["neg_x"]).then_inc(wa_in, 16)
            nc.gpsimd.memset(XP[:, :, :, :], 0.0).then_inc(made, 1)
            nc.gpsimd.memset(shared[0:96, 0:2048], 0.0).then_inc(made, 1)
            nc.gpsimd.memset(shared[0:96, 2048:4096], 0.0).then_inc(made, 1)
            nc.gpsimd.memset(sel[:, :, :], 0.0).then_inc(made, 1)
            nc.gpsimd.memset(zero_b[:, :], 0.0).then_inc(made, 1)
            nc.gpsimd.memset(ones_b[:, :], 1.0).then_inc(made, 1)
            nc.gpsimd.memset(later[:, :], 1.0).then_inc(made, 1)
            pool.wait_ge(made, 17)
            for b in range(3):
                nc.gpsimd.affine_select(out=sel[:, :, :], in_=sel[:, :, :], compare_op=ALU.not_equal, fill=1.0,
                                        base=-32 * b, pattern=[[-1, 2 * TAPS], [0, P]],
                                        channel_multiplier=1).then_inc(made, 1)
                pool.wait_ge(made, 18 + b)
            nc.gpsimd.affine_select(out=later[:, :], in_=later[:, :], compare_op=ALU.is_gt, fill=0.0, base=0,
                                    pattern=[[1, P]], channel_multiplier=-1).then_inc(made, 1)
            nc.gpsimd.iota(lane[:, :], [[1, P]], base=0, channel_multiplier=0,
                           allow_small_or_imprecise_dtypes=True).then_inc(made2, 1)
            nc.gpsimd.iota(neg_lo[:, :], [[0, 1]], base=0, channel_multiplier=-(1 << 17),
                           allow_small_or_imprecise_dtypes=True).then_inc(made2, 1)
            nc.gpsimd.memset(below[:, :, :], 1.0).then_inc(made2, 1)
            pool.wait_ge(made2, 3)
            nc.gpsimd.tensor_copy(lane_b[:, :], lane[:, :]).then_inc(made2, 1)
            nc.gpsimd.affine_select(out=below[:, :, :], in_=below[:, :, :], compare_op=ALU.is_gt, fill=0.0, base=0,
                                    pattern=[[1, EXPERTS], [-1, EXPERTS]], channel_multiplier=0).then_inc(made2, 1)
            pool.sem_inc(msk_done, 1)
            for n in range(IMGS):
                for h in range(2):
                    i = 2 * n + h
                    pool.wait_ge(ln0.normed, i + 3)
                    nc.gpsimd.tensor_copy(XP[:, n, 1 + HROWS * h:1 + HROWS * (h + 1), 1:1 + SIDE],
                                          T[:, i, :].rearrange("p (r c) -> p r c", c=SIDE)).then_inc(padded, 1)
            for i in range(CHUNKS):
                pool.wait_ge(msk_row_s, i + 3)
                nc.gpsimd.tensor_copy(MSK[0:TAPS, i, :], msk_row).then_inc(msk_hi, 1)
                pool.wait_ge(msk_hi, i + 1)
                nc.gpsimd.tensor_tensor(msk_rem, msk_row, MSK[0:TAPS, i, :], ALU.subtract).then_inc(msk_r, 1)
                pool.wait_ge(msk_r, i + 1)
                nc.gpsimd.tensor_copy(msk_mid, msk_rem).then_inc(msk_m, 1)
                pool.wait_ge(msk_m, i + 1)
                nc.gpsimd.tensor_copy(MSK[32:32 + TAPS, i, :], msk_mid).then_inc(msk_cp, 1)
                pool.wait_ge(msk_cp, i + 1)
                nc.gpsimd.tensor_tensor(MSK[64:64 + TAPS, i, :], msk_rem, msk_mid, ALU.subtract).then_inc(msk_done, 1)
            pool.wait_ge(msk_done, 1 + CHUNKS)
            pool.wait_ge(counted, 1)
            nc.gpsimd.partition_all_reduce(counts_max[:, :], counts[:, :], P, bass.bass_isa.ReduceOp.max).then_inc(reduced, 1)
            pool.wait_ge(counted, 2)
            nc.gpsimd.partition_all_reduce(counts_max[:, :], counts[:, :], P, bass.bass_isa.ReduceOp.max).then_inc(reduced, 1)
            pool.wait_ge(batches_known, 1)
            pool.wait_ge(made2, 5)
            is_far = pool.value_load(num[0:1, N_FAR:N_FAR + 1], min_val=0, max_val=1)
            with pool.If(is_far > 0):
                for n in range(IMGS):
                    pool.wait_ge(yt_done, 3 * SRC_T * n + 2)
                    nc.gpsimd.tensor_copy(own_img, image(T)[:, n, :]).then_inc(own_ready, 1)
            with pool.If(is_far < 1):
                pool.sem_inc(ten_pool, 2)
                with pool.Fori(0, IMGS) as n:
                    pool.wait_ge(yt_done, 2 * TAPS * n + 1)
                    pool.sem_inc(pool_passed, 1)
                    nc.gpsimd.tensor_copy(own_img, image(T)[:, bass.ds(n, 1), :].rearrange("p o c -> p (o c)")).then_inc(own_ready, 1)
                    with pool.Fori(0, TAPS // RING) as q:
                        for s in range(2 * RING):
                            u, h = n * (2 * TAPS) + q * (2 * RING) + s, s % 2
                            pool.wait_ge(txm_done, u + 3)
                            pool.wait_ge(relu_done, u + 1)
                            pool.sem_inc(pool_passed, 1)
                            near_mult(nc.gpsimd, s % RING, h, POOL_BLOCKS[h]).then_inc(ten_pool, 1)
                pool.nop()
            for n in range(IMGS):
                for h in range(2):
                    i = 2 * n + h
                    pool.wait_ge(ln2.normed, i + 3)
                    nc.gpsimd.tensor_copy(XP[:, n, 1 + HROWS * h:1 + HROWS * (h + 1), 1:1 + SIDE],
                                          T[:, i, :].rearrange("p (r c) -> p r c", c=SIDE)).then_inc(padded, 1)
            batches = pool.value_load(num[0:1, N_BATCH:N_BATCH + 1], min_val=1, max_val=MAX_BATCHES)
            with pool.Fori(0, batches) as b:
                for k in range(2):
                    pool.wait_ge(counted, 2 * b + 3 + k)
                    pool.sem_inc(pool_passed, 1)
                    nc.gpsimd.partition_all_reduce(counts_max[:, :], counts[:, :], P, bass.bass_isa.ReduceOp.max).then_inc(reduced, 1)
            pool.wait_ge(rounds_known, 1)
            total = pool.value_load(num[0:1, N_ALL:N_ALL + 1], min_val=1, max_val=MAX_ROUNDS)
            pool.wait_ge(last_in, 16)
            for idx_ready, used, landed in ((idx1_ready, max1_done, (rows1_in, rows1_b)), (idx2_ready, used2, (rows2_in, rows2_b))):
                with pool.Fori(0, total) as r:
                    pool.wait_ge(idx_ready, r + 2)
                    pool.sem_inc(pool_passed, 1)
                    for half in range(2):
                        pool.wait_ge(used, 2 * r + half + 1)
                        pool.sem_inc(pool_passed, 1)
                        for k in range(HALFR):
                            c = half * HALFR + k
                            pool.indirect_dma_start(rows_g[:, half, k, :], None, table_d,
                                                    bass.IndirectOffsetOnAxis(ap=g_idx[:, c:c + 1], axis=0)).then_inc(landed[half], 16)

        @block.scalar
        def _(act):
            def norm(ln, between=None):
                with act.Fori(0, IMGS) as n:
                    for h in range(2):
                        i = 2 * n + h
                        act.wait_ge(ln.centred, i + 3)
                        act.wait_ge(ln.var_ready, i + 1)
                        nc.scalar.activation(sq[:, h, :], T[:, i, :], ACT.Square).then_inc(ln.squared, 1)
                if between is not None:
                    between()
                act.wait_ge(ln.var_ready, CHUNKS + 2)
                nc.scalar.activation(dev[:, :], ps[2][:, 0:TILES], ACT.Sqrt, bias=eps[:, ln.eps:ln.eps + 1]).then_inc(ln.std_ready, 1)

            def key_tests(q):
                cols = bass.ts(q, KEY_PART)
                act.wait_ge(e_step, 10 * q + 7)
                act.sem_inc(act_passed, 1)
                nc.scalar.activation(k_src, src_i[:, cols], ACT.Relu, scale=-float(NODES)).then_inc(k_front, 1)
                act.wait_ge(e_step, 10 * q + 8)
                act.sem_inc(act_passed, 1)
                nc.scalar.activation(k_last, dst_i[:, cols], ACT.Identity, bias=k_bias[:, 0:1], scale=-1.0).then_inc(k_front, 1)
                act.wait_ge(e_step, 10 * q + 10)
                act.sem_inc(act_passed, 1)
                nc.scalar.activation(k_node, dst_i[:, cols], ACT.Abs, bias=k_bias[:, 1:2]).then_inc(k_tests, 1)
                act.wait_ge(k_tests, 2 * q + 1)
                act.sem_inc(act_passed, 1)
                nc.scalar.activation(k_node, k_node, ACT.Identity, bias=k_bias[:, 2:3], scale=-SURE).then_inc(k_tests, 1)
                act.wait_ge(e_step, 10 * q + 14)
                act.sem_inc(act_passed, 1)
                nc.scalar.activation(k_gen, k_src, ACT.Identity, bias=k_bias[:, 3:4], scale=-SURE).then_inc(k_gens, 1)

            act.wait_ge(made, 10)
            norm(ln0, lambda: (act.wait_ge(edges_in, 32), key_tests(0)))
            with act.Fori(1, ECOLS // KEY_PART) as q:
                key_tests(q)
            act.sem_inc(msk_row_s, 2)
            act.wait_ge(wa_in, WA)
            act.wait_ge(e_step, 10 * (ECOLS // KEY_PART) + 10)
            with act.Fori(0, IMGS) as n:
                for h in range(2):
                    i = 2 * n + h
                    act.wait_ge(off_ready, i + 1)
                    act.wait_ge(msk_done, i + 1)
                    nc.scalar.activation(msk_row, bank_of(i, slice(32, 32 + TAPS)), ACT.Sigmoid,
                                         bias=b_off[32:32 + TAPS, :]).then_inc(msk_row_s, 1)
            act.wait_ge(batches_known, 1)
            is_far = act.value_load(num[0:1, N_FAR:N_FAR + 1], min_val=0, max_val=1)
            with act.If(is_far > 0):
                act.sem_inc(abs_done, 4)
                act.sem_inc(ax_done, 1)
                with act.Fori(0, IMGS) as n:
                    with act.Fori(0, TAPS) as k:
                        for h in range(2):
                            u = (n * TAPS + k) * 2 + h
                            act.wait_ge(bc_ready, u + 1)
                            act.wait_ge(txm_done, u + 1)
                            nc.scalar.activation(absx[:, h, :], ps[2][:, :], ACT.Abs, bias=neg_x[:, :]).then_inc(ax_done, 1)
                            act.wait_ge(ax_done, u + 2)
                            nc.scalar.activation(absx[:, h, :], absx[:, h, :], ACT.Relu, bias=1.0, scale=-1.0).then_inc(rx_done, 1)
                            for g in range(2):
                                b, v = 2 * h + g, 2 * u + g
                                act.wait_ge(main_done, v + 1)
                                for j in range(GROUP):
                                    t = GROUP * g + j
                                    last = nc.scalar.activation(TEN[:, b, j, :], ps[h][:, :], ACT.Abs, bias=neg_y[:, t:t + 1])
                                last.then_inc(abs_done, 1)
                                act.wait_ge(abs_done, v + 5)
                                nc.scalar.activation(TEN[:, b, :, :], TEN[:, b, :, :], ACT.Relu, bias=1.0,
                                                     scale=-1.0).then_inc(relu_done, 1)
                act.nop()
            with act.If(is_far < 1):
                act.sem_inc(abs_done, 2)
                act.sem_inc(ax_done, 1)
                with act.Fori(0, IMGS) as n:
                    with act.Fori(0, TAPS // RING) as q:
                        for s in range(2 * RING):
                            u, h, w = n * (2 * TAPS) + q * (2 * RING) + s, s % 2, near_w[s % RING]
                            act.wait_ge(bc_ready, u + 1)
                            act.wait_ge(txm_done, u + 1)
                            nc.scalar.activation(absx[:, h, :], ps[2][:, :], ACT.Abs, bias=neg_x[:, :]).then_inc(ax_done, 1)
                            act.wait_ge(main_done, u + 1)
                            for t, j, c, slot in near_tiles(h):
                                last = nc.scalar.activation(w[:, slot:slot + 2 * c - 1:2, :],
                                                            ps[h][:, j * P:(j + c) * P].rearrange("p (k c) -> p k c", k=c),
                                                            ACT.Abs, bias=neg_y[:, t:t + 1])
                            last.then_inc(abs_done, 1)
                            act.wait_ge(ax_done, u + 2)
                            nc.scalar.activation(absx[:, h, :], absx[:, h, :], ACT.Relu, bias=1.0, scale=-1.0).then_inc(rx_done, 1)
                            act.wait_ge(abs_done, u + 3)
                            used = w[:, 1 - h:4 * NEAR - h, :]
                            nc.scalar.activation(used, used, ACT.Relu, bias=1.0, scale=-1.0).then_inc(relu_done, 1)
                act.nop()
            norm(ln1)
            act.wait_ge(wb_in, WB_)
            act.sem_inc(gelu_done, 2)
            act.sem_inc(yf_done, 2)
            act.wait_ge(col_done, 1)
            with act.Fori(0, IMGS) as n:
                for h in range(2):
                    i = 2 * n + h
                    for c in range(HID):
                        act.wait_ge(h_ready, HID * i + c + 1)
                        nc.scalar.activation(hid[h][:, c, :], ps[4 + c % 2][:, :], ACT.Gelu_apprx_tanh,
                                             bias=f_b1[:, c:c + 1]).then_inc(gelu_done, 1)
                    act.wait_ge(y_ready, i + 1)
                    nc.scalar.activation(YF[:, i, :], ps[6 + h][:, :], ACT.Identity, bias=f_b2[:, :]).then_inc(yf_done, 1)
            norm(ln2)
            act.wait_ge(made2, 5)
            batches = act.value_load(num[0:1, N_BATCH:N_BATCH + 1], min_val=1, max_val=MAX_BATCHES)
            act.sem_inc(turned_out, 2)
            with act.Fori(0, batches) as b:
                act.wait_ge(batch_ready, b + 1)
                for q in range(BATCH // 4):
                    act.wait_ge(turned, b * (BATCH // 4) + q + 2)
                    nc.scalar.activation(routed[:, q * CHUNK:(q + 1) * CHUNK], ps[4 + q % 2][:, :], ACT.Relu,
                                         bias=neg_lo[:, :]).then_inc(turned_out, 1)
            norm(ln3)
            act.wait_ge(rounds_known, 1)
            act.wait_ge(wc_in, WC)
            act.sem_inc(mid_done, 2)
            act.sem_inc(my_done, 2)

            def hidden(i, e):
                v = EXPERTS * i + e
                act.wait_ge(my_ready, v + 1)
                for c in range(2):
                    act.wait_ge(mid_ready, 2 * v + c + 1)
                    nc.scalar.activation(mid[:, e % 2, c, :], ps[2 + c][:, :], ACT.Gelu, bias=m_b1[:, e, c:c + 1]).then_inc(mid_done, 1)

            def expert_out(i, e):
                v = EXPERTS * i + e
                act.wait_ge(my_ready, v + 3)
                nc.scalar.activation(y_exp[e][:, i, :], ps[4 + e % 2][:, :], ACT.Identity, bias=m_b2[:, e:e + 1]).then_inc(my_done, 1)

            with act.Fori(0, CHUNKS) as i:
                hidden(i, 0)
                for e in range(1, EXPERTS):
                    hidden(i, e)
                    expert_out(i, e - 1)
                expert_out(i, EXPERTS - 1)
            total = act.value_load(num[0:1, N_ALL:N_ALL + 1], min_val=1, max_val=MAX_ROUNDS)
            with act.Fori(0, total) as r:
                for half in range(2):
                    act.wait_ge(got2, 2 * r + half + 1)
                    nc.scalar.activation(vals[:, :, 0:HEADS], z[:, :, :], ACT.Exp).then_inc(exp2, 1)
            act.wait_ge(f_ask, 1)
            nc.scalar.activation(cand[:, :, :], cand[:, :, :], ACT.Exp).then_inc(f_exp, 1)
            act.wait_ge(f_ask, 2)
            nc.scalar.activation(s_max[:, :, :], s_max[:, :, :], ACT.Exp).then_inc(f_exp, 1)
            act.wait_ge(f_ask, 3)
            nc.scalar.activation(stat[:, 1, :], stat[:, 1, :], ACT.Sqrt, bias=eps[:, 1:2]).then_inc(f_exp, 1)
            act.wait_ge(f_ask, 4)
            nc.scalar.activation(gate[:, :, :], gate[:, :, :], ACT.Exp).then_inc(f_exp, 1)

        @block.vector
        def _(dve):
            def norm(ln, res, credit, between=(None, None)):
                dve.sem_inc(ln.centred, 2)
                with dve.Fori(0, IMGS) as n:
                    for h in range(2):
                        i = 2 * n + h
                        if res is not None:
                            dve.wait_ge(res, i + credit + 1)
                        dve.wait_ge(ln.mean_ready, i + 1)
                        nc.vector.tensor_tensor(T[:, i, :], X[:, i, :], ps[h][:, :], ALU.subtract).then_inc(ln.centred, 1)
                if between[0] is not None:
                    between[0]()
                dve.wait_ge(ln.std_ready, 1)
                nc.vector.reciprocal(inv[:, :], dev[:, :]).then_inc(ln.inv_ready, 1)
                if between[1] is not None:
                    between[1]()
                dve.sem_inc(ln.normed, 2)
                with dve.Fori(0, IMGS) as n:
                    for h in range(2):
                        i = 2 * n + h
                        dve.wait_ge(ln.spread, i + 1)
                        nc.vector.tensor_tensor(T[:, i, :], T[:, i, :], ps[6 + h][:, :], ALU.mult).then_inc(ln.normed, 1)

            def chained(s_, first=0, apart=False):
                n = [0]

                def run(ins):
                    n[0] += 1
                    ins.then_inc(s_, 1)
                    dve.wait_ge(s_, first + n[0])
                    if apart:
                        dve.sem_inc(passed, 1)
                return run, n

            def make_keys(q):
                cols = bass.ts(q, KEY_PART)
                run, n = chained(e_step, 10 * q + 10)
                dve.wait_ge(k_front, 2 * q + 1)
                run(nc.vector.scalar_tensor_tensor(k_src, k_src, float(NODES), src_i[:, cols], ALU.min, ALU.add))
                run(nc.vector.tensor_scalar(k_lo, dst_i[:, cols], 0.0, float(LAST), ALU.max, ALU.min))
                run(nc.vector.tensor_scalar(k_hi, k_lo, 7, None, ALU.logical_shift_right))
                run(nc.vector.tensor_scalar(k_src, k_src, 0.0, float(LAST), ALU.max, ALU.min))
                run(nc.vector.scalar_tensor_tensor(k_key, k_hi, 4096.0, k_src, ALU.mult, ALU.add))
                run(nc.vector.scalar_tensor_tensor(k_lo, k_hi, -float(P), k_lo, ALU.mult, ALU.add))
                dve.wait_ge(k_gens, q + 1)
                run(nc.vector.tensor_tensor(k_gen, k_gen, k_last, ALU.max))
                run(nc.vector.scalar_tensor_tensor(k_key, k_lo, float(1 << 17), k_key, ALU.mult, ALU.add))
                run(nc.vector.tensor_tensor(k_key, k_key, k_gen, ALU.min))
                dve.wait_ge(k_tests, 2 * q + 2)
                run(nc.vector.scalar_tensor_tensor(keys[:, cols], k_node, NONE, k_key, ALU.max, ALU.min))
                assert n[0] == 10

            def first_keys():
                dve.wait_ge(edges_in, 32)
                make_keys(0)

            dve.sem_inc(e_step, 10)
            dve.wait_ge(x_in, 16 * IMGS)
            norm(ln0, None, 0, (first_keys, lambda: make_keys(1)))
            with dve.Fori(2, ECOLS // KEY_PART) as q:
                make_keys(q)
            run, _ = chained(e_chain)
            run(nc.vector.memset(listed, NONE))
            for c in range(ECOLS // FIRST):
                last = nc.vector.max(listed[:, 8 * c:8 * c + 8], keys[:, FIRST * c:FIRST * (c + 1)])
            run(last)
            for c in range(ECOLS // FIRST):
                part = keys[:, FIRST * c:FIRST * (c + 1)]
                last = nc.vector.match_replace(part, listed[:, 8 * c:8 * c + 8], part, NONE)
            run(last)
            dve.wait_ge(wa_in, WA)
            dve.sem_inc(off_done, 2)
            with dve.Fori(0, IMGS) as n:
                for h in range(2):
                    i = 2 * n + h
                    dve.wait_ge(off_ready, i + 1)
                    dve.wait_ge(off_done, i + 2)
                    nc.vector.scalar_tensor_tensor(off_row, bank_of(i, slice(0, 2 * TAPS)), b_off[0:2 * TAPS, :],
                                                   base[:, h * CHUNK:(h + 1) * CHUNK], ALU.add, ALU.add).then_inc(off_a, 1)
                    dve.wait_ge(off_a, i + 1)
                    nc.vector.tensor_copy(OFS[0:2 * TAPS, i, :], off_row).then_inc(off_hi, 1)
                    dve.wait_ge(off_hi, i + 1)
                    nc.vector.tensor_tensor(off_rem, off_row, OFS[0:2 * TAPS, i, :], ALU.subtract).then_inc(off_r, 1)
                    dve.wait_ge(off_r, i + 1)
                    nc.vector.tensor_copy(off_mid, off_rem).then_inc(off_m, 1)
                    dve.wait_ge(off_m, i + 1)
                    nc.vector.tensor_copy(OFS[32:32 + 2 * TAPS, i, :], off_mid)
                    nc.vector.tensor_tensor(OFS[64:64 + 2 * TAPS, i, :], off_rem, off_mid, ALU.subtract).then_inc(off_done, 1)
                    nc.vector.tensor_tensor(off_sq, off_row, base[:, h * CHUNK:(h + 1) * CHUNK], ALU.subtract).then_inc(far_chain, 1)
                    dve.wait_ge(far_chain, 3 * i + 1)
                    nc.vector.tensor_tensor(off_sq, off_sq, off_sq, ALU.mult).then_inc(far_chain, 1)
                    dve.wait_ge(far_chain, 3 * i + 2)
                    nc.vector.tensor_reduce(far[:, bass.ds(i, 1)], off_sq, AX_X, ALU.max).then_inc(far_chain, 1)
                    dve.wait_ge(far_chain, 3 * i + 3)
            dve.wait_ge(msk_done, 1 + CHUNKS)
            dve.wait_ge(made2, 5)
            run(nc.vector.memset(counts[:, :], 0.0))
            run(nc.vector.tensor_scalar(flags, keys, NONE + 1, None, ALU.is_gt))
            run(nc.vector.tensor_reduce(counts[:, 0:1], flags, AX_X, ALU.add))
            run(nc.vector.tensor_reduce(counts[0:2 * TAPS, 1:2], far[:, :], AX_X, ALU.max))
            dve.sem_inc(counted, 1)
            dve.wait_ge(reduced, 1)
            run(nc.vector.tensor_scalar(num[:, N_FAR:N_FAR + 1], counts_max[:, 1:2], FAR, None, ALU.is_gt))
            run(nc.vector.tensor_scalar(num[:, N_LEFT:N_LEFT + 1], counts_max[:, 0:1], 7.0, None, ALU.add))
            run(nc.vector.tensor_scalar(num[:, N_LEFT:N_LEFT + 1], num[:, N_LEFT:N_LEFT + 1], 3, None, ALU.logical_shift_right))
            run(nc.vector.tensor_scalar(num[:, N_LEFT:N_LEFT + 1], num[:, N_LEFT:N_LEFT + 1], 1.0, None, ALU.max))
            lefts = dve.value_load(num[0:1, N_LEFT:N_LEFT + 1], min_val=1, max_val=(ECOLS - KEPT1) // 8)
            dve.sem_inc(left_known, 1)
            with dve.Fori(0, lefts) as r:
                step, _ = chained(r_chain, r * 3, True)
                step(nc.vector.max(top8[:, :], keys))
                step(nc.vector.tensor_copy(listed[:, bass.ds(KEPT1 + 8 * r, 8)], top8[:, :]))
                step(nc.vector.match_replace(keys, top8[:, :], keys, NONE))
            code = code_i[:, 0:KEPT1]
            run(nc.vector.tensor_scalar(code, listed[:, 0:KEPT1], -1.0, -1.0, ALU.mult, ALU.add))
            run(nc.vector.tensor_scalar(code_i[:, KEPT1:2 * KEPT1], code, P - 1, None, ALU.bitwise_and))
            run(nc.vector.tensor_copy(lo_b[:, :], code_i[:, KEPT1:2 * KEPT1]))
            run(nc.vector.tensor_scalar(code, code, 7, None, ALU.arith_shift_right))
            run(nc.vector.tensor_copy(hi_b[:, :], code))
            with dve.Fori(0, lefts) as r:
                step, _ = chained(left_coded, r * 7)
                step(nc.vector.tensor_scalar(left_i[:, 0, :], listed[:, bass.ds(KEPT1 + 8 * r, 8)], -1.0, -1.0, ALU.mult, ALU.add))
                step(nc.vector.tensor_scalar(left_i[:, 1, :], left_i[:, 0, :], P - 1, None, ALU.bitwise_and))
                step(nc.vector.tensor_scalar(left_i[:, 0, :], left_i[:, 0, :], 7, None, ALU.arith_shift_right))
                step(nc.vector.tensor_copy(left_b[:, 0, :], left_i[:, 0, :]))
                step(nc.vector.tensor_copy(left_b[:, 1, :], left_i[:, 1, :]))
                dve.wait_ge(left_added, r + 1)
                step(nc.vector.tensor_tensor(oh_lo[:, 0, 0:8, :], left_b[:, 1, :].unsqueeze(2).to_broadcast([P, 8, P]),
                                             lane_b[:, :].unsqueeze(1).to_broadcast([P, 8, P]), ALU.is_equal))
                step(nc.vector.tensor_tensor(oh_hi[:, 0, 0:8, :], left_b[:, 0, :].unsqueeze(2).to_broadcast([P, 8, HIS]),
                                             lane_b[:, 0:HIS].unsqueeze(1).to_broadcast([P, 8, HIS]), ALU.is_equal))
            dve.wait_ge(left_added, lefts + 1)
            run(nc.vector.tensor_copy(to_last[:, :], ps[7][:, 0:HIS]))
            run(nc.vector.memset(generic[:, :], 0.0))
            run(nc.vector.tensor_scalar(keys, listed, 1.0, 0.0, ALU.add, ALU.max))
            run(nc.vector.tensor_scalar(flags, keys, 0.5, None, ALU.is_gt))
            run(nc.vector.tensor_reduce(counts[:, 0:1], flags[:, 0:KEPT1], AX_X, ALU.add))
            run(nc.vector.tensor_reduce(counts[:, 1:2], flags[:, KEPT1:ECOLS], AX_X, ALU.add))
            dve.sem_inc(counted, 1)
            dve.wait_ge(reduced, 2)
            ab = num[:, N_A:N_B + 1]
            run(nc.vector.tensor_scalar(ab, counts_max[:, :], 7.0, None, ALU.add))
            run(nc.vector.tensor_scalar(ab, ab, 3, None, ALU.logical_shift_right))
            run(nc.vector.tensor_scalar(num[:, N_A:N_A + 1], num[:, N_A:N_A + 1], 1.0, None, ALU.max))
            run(nc.vector.tensor_tensor(num[:, N_BATCH:N_BATCH + 1], num[:, N_A:N_A + 1], num[:, N_B:N_B + 1], ALU.add))
            run(nc.vector.tensor_scalar(num[:, N_BATCH:N_BATCH + 1], num[:, N_BATCH:N_BATCH + 1], float(BATCH // 8 - 1),
                                        float((1 << 18) // (BATCH // 8) + 1), ALU.add, ALU.mult))
            run(nc.vector.tensor_scalar(num[:, N_BATCH:N_BATCH + 1], num[:, N_BATCH:N_BATCH + 1], 18, None, ALU.logical_shift_right))
            run(nc.vector.memset(num[:, N_ALL:N_ALL + 1], 0))
            in_a = dve.value_load(num[0:1, N_A:N_A + 1], min_val=1, max_val=KEPT1 // 8)
            in_b = dve.value_load(num[0:1, N_B:N_B + 1], min_val=0, max_val=(ECOLS - KEPT1) // 8)
            batches = dve.value_load(num[0:1, N_BATCH:N_BATCH + 1], min_val=1, max_val=MAX_BATCHES)
            dve.sem_inc(batches_known, 1)
            with dve.Fori(0, in_a) as r:
                step, _ = chained(rb_chain, r * 3, True)
                part = keys[:, 0:KEPT1]
                step(nc.vector.max(top8[:, :], part))
                step(nc.vector.tensor_copy(generic[:, bass.ds(8 * r, 8)], top8[:, :]))
                step(nc.vector.match_replace(part, top8[:, :], part, 0.0))
            with dve.If(in_b > 0):
                with dve.Fori(0, in_b) as r:
                    step, _ = chained(rb_chain, (in_a + r) * 3, True)
                    part = keys[:, KEPT1:ECOLS]
                    step(nc.vector.max(top8[:, :], part))
                    step(nc.vector.tensor_copy(generic[:, bass.ds(8 * (in_a + r), 8)], top8[:, :]))
                    step(nc.vector.match_replace(part, top8[:, :], part, 0.0))
                dve.nop()
            dve.sem_inc(generic_made, 1)
            dve.wait_ge(generic_out, 16)
            def weights(n, k, h):
                u = (n * TAPS + k) * 2 + h
                dve.wait_ge(rx_done, u + 1)
                dve.wait_ge(ten_done, 2 * u + 2)
                nc.vector.tensor_tensor(txm[:, h, :], absx[:, h, :], ps[3][:, :], ALU.mult).then_inc(txm_done, 1)
                dve.wait_ge(txm_done, u + 3)
                for g in range(2):
                    b, v = 2 * h + g, 2 * u + g
                    dve.wait_ge(relu_done, v + 1)
                    nc.vector.tensor_tensor(TEN[:, b, :, :], TEN[:, b, :, :],
                                            txm[:, h:h + 1, :].to_broadcast([P, GROUP, CHUNK]), ALU.mult).then_inc(ten_done, 1)

            def one_hot(n, k, h):
                u = PIECES * n + 2 * k + h
                dve.wait_ge(piece_added, u + 1)
                cols = bass.ds(u * PIECE, PIECE)
                nc.vector.tensor_tensor(oh_lo[:, h, :, :], lo_b[:, cols].unsqueeze(2).to_broadcast([P, PIECE, P]),
                                        lane_b[:, :].unsqueeze(1).to_broadcast([P, PIECE, P]), ALU.is_equal)
                nc.vector.tensor_tensor(oh_hi[:, h, :, :], hi_b[:, cols].unsqueeze(2).to_broadcast([P, PIECE, HIS]),
                                        lane_b[:, 0:HIS].unsqueeze(1).to_broadcast([P, PIECE, HIS]), ALU.is_equal).then_inc(piece_made, 1)

            def image_sums(n):
                dve.wait_ge(piece_added, PIECES * (n + 1) + 2)
                nc.vector.tensor_tensor(to_last[:, :], to_last[:, :], ps[7][:, 0:HIS], ALU.add).then_inc(shares_added, 1)
                for h in range(2):
                    i = 2 * n + h
                    nc.vector.tensor_tensor(X[:, i, :], X[:, i, :], ps[4 + h][:, :], ALU.add).then_inc(res1, 1)

            is_far = dve.value_load(num[0:1, N_FAR:N_FAR + 1], min_val=0, max_val=1)
            dve.sem_inc(txm_done, 2)
            dve.sem_inc(shares_added, 1)
            dve.sem_inc(res1, 2)
            with dve.If(is_far > 0):
                dve.sem_inc(ten_done, 4)
                dve.sem_inc(yt_done, 2)
                with dve.Fori(0, IMGS) as n:
                    dve.wait_ge(main_done, 4 + 4 * TAPS * n)
                    for q in range(3 * SRC_T):
                        t, g = divmod(q, 3)
                        w = min(CHUNK, TAPS * P - g * CHUNK)
                        dve.wait_ge(yt_ready, 3 * SRC_T * n + q + 1)
                        nc.vector.tensor_copy(YT[:, t, g * CHUNK:g * CHUNK + w], ps[6 + q % 2][:, 0:w]).then_inc(yt_done, 1)
                    with dve.Fori(0, PIECES // 2) as k:
                        for h in range(2):
                            weights(n, k, h)
                            one_hot(n, k, h)
                    for k in range(PIECES // 2, TAPS):
                        for h in range(2):
                            weights(n, k, h)
                    dve.wait_ge(main_done, 4 + 4 * TAPS * (n + 1))
                    image_sums(n)
                dve.nop()
            with dve.If(is_far < 1):
                dve.sem_inc(ten_done, 2)
                dve.sem_inc(yt_done, 1)

                def keep_tap(n, k, r, h):
                    w = n * (2 * TAPS) + 2 * k + h
                    dve.wait_ge(yt_ready, w + 1)
                    nc.vector.tensor_copy(YTN[:, r, 4 * h:4 * h + 4, :], ps[6][:, :].rearrange("p (t c) -> p t c", c=P)).then_inc(yt_done, 1)

                def near_unit(n, q, s, ahead=True, coded=True):
                    u, h, k = n * (2 * TAPS) + q * (2 * RING) + s, s % 2, q * RING + s // 2
                    dve.wait_ge(rx_done, u + 1)
                    dve.wait_ge(ten_done, u + 1)
                    dve.wait_ge(ten_pool, u + 1)
                    nc.vector.tensor_tensor(txm[:, h, :], absx[:, h, :], ps[3][:, :], ALU.mult).then_inc(txm_done, 1)
                    dve.wait_ge(txm_done, u + 3)
                    dve.wait_ge(relu_done, u + 1)
                    near_mult(nc.vector, s % RING, h, DVE_BLOCKS[h]).then_inc(ten_done, 1)
                    if ahead:
                        keep_tap(n, k + 1, (s // 2 + 1) % RING, h)
                    if coded:
                        one_hot(n, k, h)

                with dve.Fori(0, IMGS) as n:
                    for h in range(2):
                        keep_tap(n, 0, 0, h)
                    with dve.Fori(0, TAPS // RING - 1) as q:
                        for s in range(2 * RING):
                            near_unit(n, q, s)
                    for s in range(2 * RING):
                        at = (TAPS // RING - 1) * 2 * RING + s
                        near_unit(n, TAPS // RING - 1, s, s < 2 * RING - 2, at < PIECES)
                    dve.wait_ge(main_done, 2 * TAPS * (n + 1) + RING)
                    image_sums(n)
                dve.nop()
            dve.wait_ge(wb_in, WB_)
            nc.vector.tensor_copy(wr_b[:, :], wr[:, 0:1].to_broadcast([P, P])).then_inc(wrb_done, 1)
            norm(ln1, res1, 2)
            dve.wait_ge(wb_in, WB_)
            dve.sem_inc(rw_done, 2)
            with dve.Fori(0, IMGS) as n:
                for h in range(2):
                    i = 2 * n + h
                    dve.wait_ge(rw_ready, i + 1)
                    nc.vector.tensor_scalar(RW[:, i, :], ps[h][:, :], br_b[:, :], None, ALU.add).then_inc(rw_done, 1)
            dve.wait_ge(rw_done, 2 + CHUNKS)
            nc.vector.tensor_tensor(YF[:, :, :].rearrange("p a (b c) -> p (a b) c", c=P),
                                    RW[:, :, :].rearrange("p a (b c) -> p (a b) c", c=P),
                                    ident[:, :].unsqueeze(1).to_broadcast([P, TILES, P]), ALU.mult).then_inc(diag_done, 1)
            dve.wait_ge(diag_done, 1)
            nc.vector.tensor_reduce(w_col[:, :, :].rearrange("p n t -> p (n t)"),
                                    YF[:, :, :].rearrange("p a (b c) -> p (a b) c", c=P), AX_X, ALU.add).then_inc(col_done, 1)
            dve.wait_ge(col_done, 1)
            dve.sem_inc(rank_ready, 1)
            dve.sem_inc(kept_done, 2)
            with dve.Fori(0, IMGS) as n:
                dve.wait_ge(rank_ready, n + 1)
                rows = image(RW)
                for t in range(SRC_T):
                    own = w_col[:, n, t:t + 1]
                    e = (t + 1) * P
                    nc.vector.tensor_scalar(tie[:, :], rows[:, n, e - P:e], own, None, ALU.is_equal).then_inc(cmp_part, 1)
                    nc.vector.tensor_scalar(cmp_b[:, t, 0:e], rows[:, n, 0:e], own, None, ALU.is_lt).then_inc(cmp_part, 1)
                    if e < POS:
                        nc.vector.tensor_scalar(cmp_b[:, t, e:], rows[:, n, e:], own, None, ALU.is_le)
                    dve.wait_ge(cmp_part, (n * SRC_T + t) * 3 + 2)
                    nc.vector.tensor_tensor(tie[:, :], tie[:, :], later[:, :], ALU.mult).then_inc(cmp_part, 1)
                    dve.wait_ge(cmp_part, (n * SRC_T + t) * 3 + 3)
                    nc.vector.tensor_tensor(cmp_b[:, t, e - P:e], cmp_b[:, t, e - P:e], tie[:, :], ALU.add).then_inc(cmp_done, 1)
                    dve.wait_ge(cmp_done, n * SRC_T + t + 1)
                dve.wait_ge(rank_ready, n + 2)
                for h in range(2):
                    nc.vector.scalar_tensor_tensor(RW[:, 2 * n + h, :], ps[2 + h][:, :], float(KEPT), RW[:, 2 * n + h, :],
                                                   ALU.is_lt, ALU.mult).then_inc(kept_done, 1)
            with dve.Fori(0, CHUNKS) as i:
                dve.wait_ge(yf_done, i + 3)
                dve.wait_ge(kept_done, i + 3)
                nc.vector.tensor_tensor(YF[:, i, :], YF[:, i, :], RW[:, i, :], ALU.mult).then_inc(fin_a, 1)
                dve.wait_ge(fin_a, i + 1)
                nc.vector.tensor_tensor(YF[:, i, :], YF[:, i, :], T[:, i, :], ALU.add).then_inc(fin_b, 1)
                dve.wait_ge(fin_b, i + 1)
                nc.vector.tensor_tensor(X[:, i, :], X[:, i, :], YF[:, i, :], ALU.add).then_inc(res2, 1)
            norm(ln2, res2, 0)
            BATCH_STEPS = 22
            dve.sem_inc(round_stored, 16)
            with dve.Fori(0, batches) as b:
                run, n = chained(b_chain, b * BATCH_STEPS, True)
                dve.sem_inc(batch_ready, 1)
                dve.wait_ge(turned_out, (b + 1) * (BATCH // 4) + 2)
                run(nc.vector.scalar_tensor_tensor(routed, routed, float(1 << 17), routed, ALU.is_le, ALU.mult))
                parts = routed.rearrange("p (s c) -> p c s", c=BCHUNKS)
                for c in range(BCHUNKS):
                    last = nc.vector.max(kept2[:, 8 * c:8 * c + 8], parts[:, c, :])
                run(last)
                fl = wide_buf[:, BATCH * P:BATCH * P + ECOLS]
                run(nc.vector.tensor_scalar(fl[:, 0:KEPT2], kept2[:, :], 0.5, None, ALU.is_gt))
                run(nc.vector.tensor_reduce(counts[:, 0:1], fl[:, 0:KEPT2], AX_X, ALU.add))
                run(nc.vector.tensor_reduce(counts[:, 1:2], kept2[:, :].rearrange("p (c k) -> p c k", k=8)[:, :, 7], AX_X, ALU.max))
                dve.sem_inc(counted, 1)
                dve.wait_ge(reduced, 2 * b + 3)
                dve.sem_inc(passed, 1)
                before = dve.value_load(num[0:1, N_ALL:N_ALL + 1], min_val=0, max_val=MAX_ROUNDS)
                dve.wait_ge(round_stored, before * 16 + 16)
                dve.sem_inc(passed, 1)
                e_ab = num[:, N_EA:N_EB + 1]
                run(nc.vector.tensor_scalar(e_ab, counts_max[:, :], float(ROUND - 1), None, ALU.add))
                run(nc.vector.tensor_scalar(e_ab, e_ab, 4, None, ALU.logical_shift_right))
                run(nc.vector.memset(counts[:, 1:2], 0.0))
                full = dve.value_load(num[0:1, N_EB:N_EB + 1], min_val=0, max_val=(1 << 17) // ROUND)
                with dve.If(full > 0):
                    for c in range(BCHUNKS):
                        last = nc.vector.match_replace(parts[:, c, :], kept2[:, 8 * c:8 * c + 8], parts[:, c, :], 0.0)
                    run(last)
                    for c in range(BATCH * P // ECOLS):
                        run(nc.vector.tensor_scalar(fl, routed[:, c * ECOLS:(c + 1) * ECOLS], 0.5, None, ALU.is_gt))
                        run(nc.vector.tensor_reduce(rest_n[:, c:c + 1], fl, AX_X, ALU.add))
                    run(nc.vector.tensor_reduce(counts[:, 1:2], rest_n[:, :], AX_X, ALU.add))
                with dve.If(full < 1):
                    dve.sem_inc(b_chain, 2 * (BATCH * P // ECOLS) + 2)
                dve.sem_inc(counted, 1)
                dve.wait_ge(reduced, 2 * b + 4)
                dve.sem_inc(passed, 1)
                run(nc.vector.tensor_scalar(num[:, N_EB:N_EB + 1], counts_max[:, 1:2], float(ROUND - 1), None, ALU.add))
                run(nc.vector.tensor_scalar(num[:, N_EB:N_EB + 1], num[:, N_EB:N_EB + 1], 4, None, ALU.logical_shift_right))
                run(nc.vector.tensor_scalar(num[:, N_EA:N_EA + 1], num[:, N_EA:N_EA + 1], 1.0, None, ALU.max))
                run(nc.vector.tensor_copy(num[:, N_BASE:N_BASE + 1], num[:, N_ALL:N_ALL + 1]))
                run(nc.vector.tensor_tensor(num[:, N_ALL:N_ALL + 1], num[:, N_ALL:N_ALL + 1], num[:, N_EA:N_EA + 1], ALU.add))
                run(nc.vector.tensor_tensor(num[:, N_ALL:N_ALL + 1], num[:, N_ALL:N_ALL + 1], num[:, N_EB:N_EB + 1], ALU.add))
                ea = dve.value_load(num[0:1, N_EA:N_EA + 1], min_val=1, max_val=KEPT2 // ROUND)
                eb = dve.value_load(num[0:1, N_EB:N_EB + 1], min_val=0, max_val=(BATCH * P - KEPT2) // ROUND)
                first = dve.value_load(num[0:1, N_BASE:N_BASE + 1], min_val=0, max_val=MAX_ROUNDS - BATCH * P // ROUND)
                dve.sem_inc(batch_known, 1)

                def emit(at, part):
                    step, _ = chained(r2_chain, at * 4, True)
                    dve.wait_ge(round_stored, at * 16 + 16)
                    dve.sem_inc(passed, 1)
                    for k in range(2):
                        step(nc.vector.max(round_k[:, 8 * k:8 * k + 8], part))
                        step(nc.vector.match_replace(part, round_k[:, 8 * k:8 * k + 8], part, 0.0))
                    dve.sem_inc(round_ready, 1)

                with dve.Fori(0, ea) as r:
                    emit(first + r, kept2[:, :])
                with dve.If(eb > 0):
                    with dve.Fori(0, eb) as r:
                        emit(first + ea + r, routed)
                    dve.nop()
                assert n[0] == BATCH_STEPS
                dve.nop()
            dve.sem_inc(rounds_known, 1)
            dve.sem_inc(res3, 2)
            with dve.Fori(0, IMGS) as n:
                for h in range(2):
                    i = 2 * n + h
                    dve.wait_ge(cv_ready, i + 1)
                    nc.vector.tensor_tensor(X[:, i, :], X[:, i, :], bank_of(i), ALU.add).then_inc(res3, 1)
            norm(ln3, res3, 2)
            run, _ = chained(t_chain)
            dve.wait_ge(wc_in, WC)
            dve.wait_ge(feat_ready, 1)
            feats = table[:, :, 0:HE]
            run(nc.vector.tensor_copy(feats, ps[0][:, :].rearrange("p (t f) -> p t f", f=HE)))
            for k, o in ((0, table[:, :, HE:ROW]), (1, a_dst[:, :, :])):
                run(nc.vector.tensor_tensor(prod[:, :, :], feats, att[:, k:k + 1, :].to_broadcast([P, HIS, HE]), ALU.mult))
                run(nc.vector.tensor_reduce(o, prod[:, :, :].rearrange("p t (h e) -> p t h e", h=HEADS), AX_X, ALU.add))
                if k == 0:
                    dve.sem_inc(table_ready, 1)
            a_src = table[:, :, HE:ROW]
            run(nc.vector.tensor_scalar(pen[:, :], to_last[:, :], 0.5, -BIG, ALU.is_lt, ALU.mult))
            dve.wait_ge(last_in, 16)
            run(nc.vector.tensor_tensor(cand[:, :, :], pen[:, :].unsqueeze(2).to_broadcast([P, HIS, HEADS]),
                                        last_row[:, HE:ROW].unsqueeze(1).to_broadcast([P, HIS, HEADS]), ALU.add))
            run(nc.vector.tensor_tensor(s_max[:, :, :], cand[:, :, :], a_src, ALU.max))
            total = dve.value_load(num[0:1, N_ALL:N_ALL + 1], min_val=1, max_val=MAX_ROUNDS)

            def decode(step, idx_ready):
                step(nc.vector.tensor_scalar(g_int[:, :], round_k[:, :], -1.0, None, ALU.add))
                step(nc.vector.tensor_scalar(g_idx[:, :], g_int[:, :], LAST, None, ALU.bitwise_and))
                step(nc.vector.tensor_scalar(g_int[:, :], g_int[:, :], 12, None, ALU.arith_shift_right))
                step(nc.vector.tensor_copy(g_hi[:, :], g_int[:, :]))
                dve.sem_inc(idx_ready, 1)

            dve.sem_inc(idx1_ready, 1)
            dve.sem_inc(max1_done, 2)
            lanes = lane[:, 0:HIS]
            M1 = 4 + 2 * 5
            with dve.Fori(0, total) as r:
                step, n = chained(m1_chain, r * M1)
                dve.wait_ge(key1_in, r * 16 + 16)
                decode(step, idx1_ready)
                for half in range(2):
                    hs = g_hi[:, half * HALFR:(half + 1) * HALFR]
                    step(nc.vector.tensor_tensor(oh_t[:, :, :], hs.unsqueeze(1).to_broadcast([P, HIS, HALFR]),
                                                 lanes.unsqueeze(2).to_broadcast([P, HIS, HALFR]), ALU.not_equal))
                    step(nc.vector.tensor_scalar(oh_t[:, :, :], oh_t[:, :, :], -BIG, None, ALU.mult))
                    dve.wait_ge((rows1_in, rows1_b)[half], (r + 1) * 16 * HALFR)
                    grid = sel_p[:, 0:HIS * HEADS * HALFR].rearrange("p (t h k) -> p t h k", t=HIS, h=HEADS)
                    step(nc.vector.tensor_tensor(
                        grid, oh_t[:, :, :].unsqueeze(2).to_broadcast([P, HIS, HEADS, HALFR]),
                        rows_g[:, half, :, HE:ROW].rearrange("p k h -> p h k").unsqueeze(1).to_broadcast([P, HIS, HEADS, HALFR]), ALU.add))
                    dve.sem_inc(max1_done, 1)
                    step(nc.vector.tensor_reduce(cand[:, :, :], grid, AX_X, ALU.max))
                    step(nc.vector.tensor_tensor(s_max[:, :, :], s_max[:, :, :], cand[:, :, :], ALU.max))
                assert n[0] == M1
            run(nc.vector.tensor_tensor(cand[:, :, :], s_max[:, :, :], a_dst[:, :, :], ALU.add))
            run(nc.vector.scalar_tensor_tensor(e_max[:, :, :], cand[:, :, :], 0.2, cand[:, :, :], ALU.mult, ALU.max))
            run(nc.vector.tensor_copy(per_hi[:, 0:HEADS, :], a_dst[:, :, :].rearrange("p t h -> p h t")))
            run(nc.vector.tensor_copy(per_hi[:, HEADS:8, :], e_max[:, :, :].rearrange("p t h -> p h t")))
            dve.sem_inc(idx2_ready, 1)
            dve.sem_inc(used2, 2)
            M2 = 4 + 2 * 8
            with dve.Fori(0, total) as r:
                step, n = chained(m2_chain, r * M2)
                dve.wait_ge(key2_in, r * 16 + 16)
                decode(step, idx2_ready)
                for half in range(2):
                    v = 2 * r + half
                    hs = g_hi[:, half * HALFR:(half + 1) * HALFR]
                    step(nc.vector.tensor_tensor(oh[:, :, :], hs.unsqueeze(2).to_broadcast([P, HALFR, HIS]),
                                                 lanes.unsqueeze(1).to_broadcast([P, HALFR, HIS]), ALU.is_equal))
                    grid = sel_p[:, :].rearrange("p (k f t) -> p k f t", k=HALFR, f=8)
                    step(nc.vector.tensor_tensor(grid, oh[:, :, :].unsqueeze(2).to_broadcast([P, HALFR, 8, HIS]),
                                                 per_hi[:, :, :].unsqueeze(1).to_broadcast([P, HALFR, 8, HIS]), ALU.mult))
                    step(nc.vector.tensor_reduce(got[:, :, :], grid, AX_X, ALU.add))
                    dve.wait_ge((rows2_in, rows2_b)[half], (r + 1) * 16 * HALFR)
                    step(nc.vector.tensor_tensor(z[:, :, :], rows_g[:, half, :, HE:ROW], got[:, :, 0:HEADS], ALU.add))
                    step(nc.vector.scalar_tensor_tensor(z[:, :, :], z[:, :, :], 0.2, z[:, :, :], ALU.mult, ALU.max))
                    step(nc.vector.tensor_tensor(z[:, :, :], z[:, :, :], got[:, :, HEADS:8], ALU.subtract))
                    step(nc.vector.tensor_scalar(z[:, :, :], z[:, :, :], 0.0, None, ALU.min))
                    dve.sem_inc(got2, 1)
                    dve.wait_ge(exp2, v + 1)
                    step(nc.vector.tensor_tensor(
                        vals[:, :, HEADS:ROW].rearrange("p k (h e) -> p k h e", h=HEADS),
                        rows_g[:, half, :, 0:HE].rearrange("p k (h e) -> p k h e", h=HEADS),
                        vals[:, :, 0:HEADS].unsqueeze(3).to_broadcast([P, HALFR, HEADS, EXPERTS]), ALU.mult))
                    dve.sem_inc(used2, 1)
                    for g in range(2):
                        dve.wait_ge(summed2, 2 * v + g + 1)
                        ks = slice(GROUP * g, GROUP * (g + 1))
                        nc.vector.tensor_tensor(spread_v[g].rearrange("p k (t f) -> p k t f", f=ROW),
                                                oh[:, ks, :].unsqueeze(3).to_broadcast([P, GROUP, HIS, ROW]),
                                                vals[:, ks, :].unsqueeze(2).to_broadcast([P, GROUP, HIS, ROW]), ALU.mult).then_inc(spread2, 1)
                    dve.wait_ge(spread2, 2 * v + 2)
                assert n[0] == M2
            run(nc.vector.tensor_tensor(cand[:, :, :], a_src, a_dst[:, :, :], ALU.add))
            run(nc.vector.scalar_tensor_tensor(cand[:, :, :], cand[:, :, :], 0.2, cand[:, :, :], ALU.mult, ALU.max))
            run(nc.vector.tensor_tensor(cand[:, :, :], cand[:, :, :], e_max[:, :, :], ALU.subtract))
            dve.sem_inc(f_ask, 1)
            run(nc.vector.tensor_tensor(s_max[:, :, :], a_dst[:, :, :],
                                        last_row[:, HE:ROW].unsqueeze(1).to_broadcast([P, HIS, HEADS]), ALU.add))
            run(nc.vector.scalar_tensor_tensor(s_max[:, :, :], s_max[:, :, :], 0.2, s_max[:, :, :], ALU.mult, ALU.max))
            run(nc.vector.tensor_tensor(s_max[:, :, :], s_max[:, :, :], e_max[:, :, :], ALU.subtract))
            run(nc.vector.tensor_scalar(s_max[:, :, :], s_max[:, :, :], 0.0, None, ALU.min))
            dve.sem_inc(f_ask, 1)
            dve.wait_ge(f_exp, 2)
            run(nc.vector.tensor_tensor(s_max[:, :, :], s_max[:, :, :], to_last[:, :].unsqueeze(2).to_broadcast([P, HIS, HEADS]), ALU.mult))
            acc = spread_v[0][:, 0, :].rearrange("p (t f) -> p t f", f=ROW)
            dve.wait_ge(summed2, total * 4 + 2)
            for b in range(2):
                run(nc.vector.tensor_copy(acc[:, b * (HIS // 2):(b + 1) * (HIS // 2), :],
                                          ps[b][:, 0:HIS // 2 * ROW].rearrange("p (t f) -> p t f", f=ROW)))
            den, agg = acc[:, :, 0:HEADS], acc[:, :, HEADS:ROW]
            by_head = lambda t: t.rearrange("p t (h e) -> p t h e", h=HEADS)
            for w, f in ((cand, feats), (s_max, last_row[:, 0:HE].unsqueeze(1).to_broadcast([P, HIS, HE]))):
                run(nc.vector.tensor_tensor(den, den, w[:, :, :], ALU.add))
                run(nc.vector.tensor_tensor(by_head(prod[:, :, :]), by_head(f), w[:, :, :].unsqueeze(3).to_broadcast([P, HIS, HEADS, EXPERTS]), ALU.mult))
                run(nc.vector.tensor_tensor(agg, agg, prod[:, :, :], ALU.add))
            run(nc.vector.tensor_scalar(cand[:, :, :], den, 1e-16, None, ALU.add))
            run(nc.vector.reciprocal(cand[:, :, :], cand[:, :, :]))
            run(nc.vector.tensor_tensor(by_head(prod[:, :, :]), by_head(agg), cand[:, :, :].unsqueeze(3).to_broadcast([P, HIS, HEADS, EXPERTS]), ALU.mult))
            row = lambda k: gat_v[:, k:k + 1, :].to_broadcast([P, HIS, HE])
            wide = lambda k, w=HE: stat[:, k, :].unsqueeze(2).to_broadcast([P, HIS, w])
            run(nc.vector.tensor_tensor(prod[:, :, :], prod[:, :, :], row(0), ALU.add))
            run(nc.vector.tensor_reduce(stat[:, 0, :], prod[:, :, :], AX_X, ALU.add))
            run(nc.vector.tensor_scalar(stat[:, 0, :], stat[:, 0, :], 1.0 / HE, None, ALU.mult))
            run(nc.vector.tensor_tensor(prod[:, :, :], prod[:, :, :], wide(0), ALU.subtract))
            run(nc.vector.tensor_tensor(agg, prod[:, :, :], prod[:, :, :], ALU.mult))
            run(nc.vector.tensor_reduce(stat[:, 1, :], agg, AX_X, ALU.add))
            run(nc.vector.tensor_scalar(stat[:, 1, :], stat[:, 1, :], 1.0 / HE, None, ALU.mult))
            dve.sem_inc(f_ask, 1)
            dve.wait_ge(f_exp, 3)
            run(nc.vector.reciprocal(stat[:, 1, :], stat[:, 1, :]))
            run(nc.vector.tensor_tensor(prod[:, :, :], prod[:, :, :], wide(1), ALU.mult))
            run(nc.vector.tensor_tensor(prod[:, :, :], prod[:, :, :], row(1), ALU.mult))
            run(nc.vector.tensor_tensor(prod[:, :, :], prod[:, :, :], row(2), ALU.add))
            run(nc.vector.tensor_reduce(score[:, :, :], prod[:, :, :].rearrange("p t (h e) -> p t e h", h=HEADS), AX_X, ALU.add))
            run(nc.vector.tensor_scalar(score[:, :, :], score[:, :, :], 1.0 / HEADS, None, ALU.mult))
            square = lambda k: pair[:, k, :, :].rearrange("p t (i j) -> p t i j", i=EXPERTS)
            other = score[:, :, :].unsqueeze(2).to_broadcast([P, HIS, EXPERTS, EXPERTS])
            mine = score[:, :, :].unsqueeze(3).to_broadcast([P, HIS, EXPERTS, EXPERTS])
            run(nc.vector.tensor_tensor(square(0), other, mine, ALU.is_gt))
            run(nc.vector.tensor_tensor(square(1), other, mine, ALU.is_equal))
            run(nc.vector.tensor_tensor(pair[:, 1, :, :], pair[:, 1, :, :],
                                        below[:, :, :].rearrange("p i j -> p (i j)").unsqueeze(1).to_broadcast([P, HIS, EXPERTS * EXPERTS]), ALU.mult))
            run(nc.vector.tensor_tensor(pair[:, 0, :, :], pair[:, 0, :, :], pair[:, 1, :, :], ALU.add))
            run(nc.vector.tensor_reduce(cand[:, :, :], square(0), AX_X, ALU.add))
            run(nc.vector.tensor_reduce(stat[:, 2, :], score[:, :, :], AX_X, ALU.max))
            run(nc.vector.tensor_tensor(gate[:, :, :], score[:, :, :], wide(2, EXPERTS), ALU.subtract))
            dve.sem_inc(f_ask, 1)
            dve.wait_ge(f_exp, 4)
            run(nc.vector.scalar_tensor_tensor(gate[:, :, :], cand[:, :, :], 1.5, gate[:, :, :], ALU.is_lt, ALU.mult))
            run(nc.vector.tensor_reduce(stat[:, 3, :], gate[:, :, :], AX_X, ALU.add))
            run(nc.vector.reciprocal(stat[:, 3, :], stat[:, 3, :]))
            run(nc.vector.tensor_tensor(gate[:, :, :], gate[:, :, :], wide(3, EXPERTS), ALU.mult))
            dve.sem_inc(gates_known, 1)
            dve.wait_ge(my_done, 2 + CHUNKS * EXPERTS)
            dve.sem_inc(gated, 2)
            with dve.Fori(0, CHUNKS) as i:
                for e in range(EXPERTS):
                    v = EXPERTS * i + e
                    dve.wait_ge(gates_ready, v + 1)
                    nc.vector.tensor_tensor(y_exp[e][:, i, :], y_exp[e][:, i, :], ps[6 + e % 2][:, :], ALU.mult).then_inc(gated, 1)
                dve.wait_ge(gated, EXPERTS * (i + 1) + 2)
                for e in (0, 2):
                    nc.vector.tensor_tensor(y_exp[e][:, i, :], y_exp[e][:, i, :], y_exp[e + 1][:, i, :], ALU.add).then_inc(gated_b, 1)
                dve.wait_ge(gated_b, 3 * i + 2)
                nc.vector.tensor_tensor(y_exp[0][:, i, :], y_exp[0][:, i, :], y_exp[2][:, i, :], ALU.add).then_inc(gated_b, 1)
                dve.wait_ge(gated_b, 3 * i + 3)
                nc.vector.tensor_tensor(X[:, i, :], X[:, i, :], y_exp[0][:, i, :], ALU.add).then_inc(res4, 1)

        @block.tensor
        def _(pe):
            def mm(o, l, r, start, stop, **kw):
                return nc.tensor.matmul(o, l, r, start=start, stop=stop, **kw)

            def norm(ln, res, credit):
                pe.sem_inc(ln.var_ready, 2)
                with pe.Fori(0, IMGS) as n:
                    for h in range(2):
                        i = 2 * n + h
                        if res is not None:
                            pe.wait_ge(res, i + credit + 1)
                        pe.wait_ge(ln.centred, i + 1)
                        mm(ps[h][:, :], mean_w[:, :], X[:, i, :], True, True).then_inc(ln.mean_ready, 1)
                    for h in range(2):
                        i = 2 * n + h
                        pe.wait_ge(ln.squared, i + 1)
                        for j in range(CHUNK // P):
                            last = mm(ps[2][:, bass.ds(i * (CHUNK // P) + j, 1)], sq[:, h, j * P:(j + 1) * P], mean_w[:, 0:1],
                                      True, True)
                        last.then_inc(ln.var_ready, 1)
                pe.wait_ge(ln.inv_ready, 1)
                for i in range(CHUNKS):
                    pe.wait_ge(ln.normed, i + 1)
                    for j in range(CHUNK // P):
                        t = i * (CHUNK // P) + j
                        last = mm(ps[6 + i % 2][:, j * P:(j + 1) * P], inv[:, t:t + 1].to_broadcast([P, P]), ident[:, :], True, True)
                    last.then_inc(ln.spread, 1)

            pe.wait_ge(x_in, 16 * IMGS)
            pe.wait_ge(made, 10)
            norm(ln0, None, 0)
            pe.wait_ge(wa_in, WA)
            pe.wait_ge(padded, CHUNKS)
            pe.wait_ge(made, 21)

            def conv(w, m, done):
                with pe.Fori(0, IMGS) as n:
                    for h in range(2):
                        for k in range(TAPS):
                            dy, dx = divmod(k, 3)
                            last = mm(bank_of(2 * n + h, slice(0, m)), w[:, k, :],
                                      XP[:, n, HROWS * h + dy:HROWS * h + dy + HROWS, dx:dx + SIDE], k == 0, k == TAPS - 1)
                        last.then_inc(done, 1)

            conv(w_off, 64, off_ready)

            def broadcast(n, k, h):
                u = (n * TAPS + k) * 2 + h
                pe.wait_ge(abs_done, 2 * u + 2)
                mm(ps[h][:, :], sel[:, 2 * k, :], OFS[:, 2 * n + h, :], True, True)
                pe.wait_ge(ax_done, u + 1)
                mm(ps[2][:, :], sel[:, 2 * k + 1, :], OFS[:, 2 * n + h, :], True, True)
                pe.wait_ge(txm_done, u + 2)
                mm(ps[3][:, :], sel[:, k, :], MSK[:, 2 * n + h, :], True, True).then_inc(bc_ready, 1)

            def sample(n, k, h):
                u = (n * TAPS + k) * 2 + h
                for g in range(2):
                    v = 2 * u + g
                    pe.wait_ge(ten_done, v + 5)
                    for j in range(GROUP):
                        last = mm(ps[4 + h][:, :], YT[:, GROUP * g + j, k * P:(k + 1) * P], TEN[:, 2 * h + g, j, :], False, False,
                                  skip_group_check=True)
                    last.then_inc(main_done, 1)

            pe.wait_ge(wb_in, WB_)
            pe.wait_ge(off_done, 2 + CHUNKS)
            pe.wait_ge(msk_done, 1 + CHUNKS)
            pe.wait_ge(left_known, 1)
            lefts = pe.value_load(num[0:1, N_LEFT:N_LEFT + 1], min_val=1, max_val=(ECOLS - KEPT1) // 8)
            mm(ps[7][:, 0:HIS], zero_b[:, 0:P], zero_b[:, 0:HIS], True, False, skip_group_check=True)
            pe.sem_inc(left_added, 1)
            with pe.Fori(0, lefts) as r:
                pe.wait_ge(left_coded, r * 7 + 7)
                for c in range(8):
                    last = mm(ps[7][:, 0:HIS], oh_lo[:, 0, c, :], oh_hi[:, 0, c, :], False, False, skip_group_check=True)
                last.then_inc(left_added, 1)
            pe.wait_ge(batches_known, 1)
            pe.sem_inc(piece_added, 2)

            def add_piece(n, k, h):
                pe.wait_ge(piece_made, PIECES * n + 2 * k + h + 1)
                for c in range(PIECE):
                    last = mm(ps[7][:, 0:HIS], oh_lo[:, h, c, :], oh_hi[:, h, c, :], k + h + c == 0,
                              2 * k + h == PIECES - 1 and c == PIECE - 1)
                last.then_inc(piece_added, 1)

            is_far = pe.value_load(num[0:1, N_FAR:N_FAR + 1], min_val=0, max_val=1)
            with pe.If(is_far > 0):
                pe.sem_inc(main_done, 4)
                with pe.Fori(0, IMGS) as n:
                    broadcast(n, 0, 0)
                    pe.wait_ge(res1, 2 * n + 2)
                    for h in range(2):
                        mm(ps[4 + h][:, :], zero_b[:, 0:P], zero_b[:, :], True, False, skip_group_check=True)
                    pe.wait_ge(own_ready, n + 1)
                    pe.wait_ge(shares_added, n + 1)
                    for q in range(3 * SRC_T):
                        t, g = divmod(q, 3)
                        w = min(CHUNK, TAPS * P - g * CHUNK)
                        pe.wait_ge(yt_done, 3 * SRC_T * n + q + 1)
                        mm(ps[6 + q % 2][:, 0:w], own_img[:, t * P:(t + 1) * P], w_dcn[:, g * CHUNK:g * CHUNK + w],
                           True, True).then_inc(yt_ready, 1)
                    pe.wait_ge(yt_done, 3 * SRC_T * (n + 1) + 2)
                    for k in range(TAPS):
                        broadcast(n, k, 1)
                        sample(n, k, 0)
                        if 2 * k < PIECES:
                            add_piece(n, k, 0)
                        if k + 1 < TAPS:
                            broadcast(n, k + 1, 0)
                        sample(n, k, 1)
                        if 2 * k < PIECES:
                            add_piece(n, k, 1)
                pe.nop()

            def near_broadcast(n, k, h):
                u = (n * TAPS + k) * 2 + h
                pe.wait_ge(abs_done, u + 1)
                mm(ps[h][:, :], sel[:, 2 * k, :], OFS[:, 2 * n + h, :], True, True)
                pe.wait_ge(ax_done, u + 1)
                mm(ps[2][:, :], sel[:, 2 * k + 1, :], OFS[:, 2 * n + h, :], True, True)
                pe.wait_ge(txm_done, u + 2)
                mm(ps[3][:, :], sel[:, k, :], MSK[:, 2 * n + h, :], True, True).then_inc(bc_ready, 1)

            def make_tap(n, k, h):
                pe.wait_ge(yt_done, n * (2 * TAPS) + 2 * k + h + 1)
                for j in range(4):
                    t = 4 * h + j
                    last = mm(ps[6][:, j * P:(j + 1) * P], own_img[:, t * P:(t + 1) * P], w_dcn[:, k * P:(k + 1) * P], True, True)
                last.then_inc(yt_ready, 1)

            def near_sample(n, k, h):
                u = (n * TAPS + k) * 2 + h
                pe.wait_ge(yt_done, n * (2 * TAPS) + 2 * k + 3)
                pe.wait_ge(ten_done, u + 3)
                pe.wait_ge(ten_pool, u + 3)
                for t, j, c, slot in near_tiles(h):
                    last = mm(ps[4 + h][:, j * P:(j + c) * P], YTN[:, k % RING, t, :],
                              near_w[(2 * k + h) % RING][:, slot:slot + 2 * c - 1:2, :], False, False, skip_group_check=True)
                last.then_inc(main_done, 1)

            with pe.If(is_far < 1):
                pe.sem_inc(main_done, RING)
                with pe.Fori(0, IMGS) as n:
                    near_broadcast(n, 0, 0)
                    pe.wait_ge(own_ready, n + 1)
                    for h in range(2):
                        make_tap(n, 0, h)
                    pe.wait_ge(res1, 2 * n + 2)
                    for h in range(2):
                        mm(ps[4 + h][:, :], zero_b[:, 0:P], zero_b[:, :], True, False, skip_group_check=True)
                    pe.wait_ge(shares_added, n + 1)
                    for k in range(TAPS):
                        for h in range(2):
                            if h == 0:
                                near_broadcast(n, k, 1)
                            elif k + 1 < TAPS:
                                near_broadcast(n, k + 1, 0)
                            if k + 1 < TAPS:
                                make_tap(n, k + 1, h)
                            near_sample(n, k, h)
                            if 2 * k < PIECES:
                                add_piece(n, k, h)
                pe.nop()
            norm(ln1, res1, 2)
            pe.wait_ge(wrb_done, 1)
            with pe.Fori(0, IMGS) as n:
                for h in range(2):
                    i = 2 * n + h
                    pe.wait_ge(ln1.normed, i + 3)
                    pe.wait_ge(rw_done, i + 1)
                    mm(ps[h][:, :], wr_b[:, :], T[:, i, :], True, True).then_inc(rw_ready, 1)
            with pe.Fori(0, IMGS) as n:
                for h in range(2):
                    i = 2 * n + h
                    for c in range(HID):
                        pe.wait_ge(gelu_done, HID * i + c + 1)
                        mm(ps[4 + c % 2][:, :], f_w1[:, c * P:(c + 1) * P], T[:, i, :], True, True).then_inc(h_ready, 1)
                    pe.wait_ge(gelu_done, HID * (i + 1) + 2)
                    pe.wait_ge(yf_done, i + 1)
                    for c in range(HID):
                        last = mm(ps[6 + h][:, :], f_w2[:, c, :], hid[h][:, c, :], c == 0, c == HID - 1)
                    last.then_inc(y_ready, 1)
                pe.wait_ge(cmp_done, SRC_T * (n + 1))
                pe.wait_ge(kept_done, 2 * n + 2)
                for h in range(2):
                    for t in range(SRC_T):
                        last = mm(ps[2 + h][:, :], ones_b[:, :], cmp_b[:, t, h * CHUNK:(h + 1) * CHUNK],
                                  t == 0, t == SRC_T - 1)
                last.then_inc(rank_ready, 1)
            norm(ln2, res2, 0)
            batches = pe.value_load(num[0:1, N_BATCH:N_BATCH + 1], min_val=1, max_val=MAX_BATCHES)
            pe.sem_inc(turned, 1)
            with pe.Fori(0, batches) as b:
                pe.wait_ge(batch_in, b * 16 + 16)
                for q in range(BATCH // 4):
                    pe.wait_ge(turned_out, b * (BATCH // 4) + q + 1)
                    for j in range(4):
                        last = nc.tensor.transpose(ps[4 + q % 2][:, j * P:(j + 1) * P],
                                                   batch_k[:, 4 * q + j:4 * q + j + 1].to_broadcast([P, P]), ident[:, :])
                    last.then_inc(turned, 1)
            pe.wait_ge(turned_out, batches * (BATCH // 4) + 2)
            pe.sem_inc(pe_passed, 1)
            pe.wait_ge(padded, 2 * CHUNKS)
            conv(w_conv, P, cv_ready)
            pe.wait_ge(rounds_known, 1)
            pe.wait_ge(res3, 2 + 3)
            norm(ln3, res3, 2)
            pe.wait_ge(wc_in, WC)
            pe.wait_ge(ln3.normed, 2 + CHUNKS)
            for t in range(TILES):
                i, j = divmod(t, CHUNK // P)
                last = mm(ps[0][:, t * HE:(t + 1) * HE], T[:, i, j * P:(j + 1) * P], w_gat[:, :], True, True)
            last.then_inc(feat_ready, 1)
            def hidden(i, e):
                v = EXPERTS * i + e
                for c in range(2):
                    pe.wait_ge(mid_done, 2 * v + c + 1)
                    mm(ps[2 + c][:, :], m_w1[:, e, c * P:(c + 1) * P], T[:, i, :], True, True).then_inc(mid_ready, 1)

            def expert_out(i, e):
                v = EXPERTS * i + e
                pe.wait_ge(mid_done, 2 * v + 4)
                pe.wait_ge(my_done, v + 1)
                for c in range(2):
                    last = mm(ps[4 + e % 2][:, :], m_w2[:, e, c, :], mid[:, e % 2, c, :], c == 0, c == 1)
                last.then_inc(my_ready, 1)

            pe.wait_ge(wd_in, 32)
            pe.sem_inc(my_ready, 2)
            with pe.Fori(0, CHUNKS) as i:
                hidden(i, 0)
                for e in range(1, EXPERTS):
                    hidden(i, e)
                    expert_out(i, e - 1)
                expert_out(i, EXPERTS - 1)
            pe.wait_ge(t_chain, 1)
            wide_hi = HIS // 2 * ROW
            for b in range(2):
                mm(ps[b][:, 0:wide_hi], zero_b[:, 0:P], zero_b[:, 0:wide_hi], True, False, skip_group_check=True)
            pe.sem_inc(summed2, 2)
            total = pe.value_load(num[0:1, N_ALL:N_ALL + 1], min_val=1, max_val=MAX_ROUNDS)
            with pe.Fori(0, total) as r:
                for half in range(2):
                    for g in range(2):
                        pe.wait_ge(spread2, 4 * r + 2 * half + g + 1)
                        for k in range(GROUP):
                            for b in range(2):
                                last = mm(ps[b][:, 0:wide_hi], ident[:, :], spread_v[g][:, k, b * wide_hi:(b + 1) * wide_hi],
                                          False, False, skip_group_check=True)
                        last.then_inc(summed2, 1)
            pe.wait_ge(gates_known, 1)
            for i in range(CHUNKS):
                for e in range(EXPERTS):
                    pe.wait_ge(gated, EXPERTS * i + e + 1)
                    for j in range(CHUNK // P):
                        t = i * (CHUNK // P) + j
                        last = nc.tensor.transpose(ps[6 + e % 2][:, j * P:(j + 1) * P],
                                                   gate[:, t, e:e + 1].to_broadcast([P, P]), ident[:, :])
                    last.then_inc(gates_ready, 1)

_WEIGHTS = {
    "w_off": ("L0_conv_offset_w", (P, TAPS, 3 * TAPS)), "b_off": ("L0_conv_offset_b", (3 * TAPS,)),
    "w_dcn": ("L0_conv_dcn_w", (P, TAPS * P)), "wr": ("L0_ffn_wr", (P, 1)), "br": ("L0_ffn_br", (1,)),
    "f_w1": ("L0_ffn_w1", (P, HID * P)), "f_b1": ("L0_ffn_b1", (P, HID)),
    "edges": ("L1_ffn_edge_index", (2, EDGES)), "w_gat": ("L1_ffn_W_gat", (P, HE)),
    "att_src": ("L1_ffn_att_src", (HE,)), "att_dst": ("L1_ffn_att_dst", (HE,)), "b_gat": ("L1_ffn_b_gat", (HE,)),
    "ln_gamma": ("L1_ffn_ln_gamma", (HE,)), "ln_beta": ("L1_ffn_ln_beta", (HE,)),
    "m_w1": ("L1_ffn_W1", (EXPERTS, P, 2 * P)), "m_b1": ("L1_ffn_b1", (P, EXPERTS, 2)),
    "m_w2": ("L1_ffn_W2", (EXPERTS, 2 * P, P)), "m_b2": ("L1_ffn_b2", (P, EXPERTS)),
    "f_w2": ("L0_ffn_w2", (HID * P, P)), "f_b2": ("L0_ffn_b2", (P,)), "w_conv": ("L1_conv_weight", (P, TAPS, P)),
}


def kernel(**inputs):
    import concourse.bacc as _bacc
    from concourse.bass_utils import run_bass_kernel_spmd as _run

    nc = _bacc.Bacc("TRN2", target_bir_lowering=False, num_devices=1)
    y, x = np.divmod(np.arange(POS), SIDE)
    ky, kx = np.divmod(np.arange(TAPS), 3)
    base = np.stack([y[None] - 1 + ky[:, None], x[None] - 1 + kx[:, None]], 1).reshape(2 * TAPS, POS)
    rows = np.arange(P)[:, None] // SIDE + np.arange(SRC_T)[None] * (P // SIDE)
    arrays = {"base": base.astype(np.float32), "neg_y": -rows.astype(np.float32),
              "neg_x": -(np.arange(P)[:, None] % SIDE).astype(np.float32), "x": np.asarray(inputs["x"])}
    for name, (source, shape) in _WEIGHTS.items():
        w = np.asarray(inputs[source])
        if w.ndim == 4:
            w = w.reshape(w.shape[0], P, TAPS).transpose(1, 2, 0)
        elif name == "f_b1":
            w = w.reshape(HID, P).T
        elif name == "m_b1":
            w = w.reshape(EXPERTS, 2, P).transpose(2, 0, 1)
        elif name == "m_b2":
            w = w.T
        arrays[name] = np.ascontiguousarray(w).reshape(shape)
    a = {k: nc.dram_tensor(f"in_{k}", v.shape, mybir.dt.from_np(v.dtype), kind="ExternalInput").ap()
         for k, v in arrays.items()}
    out = nc.dram_tensor("out_x", (IMGS, P, SIDE, SIDE), F32, kind="ExternalOutput").ap()
    metaformer_kernel(nc, a, out)
    r = _run(nc, [{f"in_{k}": v for k, v in arrays.items()}], core_ids=[0])
    return r.results[0]["out_x"]
```

```python
from collections import namedtuple
from contextlib import ExitStack

import numpy as np

import concourse.bass as bass
from concourse import mybir

F32 = mybir.dt.float32
BF16 = mybir.dt.bfloat16
I32 = mybir.dt.int32
ALU = mybir.AluOpType
ACT = mybir.ActivationFunctionType
AX_X = mybir.AxisListType.X

P = 128
IMGS = 4
SIDE = 32
POS = SIDE * SIDE
NODES = IMGS * POS
CHUNK = 512
CHUNKS = NODES // CHUNK
TILES = NODES // P
TAPS = 9
HROWS = SIDE // 2
SRC_T = POS // P
PAD = SIDE + 2
GROUP = 4
NEAR = 3
FAR = 2.9 * 2.9
RING = 3
KEPT = POS // 2 - 1
HID = 4


EDGES = 524288
ECOLS = EDGES // P
FIRST = 32
KEPT1 = ECOLS // FIRST * 8
FRONT = 5
FRONT_N = ECOLS // FIRST * FRONT
BATCH = 96
BCHUNKS = 64
KEPT2 = BCHUNKS * 8
ROUND = 16
HALFR = ROUND // 2
KEPT_ROUNDS = 7
MAX_BATCHES = -(-ECOLS // BATCH)
MAX_ROUNDS = ECOLS * P // ROUND
LAST = NODES - 1
NONE = -8192.0
KEY_PART = 1024
KEY_STEPS = 10
SURE = 2.0 ** 27
KEY_BIAS = (-1.0, -LAST / 2, (LAST / 2 + 0.25) * SURE, (LAST - 0.5) * SURE)
BIG = 1e30
HEADS = 4
EXPERTS = 4
HE = HEADS * EXPERTS
ROW = HE + HEADS
HIS = TILES
PIECE = 16
PIECES = KEPT1 // PIECE // IMGS

LayerNorm = namedtuple("LayerNorm", "eps mean_ready centred squared var_ready std_ready inv_ready spread normed")


def metaformer_kernel(nc, a, out):
    with ExitStack() as ctx:
        def sb(name, shape, dt=F32):
            return ctx.enter_context(nc.sbuf_tensor(name, shape, dt))

        def sem(name):
            return ctx.enter_context(nc.semaphore(name))

        banks = ctx.enter_context(nc.psum_tensor("banks", [P, 8, CHUNK], F32))
        ps = [banks[:, i, :] for i in range(8)]
        bank_of = lambda i, p=slice(0, P): banks[p, bass.ds(i, 1), :].rearrange("p o c -> p (o c)")

        X = sb("X", [P, CHUNKS, CHUNK])
        T = sb("T", [P, CHUNKS, CHUNK])
        wide_buf = sb("wide_buf", [P, SRC_T * TAPS * P + 4 * GROUP * CHUNK])
        scratch = wide_buf[:, 0:SRC_T * TAPS * P]
        RW = scratch[:, 0:NODES].rearrange("p (i c) -> p i c", c=CHUNK)
        YF = scratch[:, NODES:2 * NODES].rearrange("p (i c) -> p i c", c=CHUNK)
        XP = sb("XP", [P, IMGS, PAD, PAD])
        sq = sb("sq", [P, 2, CHUNK])
        dev = sb("dev", [P, TILES])
        inv = sb("inv", [P, TILES])
        ident = sb("ident", [P, P])
        mean_w = sb("mean_w", [P, P])
        eps = sb("eps", [P, 2])
        k_bias = sb("k_bias", [P, 4])
        ones_b = sb("ones_b", [P, P], BF16)
        later = sb("later", [P, P])

        w_off = sb("w_off", [P, TAPS, 64])
        b_off = sb("b_off", [64, 1])
        taps_w = sb("taps_w", [P, 2 * TAPS * P])
        w_dcn = taps_w[:, 0:TAPS * P]
        shared = sb("shared", [P, 4096])
        split = lambda t: t.bitcast(BF16).rearrange("p (i c) -> p i c", c=CHUNK)
        OFS = split(shared[0:96, 0:2048])
        MSK = split(shared[0:96, 2048:4096])
        sel = sb("sel", [96, 2 * TAPS, P], BF16)
        zero_b = sb("zero_b", [P, CHUNK], BF16)
        neg_x = sb("neg_x", [P, 1])
        neg_y = sb("neg_y", [P, SRC_T])
        YT = scratch[:, :].rearrange("p (t k) -> p t k", t=SRC_T)
        TEN = wide_buf[:, SRC_T * TAPS * P:].rearrange("p (a b c) -> p a b c", a=4, b=GROUP)
        small = sb("small", [P, 3072])
        txm = small[:, 0:1024].rearrange("p (h c) -> p h c", h=2)
        absx = small[:, 1024:2048].rearrange("p (h c) -> p h c", h=2)
        own_img = small[:, 2048:3072]
        near_w = [TEN[:, b, :, :].rearrange("p g c -> p (g c)")[:, 0:4 * NEAR * P].rearrange("p (s c) -> p s c", c=P)
                  for b in range(RING)]
        YTN = scratch[:, 0:RING * POS].rearrange("p (r t k) -> p r t k", r=RING, t=SRC_T)
        far = sb("far", [2 * TAPS, 2])

        def near_tiles(h):
            for t in range(SRC_T):
                js = [j for j in range(4) if abs(4 * h + j - t) <= 1]
                if js:
                    yield t, js[0], len(js), NEAR * js[0] + t - (4 * h + js[0]) + 1

        def near_parts(h):
            for j in range(4):
                ts = [t for t in range(SRC_T) if abs(4 * h + j - t) <= 1]
                yield j, NEAR * j + ts[0] - (4 * h + j) + 1, len(ts)

        wr = sb("wr", [P, 1])
        wr_b = sb("wr_b", [P, P])
        br_b = sb("br_b", [P, 1])
        f_w1 = sb("f_w1", [P, HID * P])
        f_b1 = sb("f_b1", [P, HID])
        f_w2 = sb("f_w2", [P, HID, P])
        f_b2 = sb("f_b2", [P, 1])
        w_col = sb("w_col", [P, IMGS, SRC_T])
        tie = sb("tie", [P, P])
        cmp_b = TEN[:, 0:2, :, :].rearrange("p a b c -> p (a b c)").bitcast(BF16).rearrange("p (t c) -> p t c", t=SRC_T)
        hid = [TEN[:, 2 + h, :, :] for h in range(2)]

        w_conv = taps_w[:, TAPS * P:].rearrange("p (t c) -> p t c", t=TAPS)

        src_i = TEN[:, 0:2, :, :].rearrange("p a b c -> p (a b c)").bitcast(I32)
        dst_i = TEN[:, 2:4, :, :].rearrange("p a b c -> p (a b c)").bitcast(I32)
        flags = TEN[:, 0:2, :, :].rearrange("p a b c -> p (a b c)")
        code_i = TEN[:, 2:4, :, :].rearrange("p a b c -> p (a b c)").bitcast(I32)
        routed = wide_buf[:, 0:BATCH * P]
        keys = scratch[:, 0:ECOLS]
        listed = scratch[:, ECOLS:2 * ECOLS]
        generic = sb("generic", [P, MAX_BATCHES * BATCH])
        base = scratch[0:2 * TAPS, 2 * ECOLS:2 * ECOLS + POS]
        off_row, off_rem = (generic[0:2 * TAPS, k * CHUNK:(k + 1) * CHUNK] for k in range(2))
        off_mid = generic[0:2 * TAPS, 3 * CHUNK:3 * CHUNK + CHUNK // 2].bitcast(BF16)
        msk_row, msk_rem = (generic[0:TAPS, k * CHUNK:(k + 1) * CHUNK] for k in (4, 5))
        msk_mid = generic[0:TAPS, 6 * CHUNK:6 * CHUNK + CHUNK // 2].bitcast(BF16)
        k_src, k_last, k_gen, k_node = (generic[:, k * KEY_PART:(k + 1) * KEY_PART] for k in range(4))
        k_lo, k_hi = (small[:, k * KEY_PART:(k + 1) * KEY_PART].bitcast(I32) for k in range(2))
        k_key = small[:, 2 * KEY_PART:3 * KEY_PART]
        sorted_k = wide_buf[:, BATCH * P + ECOLS:BATCH * P + ECOLS + KEPT2]
        batch_k = sb("batch_k", [P, BATCH])
        kept2 = sb("kept2", [P, KEPT2])
        top8 = sb("top8", [P, 8])
        round_k = sb("round_k", [P, ROUND])
        neg_lo = sb("neg_lo", [P, 1])
        counts = sb("counts", [P, 2])
        rest_n = sb("rest_n", [P, BATCH * P // ECOLS])
        counts_max = sb("counts_max", [P, 2])
        num = sb("num", [P, 11], I32)
        N_LEFT, N_A, N_B, N_BATCH, N_EA, N_EB, N_BASE, N_ALL, N_FAR, N_KEPT, N_REST = range(11)
        lane = sb("lane", [P, P])
        lane_b = sb("lane_b", [P, P], BF16)
        lo_b = sb("lo_b", [P, KEPT1], BF16)
        hi_b = sb("hi_b", [P, KEPT1], BF16)
        left_i = sb("left_i", [P, 2, 8], I32)
        left_b = sb("left_b", [P, 2, 8], BF16)
        pads = XP[:, :, :, :].rearrange("p n r c -> p (n r c)")
        oh_lo = pads[:, 0:2048].bitcast(BF16).rearrange("p (h c l) -> p h c l", h=2, l=P)
        oh_hi = pads[:, 2048:2560].bitcast(BF16).rearrange("p (h c l) -> p h c l", h=2, l=HIS)
        to_last = sb("to_last", [P, HIS])
        rounds_d = nc.dram_tensor("rounds_d", (MAX_ROUNDS, P, ROUND), F32, kind="Internal").ap()
        generic_d = nc.dram_tensor("generic_d", (P, MAX_BATCHES * BATCH), F32, kind="Internal").ap()
        table_d = nc.dram_tensor("table_d", (NODES, ROW), F32, kind="Internal").ap()

        w_gat = sb("w_gat", [P, HE])
        att = sb("att", [P, 2, HE])
        gat_v = sb("gat_v", [P, 3, HE])
        table = shared[:, 2048:2688].rearrange("p (t f) -> p t f", f=ROW)
        prod = shared[:, 2688:3200].rearrange("p (t f) -> p t f", f=HE)
        a_dst = sb("a_dst", [P, HIS, HEADS])
        last_row = sb("last_row", [P, ROW])
        s_max = sb("s_max", [P, HIS, HEADS])
        e_max = sb("e_max", [P, HIS, HEADS])
        pen = sb("pen", [P, HIS])
        cand = sb("cand", [P, HIS, HEADS])
        g_idx = sb("g_idx", [P, ROUND], I32)
        g_int = sb("g_int", [P, ROUND], I32)
        g_hi = sb("g_hi", [P, ROUND])
        rows_g = sb("rows_g", [P, 2, HALFR, ROW])
        oh = [shared[:, o:o + HALFR * HIS].rearrange("p (k t) -> p k t", t=HIS) for o in (3200, 3712)]
        kept_rows = taps_w[:, 0:KEPT_ROUNDS * ROUND * ROW]
        kept_hi = sb("kept_hi", [P, KEPT_ROUNDS * ROUND])
        oh_t = shared[:, 3456:3712].rearrange("p (t k) -> p t k", t=HIS)
        sel_p = shared[:, 0:HALFR * 8 * HIS]
        per_hi = sb("per_hi", [P, 8, HIS])
        got = sb("got", [P, HALFR, 8])
        z2 = sb("z2", [P, 2, HALFR, HEADS])
        vals2 = sb("vals2", [P, 2, HALFR, ROW])
        spread_v = [[t[:, 0:GROUP * HIS * ROW].rearrange("p (k f) -> p k f", k=GROUP) for t in ts]
                    for ts in ((generic, T[:, :, :].rearrange("p i c -> p (i c)")), (small, pads))]
        m_w1 = pads[:, 2048:3072].rearrange("p (e h) -> p e h", e=EXPERTS)
        m_b1 = sb("m_b1", [P, EXPERTS, 2])
        m_w2 = pads[:, 3072:4096].rearrange("p (e k d) -> p e k d", e=EXPERTS, k=2)
        m_b2 = sb("m_b2", [P, EXPERTS])
        below = sb("below", [P, EXPERTS, EXPERTS])
        stat = sb("stat", [P, 4, HIS])
        score = sb("score", [P, HIS, EXPERTS])
        gate = sb("gate", [P, HIS, EXPERTS])
        pair = shared[:, 0:1024].rearrange("p (a t f) -> p a t f", a=2, t=HIS)
        mid = pads[:, 0:4 * CHUNK].rearrange("p (a b c) -> p a b c", a=2, b=2)
        y_exp = [scratch[:, 0:NODES], scratch[:, NODES:2 * NODES],
                 TEN[:, 0:2, :, :].rearrange("p a b c -> p (a b c)"), TEN[:, 2:4, :, :].rearrange("p a b c -> p (a b c)")]
        y_exp = [y.rearrange("p (i c) -> p i c", c=CHUNK) for y in y_exp]

        def image(t):
            return t[:, :, :].rearrange("p (n h) c -> p n (h c)", n=IMGS)

        x_in, wa_in, wb_in = sem("x_in"), sem("wa_in"), sem("wb_in")
        made = sem("made")
        padded = sem("padded")

        def layer_norm(tag, e):
            return LayerNorm(e, *(sem(f"{tag}_{n}") for n in LayerNorm._fields[1:]))

        ln0, ln1, ln2, ln3 = (layer_norm(f"ln{i}", e) for i, e in enumerate((0, 1, 0, 1)))

        off_ready, off_a, off_hi, off_r, off_m, off_done = (sem(f"off_{n}") for n in ("ready", "row", "hi", "rem", "mid", "done"))
        msk_cp = sem("msk_cp")
        msk_row_s, msk_hi, msk_r, msk_m, msk_done = (sem(f"msk_{n}") for n in ("row_s", "hi", "rem_s", "mid_s", "done"))
        bc_ready, ax_done, rx_done, txm_done = sem("bc_ready"), sem("ax_done"), sem("rx_done"), sem("txm_done")
        abs_done, relu_done, ten_done, main_done = sem("abs_done"), sem("relu_done"), sem("ten_done"), sem("main_done")
        own_ready, far_chain, ten_pool, mk_ready = (sem(n) for n in ("own_ready", "far_chain", "ten_pool", "mk_ready"))
        yt_ready, yt_done, res1 = sem("yt_ready"), sem("yt_done"), sem("res1")
        wrb_done = sem("wrb_done")
        rw_ready, rw_done, diag_done, col_done = sem("rw_ready"), sem("rw_done"), sem("diag_done"), sem("col_done")
        cmp_part, cmp_done, rank_ready, kept_done = sem("cmp_part"), sem("cmp_done"), sem("rank_ready"), sem("kept_done")
        h_ready, gelu_done, y_ready, yf_done = sem("h_ready"), sem("gelu_done"), sem("y_ready"), sem("yf_done")
        fin_a, fin_b, res2 = sem("fin_a"), sem("fin_b"), sem("res2")
        cv_ready, res3 = sem("cv_ready"), sem("res3")
        stored = sem("stored")
        passed = sem("passed")
        edges_first, edges_in, wc_in, wd_in = sem("edges_first"), sem("edges_in"), sem("wc_in"), sem("wd_in")
        k_front, k_tests, k_gens, e_step, e_chain, counted, reduced, made2 = sem("k_front"), sem("k_tests"), sem("k_gens"), sem("e_step"), sem("e_chain"), sem("counted"), sem("reduced"), sem("made2")
        left_known, left_coded, left_added, piece_made, piece_added = (sem(n) for n in (
            "left_known", "left_coded", "left_added", "piece_made", "piece_added"))
        batches_known, batch_ready, turned, turned_out, batch_known = (sem(n) for n in (
            "batches_known", "batch_ready", "turned", "turned_out", "batch_known"))
        batch_in, generic_made, generic_out = sem("batch_in"), sem("generic_made"), sem("generic_out")
        round_ready, round_stored, rounds_known = sem("round_ready"), sem("round_stored"), sem("rounds_known")
        r2_chain, shares_added = sem("r2_chain"), sem("shares_added")
        r_chain, rb_chain, b_chain = sem("r_chain"), sem("rb_chain"), sem("b_chain")
        feat_ready, t_chain, table_ready, table_out, last_in = (sem(n) for n in (
            "feat_ready", "t_chain", "table_ready", "table_out", "last_in"))
        key1_in, idx1_ready, rows1_in, max1_done, m1_chain = (sem(n) for n in (
            "key1_in", "idx1_ready", "rows1_in", "max1_done", "m1_chain"))
        key2_in, idx2_ready, rows2_in, got2, exp2, spread2, summed2, m2_chain = (sem(n) for n in (
            "key2_in", "idx2_ready", "rows2_in", "got2", "exp2", "spread2", "summed2", "m2_chain"))
        rows1_b, rows2_b, used2, vals_ready, spread2_b, kept_chain, m3_chain, pair_chain, summed2_b = (sem(n) for n in (
            "rows1_b", "rows2_b", "used2", "vals_ready", "spread2_b", "kept_chain", "m3_chain", "pair_chain", "summed2_b"))
        f_exp, f_ask = sem("f_exp"), sem("f_ask")
        mid_ready, mid_done, my_ready, my_done = sem("mid_ready"), sem("mid_done"), sem("my_ready"), sem("my_done")
        gates_known, gates_ready, gated, gated_b, res4 = (sem(n) for n in ("gates_known", "gates_ready", "gated", "gated_b", "res4"))

        POOL_BLOCKS, DVE_BLOCKS = ((0, 1), (2, 3)), ((2, 3), (0, 1))

        def spread(engine, half, g):
            ks = slice(GROUP * g, GROUP * (g + 1))
            return engine.tensor_tensor(spread_v[g][half].rearrange("p k (t f) -> p k t f", f=ROW),
                                        oh[half][:, ks, :].unsqueeze(3).to_broadcast([P, GROUP, HIS, ROW]),
                                        vals2[:, half, ks, :].unsqueeze(2).to_broadcast([P, GROUP, HIS, ROW]), ALU.mult)

        def spread_pairs(engine, half, wait):
            spread(engine, half, 1).then_inc(pair_chain, 1)
            wait()
            t = spread_v[1][half]
            return engine.tensor_tensor(t[:, 0:GROUP // 2, :], t[:, 0:GROUP // 2, :], t[:, GROUP // 2:GROUP, :], ALU.add)

        def near_mult(engine, b, h, blocks):
            parts = {}
            for j, s, c in near_parts(h):
                if j in blocks:
                    parts.setdefault(c, []).append((j, s))
            for c, js in parts.items():
                (j, s), k = js[0], len(js)
                t = near_w[b][:, s:s + NEAR * (k - 1) + c, :]
                m = txm[:, h, j * P:(j + k) * P].rearrange("p (k c) -> p k c", k=k).unsqueeze(2).to_broadcast([P, k, c, P])
                t = t.rearrange("p (k s) c -> p k s c", k=k)
                last = engine.tensor_tensor(t, t, m, ALU.mult)
            return last

        block = ctx.enter_context(nc.Block())

        WA, WB_, WC = 16 * 7, 16 * 8, 16 * 8

        @block.sync
        def _(sp):
            for n in range(IMGS):
                sp.dma_start(image(X)[:, n, :], a["x"][n].rearrange("c h w -> c (h w)")).then_inc(x_in, 16)
            for landed, cols in ((edges_first, slice(0, KEY_PART)), (edges_in, slice(KEY_PART, ECOLS))):
                sp.dma_start(src_i[:, cols], a["edges"][0].rearrange("(p c) -> p c", p=P)[:, cols]).then_inc(landed, 16)
                sp.dma_start(dst_i[:, cols], a["edges"][1].rearrange("(p c) -> p c", p=P)[:, cols]).then_inc(landed, 16)
            sp.dma_start(w_dcn[:, :], a["w_dcn"]).then_inc(wb_in, 16)
            sp.dma_start(wr[:, :], a["wr"]).then_inc(wb_in, 16)
            sp.dma_start(br_b[:, :], a["br"].partition_broadcast(P)).then_inc(wb_in, 16)
            sp.dma_start(f_w1[:, :], a["f_w1"]).then_inc(wb_in, 16)
            sp.dma_start(f_b1[:, :], a["f_b1"]).then_inc(wb_in, 16)
            sp.dma_start(f_w2[:, :, :], a["f_w2"].rearrange("(c p) d -> p c d", p=P)).then_inc(wb_in, 16)
            sp.dma_start(f_b2[:, :], a["f_b2"].rearrange("(p c) -> p c", c=1)).then_inc(wb_in, 16)
            sp.dma_start(w_conv[:, :, :], a["w_conv"]).then_inc(wb_in, 16)
            sp.dma_start(w_gat[:, :], a["w_gat"]).then_inc(wc_in, 16)
            for k, name in enumerate(("att_src", "att_dst")):
                sp.dma_start(att[:, k, :], a[name].partition_broadcast(P)).then_inc(wc_in, 16)
            for k, name in enumerate(("b_gat", "ln_gamma", "ln_beta")):
                sp.dma_start(gat_v[:, k, :], a[name].partition_broadcast(P)).then_inc(wc_in, 16)
            sp.dma_start(m_b1[:, :, :], a["m_b1"]).then_inc(wc_in, 16)
            sp.dma_start(m_b2[:, :], a["m_b2"]).then_inc(wc_in, 16)
            sp.wait_ge(generic_made, 1)
            sp.dma_start(generic_d, generic[:, :]).then_inc(generic_out, 16)
            sp.wait_ge(generic_out, 16)
            sp.wait_ge(batches_known, 1)
            batches = sp.value_load(num[0:1, N_BATCH:N_BATCH + 1], min_val=1, max_val=MAX_BATCHES)
            with sp.Fori(0, batches) as b:
                sp.wait_ge(turned, b * (BATCH // 4) + 1)
                sp.dma_start(batch_k[:, :], generic_d[:, bass.ds(b * BATCH, BATCH)]).then_inc(batch_in, 16)
                sp.wait_ge(batch_known, b + 1)
                sp.sem_inc(passed, 1)
                ea = sp.value_load(num[0:1, N_EA:N_EA + 1], min_val=1, max_val=KEPT2 // ROUND)
                eb = sp.value_load(num[0:1, N_EB:N_EB + 1], min_val=0, max_val=(BATCH * P - KEPT2) // ROUND)
                first = sp.value_load(num[0:1, N_BASE:N_BASE + 1], min_val=0, max_val=MAX_ROUNDS - BATCH * P // ROUND)
                with sp.Fori(0, ea) as r:
                    sp.wait_ge(round_ready, first + r + 1)
                    sp.dma_start(rounds_d[bass.ds(first + r, 1)].rearrange("o p s -> (o p) s"),
                                 sorted_k[:, bass.ds(r * ROUND, ROUND)]).then_inc(round_stored, 16)
                with sp.If(eb > 0):
                    with sp.Fori(0, eb) as r:
                        sp.wait_ge(round_ready, first + ea + r + 1)
                        sp.dma_start(rounds_d[bass.ds(first + ea + r, 1)].rearrange("o p s -> (o p) s"), round_k[:, :]).then_inc(round_stored, 16)
                    sp.nop()
                sp.nop()
            sp.wait_ge(rounds_known, 1)
            total = sp.value_load(num[0:1, N_ALL:N_ALL + 1], min_val=1, max_val=MAX_ROUNDS)
            sp.wait_ge(round_stored, total * 16 + 16)
            sp.wait_ge(cv_ready, CHUNKS)
            sp.dma_start(m_w1[:, :, :], a["m_w1"].rearrange("e c h -> c e h")).then_inc(wd_in, 16)
            sp.dma_start(m_w2[:, :, :, :], a["m_w2"].rearrange("e (k p) d -> p e k d", p=P)).then_inc(wd_in, 16)
            sp.wait_ge(table_ready, 1)
            sp.dma_start(table_d.rearrange("(t p) f -> p t f", p=P), table[:, :, :]).then_inc(table_out, 16)
            sp.wait_ge(table_out, 16)
            sp.dma_start(last_row[:, :], table_d[LAST].partition_broadcast(P)).then_inc(last_in, 16)
            with sp.Fori(0, total) as r:
                sp.wait_ge(idx1_ready, 2 * r + 1)
                sp.dma_start(round_k[:, :], rounds_d[bass.ds(r, 1)].rearrange("o p s -> (o p) s")).then_inc(key1_in, 16)
            sp.wait_ge(key1_in, total * 16)
            sp.sem_inc(key1_in, 16)
            kept_n = sp.value_load(num[0:1, N_KEPT:N_KEPT + 1], min_val=1, max_val=KEPT_ROUNDS)
            rest = sp.value_load(num[0:1, N_REST:N_REST + 1], min_val=0, max_val=MAX_ROUNDS - KEPT_ROUNDS)
            with sp.If(rest > 0):
                with sp.Fori(0, rest) as r:
                    sp.wait_ge(idx2_ready, r + 1)
                    sp.dma_start(round_k[:, :], rounds_d[bass.ds(kept_n + r, 1)].rearrange("o p s -> (o p) s")).then_inc(key2_in, 16)
                sp.nop()
            for n in range(IMGS):
                sp.wait_ge(res4, 2 * n + 2)
                sp.dma_start(out[n].rearrange("c h w -> c (h w)"), image(X)[:, n, :]).then_inc(stored, 16)
            sp.wait_ge(stored, 16 * IMGS)

        @block.gpsimd
        def _(pool):
            nc.gpsimd.memset(mean_w[:, :], 1.0 / P).then_inc(made, 1)
            nc.gpsimd.memset(ident[:, :], 0.0).then_inc(made, 1)
            nc.gpsimd.memset(eps[:, 0:1], 1e-6).then_inc(made, 1)
            nc.gpsimd.memset(eps[:, 1:2], 1e-5).then_inc(made, 1)
            for k, v in enumerate(KEY_BIAS):
                nc.gpsimd.memset(k_bias[:, k:k + 1], v).then_inc(made, 1)
            nc.gpsimd.memset(w_off[:, :, :], 0.0).then_inc(made, 1)
            pool.wait_ge(made, 9)
            nc.gpsimd.affine_select(out=ident[:, :], in_=ident[:, :], compare_op=ALU.not_equal, fill=1.0, base=0,
                                    pattern=[[-1, P]], channel_multiplier=1).then_inc(made, 1)
            pool.dma_start(w_off[:, :, 0:2 * TAPS], a["w_off"][:, :, 0:2 * TAPS]).then_inc(wa_in, 16)
            pool.dma_start(w_off[:, :, 32:32 + TAPS], a["w_off"][:, :, 2 * TAPS:3 * TAPS]).then_inc(wa_in, 16)
            pool.dma_start(b_off[0:2 * TAPS, :], a["b_off"][0:2 * TAPS].rearrange("(p c) -> p c", c=1)).then_inc(wa_in, 16)
            pool.dma_start(b_off[32:32 + TAPS, :], a["b_off"][2 * TAPS:3 * TAPS].rearrange("(p c) -> p c", c=1)).then_inc(wa_in, 16)
            pool.dma_start(base, a["base"]).then_inc(wa_in, 16)
            pool.dma_start(neg_y[:, :], a["neg_y"]).then_inc(wa_in, 16)
            pool.dma_start(neg_x[:, :], a["neg_x"]).then_inc(wa_in, 16)
            nc.gpsimd.memset(XP[:, :, :, :], 0.0).then_inc(made, 1)
            nc.gpsimd.memset(shared[0:96, 0:2048], 0.0).then_inc(made, 1)
            nc.gpsimd.memset(shared[0:96, 2048:4096], 0.0).then_inc(made, 1)
            nc.gpsimd.memset(sel[:, :, :], 0.0).then_inc(made, 1)
            nc.gpsimd.memset(zero_b[:, :], 0.0).then_inc(made, 1)
            nc.gpsimd.memset(ones_b[:, :], 1.0).then_inc(made, 1)
            nc.gpsimd.memset(later[:, :], 1.0).then_inc(made, 1)
            pool.wait_ge(made, 17)
            for b in range(3):
                nc.gpsimd.affine_select(out=sel[:, :, :], in_=sel[:, :, :], compare_op=ALU.not_equal, fill=1.0,
                                        base=-32 * b, pattern=[[-1, 2 * TAPS], [0, P]],
                                        channel_multiplier=1).then_inc(made, 1)
                pool.wait_ge(made, 18 + b)
            nc.gpsimd.affine_select(out=later[:, :], in_=later[:, :], compare_op=ALU.is_gt, fill=0.0, base=0,
                                    pattern=[[1, P]], channel_multiplier=-1).then_inc(made, 1)
            nc.gpsimd.iota(lane[:, :], [[1, P]], base=0, channel_multiplier=0,
                           allow_small_or_imprecise_dtypes=True).then_inc(made2, 1)
            nc.gpsimd.iota(neg_lo[:, :], [[0, 1]], base=0, channel_multiplier=-(1 << 17),
                           allow_small_or_imprecise_dtypes=True).then_inc(made2, 1)
            nc.gpsimd.memset(below[:, :, :], 1.0).then_inc(made2, 1)
            pool.wait_ge(made2, 3)
            nc.gpsimd.tensor_copy(lane_b[:, :], lane[:, :]).then_inc(made2, 1)
            nc.gpsimd.affine_select(out=below[:, :, :], in_=below[:, :, :], compare_op=ALU.is_gt, fill=0.0, base=0,
                                    pattern=[[1, EXPERTS], [-1, EXPERTS]], channel_multiplier=0).then_inc(made2, 1)
            pool.sem_inc(msk_done, 1)
            nc.gpsimd.memset(listed, NONE).then_inc(made2, 1)
            for n in range(IMGS):
                for h in range(2):
                    i = 2 * n + h
                    pool.wait_ge(ln0.normed, i + 3)
                    nc.gpsimd.tensor_copy(XP[:, n, 1 + HROWS * h:1 + HROWS * (h + 1), 1:1 + SIDE],
                                          T[:, i, :].rearrange("p (r c) -> p r c", c=SIDE)).then_inc(padded, 1)
            for i in range(CHUNKS):
                pool.wait_ge(msk_row_s, i + 3)
                pool.wait_ge(msk_hi, i + 1)
                nc.gpsimd.tensor_tensor(msk_rem, msk_row, MSK[0:TAPS, i, :], ALU.subtract).then_inc(msk_r, 1)
                pool.wait_ge(msk_r, i + 1)
                nc.gpsimd.tensor_copy(msk_mid, msk_rem).then_inc(msk_m, 1)
                pool.wait_ge(msk_m, i + 1)
                nc.gpsimd.tensor_copy(MSK[32:32 + TAPS, i, :], msk_mid).then_inc(msk_cp, 1)
                pool.wait_ge(msk_cp, i + 1)
                nc.gpsimd.tensor_tensor(MSK[64:64 + TAPS, i, :], msk_rem, msk_mid, ALU.subtract).then_inc(msk_done, 1)
            pool.wait_ge(msk_done, 1 + CHUNKS)
            pool.wait_ge(off_done, 2 + CHUNKS)
            nc.gpsimd.memset(generic[:, :], 0.0).then_inc(made2, 1)
            pool.wait_ge(counted, 1)
            nc.gpsimd.partition_all_reduce(counts_max[:, :], counts[:, :], P, bass.bass_isa.ReduceOp.max).then_inc(reduced, 1)
            pool.wait_ge(counted, 2)
            nc.gpsimd.partition_all_reduce(counts_max[:, :], counts[:, :], P, bass.bass_isa.ReduceOp.max).then_inc(reduced, 1)
            pool.wait_ge(batches_known, 1)
            pool.wait_ge(made2, 5)
            is_far = pool.value_load(num[0:1, N_FAR:N_FAR + 1], min_val=0, max_val=1)
            with pool.If(is_far > 0):
                for n in range(IMGS):
                    pool.wait_ge(yt_done, 3 * SRC_T * n + 2)
                    nc.gpsimd.tensor_copy(own_img, image(T)[:, n, :]).then_inc(own_ready, 1)
            with pool.If(is_far < 1):
                pool.sem_inc(ten_pool, 2)

                def pool_unit(n, q, s):
                    u, h = n * (2 * TAPS) + q * (2 * RING) + s, s % 2
                    pool.wait_ge(txm_done, u + 3)
                    pool.wait_ge(relu_done, u + 1)
                    pool.sem_inc(passed, 1)
                    near_mult(nc.gpsimd, s % RING, h, POOL_BLOCKS[h]).then_inc(ten_pool, 1)

                def pool_units(n, copy_next):
                    with pool.Fori(0, TAPS // RING - 1) as q:
                        for s in range(2 * RING):
                            pool_unit(n, q, s)
                    for s in range(2 * RING):
                        if s == 2 * RING - 2:
                            copy_next()
                        pool_unit(n, TAPS // RING - 1, s)

                def copy_own(n):
                    pool.wait_ge(yt_done, 2 * TAPS * n + 1)
                    pool.sem_inc(passed, 1)
                    nc.gpsimd.tensor_copy(own_img, image(T)[:, bass.ds(n, 1), :].rearrange("p o c -> p (o c)")).then_inc(own_ready, 1)

                nc.gpsimd.tensor_copy(own_img, image(T)[:, 0, :]).then_inc(own_ready, 1)
                with pool.Fori(0, IMGS - 1) as n:
                    pool_units(n, lambda: copy_own(n + 1))
                pool_units(IMGS - 1, lambda: pool.sem_inc(own_ready, 1))
                pool.nop()
            pool.wait_ge(piece_added, PIECES * IMGS + 2)
            nc.gpsimd.memset(XP[:, :, :, :], 0.0).then_inc(made2, 1)
            for i in range(CHUNKS):
                pool.wait_ge(ln1.normed, i + 3)
                nc.gpsimd.tensor_tensor(X[:, i, :], X[:, i, :], T[:, i, :], ALU.add).then_inc(fin_b, 1)
            for n in range(IMGS):
                for h in range(2):
                    i = 2 * n + h
                    pool.wait_ge(ln2.normed, i + 3)
                    nc.gpsimd.tensor_copy(XP[:, n, 1 + HROWS * h:1 + HROWS * (h + 1), 1:1 + SIDE],
                                          T[:, i, :].rearrange("p (r c) -> p r c", c=SIDE)).then_inc(padded, 1)
            batches = pool.value_load(num[0:1, N_BATCH:N_BATCH + 1], min_val=1, max_val=MAX_BATCHES)
            with pool.Fori(0, batches) as b:
                for k in range(2):
                    pool.wait_ge(counted, 2 * b + 3 + k)
                    pool.sem_inc(passed, 1)
                    nc.gpsimd.partition_all_reduce(counts_max[:, :], counts[:, :], P, bass.bass_isa.ReduceOp.max).then_inc(reduced, 1)
            pool.wait_ge(rounds_known, 1)
            total = pool.value_load(num[0:1, N_ALL:N_ALL + 1], min_val=1, max_val=MAX_ROUNDS)
            pool.wait_ge(table_out, 16)

            def gather(r, idx_ready, used, landed, by_half):
                for half in range(2):
                    pool.wait_ge(idx_ready, 2 * r + half + 2 if by_half else r + 2)
                    pool.sem_inc(passed, 1)
                    pool.wait_ge(used, 2 * r + half + 1)
                    pool.sem_inc(passed, 1)
                    for k in range(HALFR):
                        c = half * HALFR + k
                        pool.indirect_dma_start(rows_g[:, half, k, :], None, table_d,
                                                bass.IndirectOffsetOnAxis(ap=g_idx[:, c:c + 1], axis=0)).then_inc(landed[half], 16)

            with pool.Fori(0, total) as r:
                gather(r, idx1_ready, max1_done, (rows1_in, rows1_b), True)
            kept_n = pool.value_load(num[0:1, N_KEPT:N_KEPT + 1], min_val=1, max_val=KEPT_ROUNDS)
            pool.sem_inc(spread2_b, 2)
            with pool.Fori(0, kept_n) as r:
                for half in range(2):
                    v = 2 * r + half
                    pool.wait_ge(vals_ready, v + 1)
                    pool.wait_ge(summed2_b, v + 1)
                    pool.sem_inc(passed, 1)
                    spread_pairs(nc.gpsimd, half, lambda: (pool.wait_ge(pair_chain, v + 1), pool.sem_inc(passed, 1))).then_inc(spread2_b, 1)
            rest = pool.value_load(num[0:1, N_REST:N_REST + 1], min_val=0, max_val=MAX_ROUNDS - KEPT_ROUNDS)
            with pool.If(rest > 0):
                with pool.Fori(0, rest) as r:
                    gather(r, idx2_ready, used2, (rows2_in, rows2_b), False)
                pool.nop()

            with pool.Fori(0, CHUNKS) as i:
                pool.wait_ge(gated, EXPERTS * (i + 1) + 2)
                pool.sem_inc(passed, 1)
                for e in (0, 2):
                    nc.gpsimd.tensor_tensor(y_exp[e][:, bass.ds(i, 1), :], y_exp[e][:, bass.ds(i, 1), :],
                                            y_exp[e + 1][:, bass.ds(i, 1), :], ALU.add).then_inc(gated_b, 1)
                pool.wait_ge(gated_b, 3 * i + 2)
                pool.sem_inc(passed, 1)
                nc.gpsimd.tensor_tensor(y_exp[0][:, bass.ds(i, 1), :], y_exp[0][:, bass.ds(i, 1), :],
                                        y_exp[2][:, bass.ds(i, 1), :], ALU.add).then_inc(gated_b, 1)

        @block.scalar
        def _(act):
            def norm(ln, between=None):
                for i in range(CHUNKS):
                    act.wait_ge(ln.centred, i + 3)
                    act.wait_ge(ln.var_ready, i + 1)
                    nc.scalar.activation(sq[:, i % 2, :], T[:, i, :], ACT.Square).then_inc(ln.squared, 1)
                if between is not None:
                    between()
                act.wait_ge(ln.var_ready, CHUNKS + 2)
                nc.scalar.activation(dev[:, :], ps[2][:, 0:TILES], ACT.Sqrt, bias=eps[:, ln.eps:ln.eps + 1]).then_inc(ln.std_ready, 1)

            def key_tests(q):
                cols = bass.ts(q, KEY_PART)
                act.wait_ge(e_step, KEY_STEPS * q + 7)
                act.sem_inc(passed, 1)
                nc.scalar.activation(k_src, src_i[:, cols], ACT.Relu, scale=-float(NODES)).then_inc(k_front, 1)
                act.wait_ge(e_step, KEY_STEPS * q + 8)
                act.sem_inc(passed, 1)
                nc.scalar.activation(k_last, dst_i[:, cols], ACT.Identity, bias=k_bias[:, 0:1], scale=-1.0).then_inc(k_front, 1)
                act.wait_ge(e_step, KEY_STEPS * q + KEY_STEPS)
                act.sem_inc(passed, 1)
                nc.scalar.activation(k_node, dst_i[:, cols], ACT.Abs, bias=k_bias[:, 1:2]).then_inc(k_tests, 1)
                act.wait_ge(k_tests, 2 * q + 1)
                act.sem_inc(passed, 1)
                nc.scalar.activation(k_node, k_node, ACT.Identity, bias=k_bias[:, 2:3], scale=-SURE).then_inc(k_tests, 1)
                act.wait_ge(e_step, KEY_STEPS * (q + 1) + 4)
                act.sem_inc(passed, 1)
                nc.scalar.activation(k_gen, k_src, ACT.Identity, bias=k_bias[:, 3:4], scale=-SURE).then_inc(k_gens, 1)

            act.wait_ge(made, 10)
            norm(ln0, lambda: (act.wait_ge(edges_first, 32), act.sem_inc(passed, 1), key_tests(0)))
            act.wait_ge(edges_in, 32)
            with act.Fori(1, ECOLS // KEY_PART) as q:
                key_tests(q)
            act.sem_inc(msk_row_s, 2)
            act.wait_ge(wa_in, WA)
            act.wait_ge(e_step, KEY_STEPS * (ECOLS // KEY_PART) + KEY_STEPS)
            with act.Fori(0, IMGS) as n:
                for h in range(2):
                    i = 2 * n + h
                    act.wait_ge(off_ready, i + 1)
                    act.wait_ge(msk_done, i + 1)
                    nc.scalar.activation(msk_row, bank_of(i, slice(32, 32 + TAPS)), ACT.Sigmoid,
                                         bias=b_off[32:32 + TAPS, :]).then_inc(msk_row_s, 1)
                    act.wait_ge(msk_row_s, i + 3)
                    nc.scalar.copy(MSK[0:TAPS, i, :], msk_row).then_inc(msk_hi, 1)
            act.wait_ge(batches_known, 1)
            is_far = act.value_load(num[0:1, N_FAR:N_FAR + 1], min_val=0, max_val=1)
            with act.If(is_far > 0):
                act.sem_inc(abs_done, 4)
                act.sem_inc(ax_done, 1)
                with act.Fori(0, IMGS) as n:
                    with act.Fori(0, TAPS) as k:
                        for h in range(2):
                            u = (n * TAPS + k) * 2 + h
                            act.wait_ge(bc_ready, u + 1)
                            act.wait_ge(txm_done, u + 1)
                            nc.scalar.activation(absx[:, h, :], ps[2][:, :], ACT.Abs, bias=neg_x[:, :]).then_inc(ax_done, 1)
                            act.wait_ge(ax_done, u + 2)
                            nc.scalar.activation(absx[:, h, :], absx[:, h, :], ACT.Relu, bias=1.0, scale=-1.0).then_inc(rx_done, 1)
                            for g in range(2):
                                b, v = 2 * h + g, 2 * u + g
                                act.wait_ge(main_done, v + 1)
                                for j in range(GROUP):
                                    t = GROUP * g + j
                                    last = nc.scalar.activation(TEN[:, b, j, :], ps[h][:, :], ACT.Abs, bias=neg_y[:, t:t + 1])
                                last.then_inc(abs_done, 1)
                                act.wait_ge(abs_done, v + 5)
                                nc.scalar.activation(TEN[:, b, :, :], TEN[:, b, :, :], ACT.Relu, bias=1.0,
                                                     scale=-1.0).then_inc(relu_done, 1)
                act.nop()
            with act.If(is_far < 1):
                act.sem_inc(abs_done, 2)
                act.sem_inc(ax_done, 1)
                with act.Fori(0, IMGS) as n:
                    with act.Fori(0, TAPS // RING) as q:
                        for s in range(2 * RING):
                            u, h, w = n * (2 * TAPS) + q * (2 * RING) + s, s % 2, near_w[s % RING]
                            act.wait_ge(bc_ready, u + 1)
                            act.wait_ge(txm_done, u + 1)
                            nc.scalar.activation(absx[:, h, :], ps[2][:, :], ACT.Abs, bias=neg_x[:, :]).then_inc(ax_done, 1)
                            act.wait_ge(main_done, u + 1)
                            for at, (t, j, c, slot) in enumerate(near_tiles(h)):
                                if at == 1:
                                    act.wait_ge(ax_done, u + 2)
                                    nc.scalar.activation(absx[:, h, :], absx[:, h, :], ACT.Relu, bias=1.0, scale=-1.0).then_inc(rx_done, 1)
                                last = nc.scalar.activation(w[:, slot:slot + 2 * c - 1:2, :],
                                                            ps[h][:, j * P:(j + c) * P].rearrange("p (k c) -> p k c", k=c),
                                                            ACT.Abs, bias=neg_y[:, t:t + 1])
                            last.then_inc(abs_done, 1)
                            act.wait_ge(abs_done, u + 3)
                            used = w[:, 1 - h:4 * NEAR - h, :]
                            nc.scalar.activation(used, used, ACT.Relu, bias=1.0, scale=-1.0).then_inc(relu_done, 1)
                act.nop()
            act.sem_inc(gelu_done, 2)
            act.sem_inc(yf_done, 2)
            norm(ln1)
            act.wait_ge(wb_in, WB_)
            with act.Fori(0, IMGS) as n:
                for h in range(2):
                    i = 2 * n + h
                    for c in range(HID):
                        act.wait_ge(h_ready, HID * i + c + 1)
                        nc.scalar.activation(hid[h][:, c, :], ps[4 + c % 2][:, :], ACT.Gelu_apprx_tanh,
                                             bias=f_b1[:, c:c + 1]).then_inc(gelu_done, 1)
                    act.wait_ge(y_ready, i + 1)
                    act.wait_ge(col_done, 1)
                    nc.scalar.activation(YF[:, i, :], ps[6 + h][:, :], ACT.Identity, bias=f_b2[:, :]).then_inc(yf_done, 1)
            norm(ln2)
            act.wait_ge(made2, 5)
            batches = act.value_load(num[0:1, N_BATCH:N_BATCH + 1], min_val=1, max_val=MAX_BATCHES)
            act.sem_inc(turned_out, 2)
            with act.Fori(0, batches) as b:
                act.wait_ge(batch_ready, b + 1)
                for q in range(BATCH // 4):
                    act.wait_ge(turned, b * (BATCH // 4) + q + 2)
                    nc.scalar.activation(routed[:, q * CHUNK:(q + 1) * CHUNK], ps[4 + q % 2][:, :], ACT.Relu,
                                         bias=neg_lo[:, :]).then_inc(turned_out, 1)
            norm(ln3)
            act.wait_ge(rounds_known, 1)
            act.wait_ge(wc_in, WC)
            act.sem_inc(mid_done, 2)
            act.sem_inc(my_done, 2)

            def hidden(i, e):
                v = EXPERTS * i + e
                act.wait_ge(my_ready, v + 1)
                for c in range(2):
                    act.wait_ge(mid_ready, 2 * v + c + 1)
                    nc.scalar.activation(mid[:, e % 2, c, :], ps[2 + c][:, :], ACT.Gelu, bias=m_b1[:, e, c:c + 1]).then_inc(mid_done, 1)

            def expert_out(i, e):
                v = EXPERTS * i + e
                act.wait_ge(my_ready, v + 3)
                nc.scalar.activation(y_exp[e][:, i, :], ps[4 + e % 2][:, :], ACT.Identity, bias=m_b2[:, e:e + 1]).then_inc(my_done, 1)

            with act.Fori(0, CHUNKS) as i:
                hidden(i, 0)
                for e in range(1, EXPERTS):
                    hidden(i, e)
                    expert_out(i, e - 1)
                expert_out(i, EXPERTS - 1)
            total = act.value_load(num[0:1, N_ALL:N_ALL + 1], min_val=1, max_val=MAX_ROUNDS)
            with act.Fori(0, total) as r:
                for half in range(2):
                    act.wait_ge(got2, 2 * r + half + 1)
                    nc.scalar.activation(vals2[:, half, :, 0:HEADS], z2[:, half, :, :], ACT.Exp).then_inc(exp2, 1)
            act.wait_ge(f_ask, 1)
            nc.scalar.activation(cand[:, :, :], cand[:, :, :], ACT.Exp).then_inc(f_exp, 1)
            act.wait_ge(f_ask, 2)
            nc.scalar.activation(s_max[:, :, :], s_max[:, :, :], ACT.Exp).then_inc(f_exp, 1)
            act.wait_ge(f_ask, 3)
            nc.scalar.activation(stat[:, 1, :], stat[:, 1, :], ACT.Sqrt, bias=eps[:, 1:2]).then_inc(f_exp, 1)
            act.wait_ge(f_ask, 4)
            nc.scalar.activation(gate[:, :, :], gate[:, :, :], ACT.Exp).then_inc(f_exp, 1)

        @block.vector
        def _(dve):
            def norm(ln, res, credit, between=(None, None)):
                dve.sem_inc(ln.centred, 2)
                with dve.Fori(0, IMGS) as n:
                    for h in range(2):
                        i = 2 * n + h
                        if res is not None:
                            dve.wait_ge(res, i + credit + 1)
                        dve.wait_ge(ln.mean_ready, i + 1)
                        nc.vector.tensor_tensor(T[:, i, :], X[:, i, :], ps[h][:, :], ALU.subtract).then_inc(ln.centred, 1)
                if between[0] is not None:
                    between[0]()
                dve.wait_ge(ln.std_ready, 1)
                nc.vector.reciprocal(inv[:, :], dev[:, :]).then_inc(ln.inv_ready, 1)
                if between[1] is not None:
                    between[1]()
                dve.sem_inc(ln.normed, 2)
                with dve.Fori(0, IMGS) as n:
                    for h in range(2):
                        i = 2 * n + h
                        dve.wait_ge(ln.spread, i + 1)
                        nc.vector.tensor_tensor(T[:, i, :], T[:, i, :], ps[6 + h][:, :], ALU.mult).then_inc(ln.normed, 1)

            def chained(s_, first=0, apart=False):
                n = [0]

                def run(ins):
                    n[0] += 1
                    ins.then_inc(s_, 1)
                    dve.wait_ge(s_, first + n[0])
                    if apart:
                        dve.sem_inc(passed, 1)
                return run, n

            def make_keys(q):
                cols = bass.ts(q, KEY_PART)
                run, n = chained(e_step, KEY_STEPS * q + KEY_STEPS)
                dve.wait_ge(k_front, 2 * q + 1)
                run(nc.vector.scalar_tensor_tensor(k_src, k_src, float(NODES), src_i[:, cols], ALU.min, ALU.add))
                run(nc.vector.tensor_scalar(k_lo, dst_i[:, cols], 0.0, float(LAST), ALU.max, ALU.min))
                run(nc.vector.tensor_scalar(k_hi, k_lo, 7, None, ALU.logical_shift_right))
                run(nc.vector.tensor_scalar(k_src, k_src, 0.0, float(LAST), ALU.max, ALU.min))
                run(nc.vector.scalar_tensor_tensor(k_key, k_hi, 4096.0, k_src, ALU.mult, ALU.add))
                run(nc.vector.scalar_tensor_tensor(k_lo, k_hi, -float(P), k_lo, ALU.mult, ALU.add))
                dve.wait_ge(k_gens, q + 1)
                run(nc.vector.tensor_tensor(k_gen, k_gen, k_last, ALU.max))
                run(nc.vector.scalar_tensor_tensor(k_key, k_lo, float(1 << 17), k_key, ALU.mult, ALU.add))
                run(nc.vector.tensor_tensor(k_key, k_key, k_gen, ALU.min))
                dve.wait_ge(k_tests, 2 * q + 2)
                run(nc.vector.scalar_tensor_tensor(keys[:, cols], k_node, NONE, k_key, ALU.max, ALU.min))
                assert n[0] == KEY_STEPS

            def first_keys():
                dve.wait_ge(edges_first, 32)
                make_keys(0)

            def second_keys():
                dve.wait_ge(edges_in, 32)
                make_keys(1)

            dve.sem_inc(e_step, KEY_STEPS)
            dve.wait_ge(x_in, 16 * IMGS)
            norm(ln0, None, 0, (first_keys, second_keys))
            with dve.Fori(2, ECOLS // KEY_PART) as q:
                make_keys(q)
            run, _ = chained(e_chain)
            dve.wait_ge(made2, 6)
            for c in range(ECOLS // FIRST):
                last = nc.vector.max(listed[:, 8 * c:8 * c + 8], keys[:, FIRST * c:FIRST * (c + 1)])
            run(last)
            for c in range(ECOLS // FIRST):
                part = keys[:, FIRST * c:FIRST * (c + 1)]
                last = nc.vector.match_replace(part, listed[:, 8 * c:8 * c + 8], part, NONE)
            run(last)
            dve.wait_ge(wa_in, WA)
            dve.sem_inc(off_done, 2)
            with dve.Fori(0, IMGS) as n:
                for h in range(2):
                    i = 2 * n + h
                    dve.wait_ge(off_ready, i + 1)
                    dve.wait_ge(off_done, i + 2)
                    nc.vector.scalar_tensor_tensor(off_row, bank_of(i, slice(0, 2 * TAPS)), b_off[0:2 * TAPS, :],
                                                   base[:, h * CHUNK:(h + 1) * CHUNK], ALU.add, ALU.add).then_inc(off_a, 1)
                    dve.wait_ge(off_a, i + 1)
                    nc.vector.tensor_copy(OFS[0:2 * TAPS, i, :], off_row).then_inc(off_hi, 1)
                    dve.wait_ge(off_hi, i + 1)
                    nc.vector.tensor_tensor(off_rem, off_row, OFS[0:2 * TAPS, i, :], ALU.subtract).then_inc(off_r, 1)
                    dve.wait_ge(off_r, i + 1)
                    nc.vector.tensor_copy(off_mid, off_rem).then_inc(off_m, 1)
                    dve.wait_ge(off_m, i + 1)
                    nc.vector.tensor_copy(OFS[32:32 + 2 * TAPS, i, :], off_mid)
                    nc.vector.tensor_tensor(OFS[64:64 + 2 * TAPS, i, :], off_rem, off_mid, ALU.subtract).then_inc(off_done, 1)
            for k, op in enumerate((ALU.max, ALU.min)):
                nc.vector.tensor_reduce(far[:, k:k + 1], banks[0:2 * TAPS, :, :].rearrange("p i c -> p (i c)"), AX_X, op).then_inc(far_chain, 1)
            dve.wait_ge(far_chain, 2)
            nc.vector.tensor_scalar(far[:, :], far[:, :], b_off[0:2 * TAPS, :], None, ALU.add).then_inc(far_chain, 1)
            dve.wait_ge(far_chain, 3)
            nc.vector.tensor_tensor(far[:, :], far[:, :], far[:, :], ALU.mult).then_inc(far_chain, 1)
            dve.wait_ge(far_chain, 4)
            dve.wait_ge(made2, 5)
            run(nc.vector.memset(counts[:, :], 0.0))
            run(nc.vector.tensor_scalar(flags, keys, NONE + 1, None, ALU.is_gt))
            run(nc.vector.tensor_reduce(counts[:, 0:1], flags, AX_X, ALU.add))
            run(nc.vector.tensor_reduce(counts[0:2 * TAPS, 1:2], far[:, :], AX_X, ALU.max))
            dve.sem_inc(counted, 1)
            dve.wait_ge(reduced, 1)
            run(nc.vector.tensor_scalar(num[:, N_FAR:N_FAR + 1], counts_max[:, 1:2], FAR, None, ALU.is_gt))
            run(nc.vector.tensor_scalar(num[:, N_LEFT:N_LEFT + 1], counts_max[:, 0:1], 7.0, None, ALU.add))
            run(nc.vector.tensor_scalar(num[:, N_LEFT:N_LEFT + 1], num[:, N_LEFT:N_LEFT + 1], 3, None, ALU.logical_shift_right))
            run(nc.vector.tensor_scalar(num[:, N_LEFT:N_LEFT + 1], num[:, N_LEFT:N_LEFT + 1], 1.0, None, ALU.max))
            lefts = dve.value_load(num[0:1, N_LEFT:N_LEFT + 1], min_val=1, max_val=(ECOLS - KEPT1) // 8)
            dve.sem_inc(left_known, 1)
            with dve.Fori(0, lefts) as r:
                step, _ = chained(r_chain, r * 3, True)
                step(nc.vector.max(top8[:, :], keys))
                step(nc.vector.tensor_copy(listed[:, bass.ds(KEPT1 + 8 * r, 8)], top8[:, :]))
                step(nc.vector.match_replace(keys, top8[:, :], keys, NONE))
            code = code_i[:, 0:KEPT1]
            run(nc.vector.tensor_scalar(code, listed[:, 0:KEPT1], -1.0, -1.0, ALU.mult, ALU.add))
            run(nc.vector.tensor_scalar(code_i[:, KEPT1:2 * KEPT1], code, P - 1, None, ALU.bitwise_and))
            run(nc.vector.tensor_copy(lo_b[:, :], code_i[:, KEPT1:2 * KEPT1]))
            run(nc.vector.tensor_scalar(code, code, 7, None, ALU.arith_shift_right))
            run(nc.vector.tensor_copy(hi_b[:, :], code))
            with dve.Fori(0, lefts) as r:
                step, _ = chained(left_coded, r * 7)
                step(nc.vector.tensor_scalar(left_i[:, 0, :], listed[:, bass.ds(KEPT1 + 8 * r, 8)], -1.0, -1.0, ALU.mult, ALU.add))
                step(nc.vector.tensor_scalar(left_i[:, 1, :], left_i[:, 0, :], P - 1, None, ALU.bitwise_and))
                step(nc.vector.tensor_scalar(left_i[:, 0, :], left_i[:, 0, :], 7, None, ALU.arith_shift_right))
                step(nc.vector.tensor_copy(left_b[:, 0, :], left_i[:, 0, :]))
                step(nc.vector.tensor_copy(left_b[:, 1, :], left_i[:, 1, :]))
                dve.wait_ge(left_added, r + 1)
                step(nc.vector.tensor_tensor(oh_lo[:, 0, 0:8, :], left_b[:, 1, :].unsqueeze(2).to_broadcast([P, 8, P]),
                                             lane_b[:, :].unsqueeze(1).to_broadcast([P, 8, P]), ALU.is_equal))
                step(nc.vector.tensor_tensor(oh_hi[:, 0, 0:8, :], left_b[:, 0, :].unsqueeze(2).to_broadcast([P, 8, HIS]),
                                             lane_b[:, 0:HIS].unsqueeze(1).to_broadcast([P, 8, HIS]), ALU.is_equal))
            dve.wait_ge(left_added, lefts + 1)
            run(nc.vector.tensor_copy(to_last[:, :], ps[7][:, 0:HIS]))
            dve.wait_ge(made2, 7)
            by_part = listed[:, 0:KEPT1].rearrange("p (c k) -> p c k", k=8)
            for out_, in_ in ((keys[:, 0:FRONT_N].rearrange("p (c k) -> p c k", k=FRONT), by_part[:, :, 0:FRONT]),
                              (keys[:, FRONT_N:KEPT1].rearrange("p (c k) -> p c k", k=8 - FRONT), by_part[:, :, FRONT:8]),
                              (keys[:, KEPT1:ECOLS], listed[:, KEPT1:ECOLS])):
                run(nc.vector.tensor_scalar(out_, in_, 1.0, 0.0, ALU.add, ALU.max))
            run(nc.vector.tensor_scalar(flags, keys, 0.5, None, ALU.is_gt))
            run(nc.vector.tensor_reduce(counts[:, 0:1], flags[:, 0:FRONT_N], AX_X, ALU.add))
            run(nc.vector.tensor_reduce(counts[:, 1:2], flags[:, FRONT_N:ECOLS], AX_X, ALU.add))
            dve.sem_inc(counted, 1)
            dve.wait_ge(reduced, 2)
            ab = num[:, N_A:N_B + 1]
            run(nc.vector.tensor_scalar(ab, counts_max[:, :], 7.0, None, ALU.add))
            run(nc.vector.tensor_scalar(ab, ab, 3, None, ALU.logical_shift_right))
            run(nc.vector.tensor_scalar(num[:, N_A:N_A + 1], num[:, N_A:N_A + 1], 1.0, None, ALU.max))
            run(nc.vector.tensor_tensor(num[:, N_BATCH:N_BATCH + 1], num[:, N_A:N_A + 1], num[:, N_B:N_B + 1], ALU.add))
            run(nc.vector.tensor_scalar(num[:, N_BATCH:N_BATCH + 1], num[:, N_BATCH:N_BATCH + 1], float(BATCH // 8 - 1),
                                        float((1 << 18) // (BATCH // 8) + 1), ALU.add, ALU.mult))
            run(nc.vector.tensor_scalar(num[:, N_BATCH:N_BATCH + 1], num[:, N_BATCH:N_BATCH + 1], 18, None, ALU.logical_shift_right))
            run(nc.vector.memset(num[:, N_ALL:N_ALL + 1], 0))
            in_a = dve.value_load(num[0:1, N_A:N_A + 1], min_val=1, max_val=FRONT_N // 8)
            in_b = dve.value_load(num[0:1, N_B:N_B + 1], min_val=0, max_val=(ECOLS - FRONT_N) // 8)
            batches = dve.value_load(num[0:1, N_BATCH:N_BATCH + 1], min_val=1, max_val=MAX_BATCHES)
            dve.sem_inc(batches_known, 1)
            with dve.Fori(0, in_a) as r:
                step, _ = chained(rb_chain, r * 3, True)
                part = keys[:, 0:FRONT_N]
                step(nc.vector.max(top8[:, :], part))
                step(nc.vector.tensor_copy(generic[:, bass.ds(8 * r, 8)], top8[:, :]))
                step(nc.vector.match_replace(part, top8[:, :], part, 0.0))
            with dve.If(in_b > 0):
                with dve.Fori(0, in_b) as r:
                    step, _ = chained(rb_chain, (in_a + r) * 3, True)
                    part = keys[:, FRONT_N:ECOLS]
                    step(nc.vector.max(top8[:, :], part))
                    step(nc.vector.tensor_copy(generic[:, bass.ds(8 * (in_a + r), 8)], top8[:, :]))
                    step(nc.vector.match_replace(part, top8[:, :], part, 0.0))
                dve.nop()
            dve.sem_inc(generic_made, 1)
            def weights(n, k, h):
                u = (n * TAPS + k) * 2 + h
                dve.wait_ge(rx_done, u + 1)
                dve.wait_ge(ten_done, 2 * u + 2)
                nc.vector.tensor_tensor(txm[:, h, :], absx[:, h, :], ps[3][:, :], ALU.mult).then_inc(txm_done, 1)
                dve.wait_ge(txm_done, u + 3)
                for g in range(2):
                    b, v = 2 * h + g, 2 * u + g
                    dve.wait_ge(relu_done, v + 1)
                    nc.vector.tensor_tensor(TEN[:, b, :, :], TEN[:, b, :, :],
                                            txm[:, h:h + 1, :].to_broadcast([P, GROUP, CHUNK]), ALU.mult).then_inc(ten_done, 1)

            def one_hot(n, k, h):
                u = PIECES * n + 2 * k + h
                dve.wait_ge(piece_added, u + 1)
                cols = bass.ds(u * PIECE, PIECE)
                nc.vector.tensor_tensor(oh_lo[:, h, :, :], lo_b[:, cols].unsqueeze(2).to_broadcast([P, PIECE, P]),
                                        lane_b[:, :].unsqueeze(1).to_broadcast([P, PIECE, P]), ALU.is_equal)
                nc.vector.tensor_tensor(oh_hi[:, h, :, :], hi_b[:, cols].unsqueeze(2).to_broadcast([P, PIECE, HIS]),
                                        lane_b[:, 0:HIS].unsqueeze(1).to_broadcast([P, PIECE, HIS]), ALU.is_equal).then_inc(piece_made, 1)

            def image_sums(n):
                dve.wait_ge(piece_added, PIECES * (n + 1) + 2)
                nc.vector.tensor_tensor(to_last[:, :], to_last[:, :], ps[7][:, 0:HIS], ALU.add).then_inc(shares_added, 1)
                for h in range(2):
                    i = 2 * n + h
                    nc.vector.tensor_tensor(X[:, i, :], X[:, i, :], ps[4 + h][:, :], ALU.add).then_inc(res1, 1)

            is_far = dve.value_load(num[0:1, N_FAR:N_FAR + 1], min_val=0, max_val=1)
            dve.sem_inc(txm_done, 2)
            dve.sem_inc(shares_added, 1)
            dve.sem_inc(res1, 2)
            with dve.If(is_far > 0):
                dve.sem_inc(ten_done, 4)
                dve.sem_inc(yt_done, 2)
                with dve.Fori(0, IMGS) as n:
                    dve.wait_ge(main_done, 4 + 4 * TAPS * n)
                    for q in range(3 * SRC_T):
                        t, g = divmod(q, 3)
                        w = min(CHUNK, TAPS * P - g * CHUNK)
                        dve.wait_ge(yt_ready, 3 * SRC_T * n + q + 1)
                        nc.vector.tensor_copy(YT[:, t, g * CHUNK:g * CHUNK + w], ps[6 + q % 2][:, 0:w]).then_inc(yt_done, 1)
                    with dve.Fori(0, PIECES // 2) as k:
                        for h in range(2):
                            weights(n, k, h)
                            one_hot(n, k, h)
                    for k in range(PIECES // 2, TAPS):
                        for h in range(2):
                            weights(n, k, h)
                    dve.wait_ge(main_done, 4 + 4 * TAPS * (n + 1))
                    image_sums(n)
                dve.nop()
            with dve.If(is_far < 1):
                dve.sem_inc(ten_done, 2)
                dve.sem_inc(yt_done, 1)

                def keep_tap(n, k, r, h):
                    w = n * (2 * TAPS) + 2 * k + h
                    dve.wait_ge(yt_ready, w + 1)
                    nc.vector.tensor_copy(YTN[:, r, 4 * h:4 * h + 4, :], ps[6][:, :].rearrange("p (t c) -> p t c", c=P)).then_inc(yt_done, 1)

                def near_unit(n, s):
                    u, h, k = n * (2 * TAPS) + s, s % 2, s // 2
                    dve.wait_ge(rx_done, u + 1)
                    dve.wait_ge(mk_ready, u + 1)
                    dve.wait_ge(ten_done, u + 1)
                    dve.wait_ge(ten_pool, u + 1)
                    nc.vector.tensor_tensor(txm[:, h, :], absx[:, h, :], ps[3][:, :], ALU.mult).then_inc(txm_done, 1)
                    if s < PIECES:
                        one_hot(n, k, h)
                    dve.wait_ge(txm_done, u + 3)
                    dve.wait_ge(relu_done, u + 1)
                    near_mult(nc.vector, s % RING, h, DVE_BLOCKS[h]).then_inc(ten_done, 1)
                    if s == 0:
                        with dve.If(n > 0):
                            last_sums(nc.s_assert_within(n - 1, 0, IMGS - 2, skip_runtime_bounds_check_because="n is above 0 here"))
                    keep_tap(n, k + 1, (k + 1) % RING, h)

                def last_sums(n):
                    dve.wait_ge(main_done, 2 * TAPS * (n + 1) + RING)
                    dve.sem_inc(passed, 1)
                    image_sums(n)

                for h in range(2):
                    keep_tap(0, 0, 0, h)
                with dve.Fori(0, IMGS) as n:
                    for s in range(2 * TAPS):
                        near_unit(n, s)
                last_sums(IMGS - 1)
                dve.nop()
            dve.wait_ge(wb_in, WB_)
            nc.vector.tensor_copy(wr_b[:, :], wr[:, 0:1].to_broadcast([P, P])).then_inc(wrb_done, 1)
            norm(ln1, res1, 2)
            dve.wait_ge(wb_in, WB_)
            dve.sem_inc(rw_done, 2)
            with dve.Fori(0, IMGS) as n:
                for h in range(2):
                    i = 2 * n + h
                    dve.wait_ge(rw_ready, i + 1)
                    nc.vector.tensor_scalar(RW[:, i, :], ps[h][:, :], br_b[:, :], None, ALU.add).then_inc(rw_done, 1)
            dve.wait_ge(rw_done, 2 + CHUNKS)
            nc.vector.tensor_tensor(YF[:, :, :].rearrange("p a (b c) -> p (a b) c", c=P),
                                    RW[:, :, :].rearrange("p a (b c) -> p (a b) c", c=P),
                                    ident[:, :].unsqueeze(1).to_broadcast([P, TILES, P]), ALU.mult).then_inc(diag_done, 1)
            dve.wait_ge(diag_done, 1)
            nc.vector.tensor_reduce(w_col[:, :, :].rearrange("p n t -> p (n t)"),
                                    YF[:, :, :].rearrange("p a (b c) -> p (a b) c", c=P), AX_X, ALU.add).then_inc(col_done, 1)
            dve.wait_ge(col_done, 1)
            dve.sem_inc(rank_ready, 1)
            dve.sem_inc(kept_done, 2)
            with dve.Fori(0, IMGS) as n:
                dve.wait_ge(rank_ready, n + 1)
                rows = image(RW)
                for t in range(SRC_T):
                    own = w_col[:, n, t:t + 1]
                    e = (t + 1) * P
                    nc.vector.tensor_scalar(tie[:, :], rows[:, n, e - P:e], own, None, ALU.is_equal).then_inc(cmp_part, 1)
                    nc.vector.tensor_scalar(cmp_b[:, t, 0:e], rows[:, n, 0:e], own, None, ALU.is_lt).then_inc(cmp_part, 1)
                    if e < POS:
                        nc.vector.tensor_scalar(cmp_b[:, t, e:], rows[:, n, e:], own, None, ALU.is_le)
                    dve.wait_ge(cmp_part, (n * SRC_T + t) * 3 + 2)
                    nc.vector.tensor_tensor(tie[:, :], tie[:, :], later[:, :], ALU.mult).then_inc(cmp_part, 1)
                    dve.wait_ge(cmp_part, (n * SRC_T + t) * 3 + 3)
                    nc.vector.tensor_tensor(cmp_b[:, t, e - P:e], cmp_b[:, t, e - P:e], tie[:, :], ALU.add).then_inc(cmp_done, 1)
                    dve.wait_ge(cmp_done, n * SRC_T + t + 1)
                dve.wait_ge(rank_ready, n + 2)
                for h in range(2):
                    nc.vector.scalar_tensor_tensor(RW[:, 2 * n + h, :], ps[2 + h][:, :], float(KEPT), RW[:, 2 * n + h, :],
                                                   ALU.is_lt, ALU.mult).then_inc(kept_done, 1)
                for h in range(2):
                    i = 2 * n + h
                    dve.wait_ge(yf_done, i + 3)
                    dve.wait_ge(kept_done, i + 3)
                    nc.vector.tensor_tensor(YF[:, i, :], YF[:, i, :], RW[:, i, :], ALU.mult).then_inc(fin_a, 1)
                for h in range(2):
                    i = 2 * n + h
                    dve.wait_ge(fin_a, i + 1)
                    dve.wait_ge(fin_b, i + 1)
                    nc.vector.tensor_tensor(X[:, i, :], X[:, i, :], YF[:, i, :], ALU.add).then_inc(res2, 1)
            norm(ln2, res2, 0)
            BATCH_STEPS = 22
            dve.sem_inc(round_stored, 16)
            with dve.Fori(0, batches) as b:
                run, n = chained(b_chain, b * BATCH_STEPS, True)
                dve.sem_inc(batch_ready, 1)
                for c in range(BATCH // 16):
                    dve.wait_ge(turned_out, b * (BATCH // 4) + 4 * (c + 1) + 2)
                    dve.sem_inc(passed, 1)
                    part = routed[:, c * 4 * CHUNK:(c + 1) * 4 * CHUNK]
                    last = nc.vector.scalar_tensor_tensor(part, part, float(1 << 17), part, ALU.is_le, ALU.mult)
                run(last)
                parts = routed.rearrange("p (s c) -> p c s", c=BCHUNKS)
                for c in range(BCHUNKS):
                    last = nc.vector.max(kept2[:, 8 * c:8 * c + 8], parts[:, c, :])
                run(last)
                fl = wide_buf[:, BATCH * P:BATCH * P + ECOLS]
                run(nc.vector.tensor_scalar(fl[:, 0:KEPT2], kept2[:, :], 0.5, None, ALU.is_gt))
                run(nc.vector.tensor_reduce(counts[:, 0:1], fl[:, 0:KEPT2], AX_X, ALU.add))
                run(nc.vector.tensor_reduce(counts[:, 1:2], kept2[:, :].rearrange("p (c k) -> p c k", k=8)[:, :, 7], AX_X, ALU.max))
                dve.sem_inc(counted, 1)
                dve.wait_ge(reduced, 2 * b + 3)
                dve.sem_inc(passed, 1)
                before = dve.value_load(num[0:1, N_ALL:N_ALL + 1], min_val=0, max_val=MAX_ROUNDS)
                dve.wait_ge(round_stored, before * 16 + 16)
                dve.sem_inc(passed, 1)
                e_ab = num[:, N_EA:N_EB + 1]
                run(nc.vector.tensor_scalar(e_ab, counts_max[:, :], float(ROUND - 1), None, ALU.add))
                run(nc.vector.tensor_scalar(e_ab, e_ab, 4, None, ALU.logical_shift_right))
                run(nc.vector.memset(counts[:, 1:2], 0.0))
                full = dve.value_load(num[0:1, N_EB:N_EB + 1], min_val=0, max_val=(1 << 17) // ROUND)
                with dve.If(full > 0):
                    for c in range(BCHUNKS):
                        last = nc.vector.match_replace(parts[:, c, :], kept2[:, 8 * c:8 * c + 8], parts[:, c, :], 0.0)
                    run(last)
                    for c in range(BATCH * P // ECOLS):
                        run(nc.vector.tensor_scalar(fl, routed[:, c * ECOLS:(c + 1) * ECOLS], 0.5, None, ALU.is_gt))
                        run(nc.vector.tensor_reduce(rest_n[:, c:c + 1], fl, AX_X, ALU.add))
                    run(nc.vector.tensor_reduce(counts[:, 1:2], rest_n[:, :], AX_X, ALU.add))
                with dve.If(full < 1):
                    dve.sem_inc(b_chain, 2 * (BATCH * P // ECOLS) + 2)
                dve.sem_inc(counted, 1)
                dve.wait_ge(reduced, 2 * b + 4)
                dve.sem_inc(passed, 1)
                run(nc.vector.tensor_scalar(num[:, N_EB:N_EB + 1], counts_max[:, 1:2], float(ROUND - 1), None, ALU.add))
                run(nc.vector.tensor_scalar(num[:, N_EB:N_EB + 1], num[:, N_EB:N_EB + 1], 4, None, ALU.logical_shift_right))
                run(nc.vector.tensor_scalar(num[:, N_EA:N_EA + 1], num[:, N_EA:N_EA + 1], 1.0, None, ALU.max))
                run(nc.vector.tensor_copy(num[:, N_BASE:N_BASE + 1], num[:, N_ALL:N_ALL + 1]))
                run(nc.vector.tensor_tensor(num[:, N_ALL:N_ALL + 1], num[:, N_ALL:N_ALL + 1], num[:, N_EA:N_EA + 1], ALU.add))
                run(nc.vector.tensor_tensor(num[:, N_ALL:N_ALL + 1], num[:, N_ALL:N_ALL + 1], num[:, N_EB:N_EB + 1], ALU.add))
                ea = dve.value_load(num[0:1, N_EA:N_EA + 1], min_val=1, max_val=KEPT2 // ROUND)
                eb = dve.value_load(num[0:1, N_EB:N_EB + 1], min_val=0, max_val=(BATCH * P - KEPT2) // ROUND)
                first = dve.value_load(num[0:1, N_BASE:N_BASE + 1], min_val=0, max_val=MAX_ROUNDS - BATCH * P // ROUND)
                dve.sem_inc(batch_known, 1)

                def emit(at, part, place=None):
                    step, _ = chained(r2_chain, at * 5, True)
                    if place is None:
                        dve.wait_ge(round_stored, at * 16 + 16)
                        dve.sem_inc(passed, 1)
                    for k in range(2):
                        step(nc.vector.max(round_k[:, 8 * k:8 * k + 8], part))
                        step(nc.vector.match_replace(part, round_k[:, 8 * k:8 * k + 8], part, 0.0))
                    if place is None:
                        dve.sem_inc(r2_chain, 1)
                    else:
                        step(nc.vector.tensor_copy(place, round_k[:, :]))
                    dve.sem_inc(round_ready, 1)

                with dve.Fori(0, ea) as r:
                    emit(first + r, kept2[:, :], sorted_k[:, bass.ds(r * ROUND, ROUND)])
                with dve.If(eb > 0):
                    with dve.Fori(0, eb) as r:
                        emit(first + ea + r, routed)
                    dve.nop()
                assert n[0] == BATCH_STEPS
                dve.nop()
            run, _ = chained(t_chain)
            run(nc.vector.tensor_scalar(num[:, N_KEPT:N_KEPT + 1], num[:, N_ALL:N_ALL + 1], float(KEPT_ROUNDS), None, ALU.min))
            run(nc.vector.tensor_tensor(num[:, N_REST:N_REST + 1], num[:, N_ALL:N_ALL + 1], num[:, N_KEPT:N_KEPT + 1], ALU.subtract))
            dve.sem_inc(rounds_known, 1)
            dve.sem_inc(res3, 2)
            with dve.Fori(0, IMGS) as n:
                for h in range(2):
                    i = 2 * n + h
                    dve.wait_ge(cv_ready, i + 1)
                    nc.vector.tensor_tensor(X[:, i, :], X[:, i, :], bank_of(i), ALU.add).then_inc(res3, 1)
            norm(ln3, res3, 2)
            run, _ = chained(t_chain, 2)
            dve.wait_ge(wc_in, WC)
            dve.wait_ge(feat_ready, 1)
            feats = table[:, :, 0:HE]
            run(nc.vector.tensor_copy(feats, ps[0][:, :].rearrange("p (t f) -> p t f", f=HE)))
            for k, o in ((0, table[:, :, HE:ROW]), (1, a_dst[:, :, :])):
                run(nc.vector.tensor_tensor(prod[:, :, :], feats, att[:, k:k + 1, :].to_broadcast([P, HIS, HE]), ALU.mult))
                run(nc.vector.tensor_reduce(o, prod[:, :, :].rearrange("p t (h e) -> p t h e", h=HEADS), AX_X, ALU.add))
                if k == 0:
                    dve.sem_inc(table_ready, 1)
            a_src = table[:, :, HE:ROW]
            run(nc.vector.tensor_scalar(pen[:, :], to_last[:, :], 0.5, -BIG, ALU.is_lt, ALU.mult))
            total = dve.value_load(num[0:1, N_ALL:N_ALL + 1], min_val=1, max_val=MAX_ROUNDS)

            def decode(step, idx_ready, part=slice(0, ROUND)):
                step(nc.vector.tensor_scalar(g_int[:, part], round_k[:, part], -1.0, None, ALU.add))
                step(nc.vector.tensor_scalar(g_idx[:, part], g_int[:, part], LAST, None, ALU.bitwise_and))
                step(nc.vector.tensor_scalar(g_int[:, part], g_int[:, part], 12, None, ALU.arith_shift_right))
                step(nc.vector.tensor_copy(g_hi[:, part], g_int[:, part]))
                dve.sem_inc(idx_ready, 1)

            run(nc.vector.tensor_copy(per_hi[:, 0:HEADS, :], a_dst[:, :, :].rearrange("p t h -> p h t")))
            dve.sem_inc(idx1_ready, 1)
            dve.sem_inc(max1_done, 2)
            lanes = lane[:, 0:HIS]
            M1, KEEPS = 2 * (5 + 4), 1 + 2 * 6
            halves = (slice(0, HALFR), slice(HALFR, ROUND))
            kept_n = dve.value_load(num[0:1, N_KEPT:N_KEPT + 1], min_val=1, max_val=KEPT_ROUNDS)
            rest = dve.value_load(num[0:1, N_REST:N_REST + 1], min_val=0, max_val=MAX_ROUNDS - KEPT_ROUNDS)

            def pick(step, half, first, out):
                k4 = out.shape[2]
                grid = sel_p[:, 2048 - HALFR * k4 * HIS:2048].rearrange("p (k f t) -> p k f t", k=HALFR, f=k4)
                step(nc.vector.tensor_tensor(grid, oh[half][:, :, :].unsqueeze(2).to_broadcast([P, HALFR, k4, HIS]),
                                             per_hi[:, first:first + k4, :].unsqueeze(1).to_broadcast([P, HALFR, k4, HIS]), ALU.mult))
                step(nc.vector.tensor_reduce(out, grid, AX_X, ALU.add))

            def one_hot_hi(half, hs):
                return nc.vector.tensor_tensor(oh[half][:, :, :], hs.unsqueeze(2).to_broadcast([P, HALFR, HIS]),
                                               lanes.unsqueeze(1).to_broadcast([P, HALFR, HIS]), ALU.is_equal)

            def kept_at(r, half):
                return kept_rows[:, bass.ds(r * (ROUND * ROW) + half * (HALFR * ROW), HALFR * ROW)].rearrange("p (k f) -> p k f", f=ROW)

            def first_pass(r, keep):
                step, n = chained(m1_chain, r * M1 + 8, True)
                keep_step, kn = chained(kept_chain, r * KEEPS, True)
                if keep:
                    keep_step(nc.vector.tensor_copy(kept_hi[:, bass.ds(r * ROUND, ROUND)], g_hi[:, :]))
                for half in range(2):
                    hs = g_hi[:, half * HALFR:(half + 1) * HALFR]
                    if keep:
                        keep_step(one_hot_hi(half, hs))
                        pick(keep_step, half, 0, got[:, :, 0:HEADS])
                    step(nc.vector.tensor_tensor(oh_t[:, :, :], hs.unsqueeze(1).to_broadcast([P, HIS, HALFR]),
                                                 lanes.unsqueeze(2).to_broadcast([P, HIS, HALFR]), ALU.not_equal))
                    step(nc.vector.tensor_scalar(oh_t[:, :, :], oh_t[:, :, :], -BIG, None, ALU.mult))
                    dve.wait_ge((rows1_in, rows1_b)[half], (r + 1) * 16 * HALFR)
                    dve.sem_inc(passed, 1)
                    if half == 0:
                        dve.wait_ge(key1_in, r * 16 + 32)
                        dve.sem_inc(passed, 1)
                    decode(step, idx1_ready, halves[half])
                    grid = sel_p[:, 0:HIS * HEADS * HALFR].rearrange("p (t h k) -> p t h k", t=HIS, h=HEADS)
                    step(nc.vector.tensor_tensor(
                        grid, oh_t[:, :, :].unsqueeze(2).to_broadcast([P, HIS, HEADS, HALFR]),
                        rows_g[:, half, :, HE:ROW].rearrange("p k h -> p h k").unsqueeze(1).to_broadcast([P, HIS, HEADS, HALFR]), ALU.add))
                    if keep:
                        keep_step(nc.vector.tensor_copy(kept_at(r, half)[:, :, 0:HE], rows_g[:, half, :, 0:HE]))
                        keep_step(nc.vector.tensor_tensor(z2[:, half, :, :], rows_g[:, half, :, HE:ROW], got[:, :, 0:HEADS], ALU.add))
                        keep_step(nc.vector.scalar_tensor_tensor(kept_at(r, half)[:, :, HE:ROW], z2[:, half, :, :], 0.2,
                                                                 z2[:, half, :, :], ALU.mult, ALU.max))
                    dve.sem_inc(max1_done, 1)
                    step(nc.vector.tensor_reduce(cand[:, :, :], grid, AX_X, ALU.max))
                    step(nc.vector.tensor_tensor(s_max[:, :, :], s_max[:, :, :], cand[:, :, :], ALU.max))
                assert n[0] == M1 and kn[0] in (0, KEEPS)

            step, _ = chained(m1_chain)
            dve.wait_ge(key1_in, 16)
            for half in range(2):
                decode(step, idx1_ready, halves[half])
            dve.wait_ge(last_in, 16)
            run(nc.vector.tensor_tensor(cand[:, :, :], pen[:, :].unsqueeze(2).to_broadcast([P, HIS, HEADS]),
                                        last_row[:, HE:ROW].unsqueeze(1).to_broadcast([P, HIS, HEADS]), ALU.add))
            run(nc.vector.tensor_tensor(s_max[:, :, :], cand[:, :, :], a_src, ALU.max))
            with dve.Fori(0, kept_n) as r:
                first_pass(r, True)
            with dve.If(rest > 0):
                with dve.Fori(0, rest) as r:
                    first_pass(kept_n + r, False)
                dve.nop()
            run(nc.vector.tensor_tensor(cand[:, :, :], s_max[:, :, :], a_dst[:, :, :], ALU.add))
            run(nc.vector.scalar_tensor_tensor(e_max[:, :, :], cand[:, :, :], 0.2, cand[:, :, :], ALU.mult, ALU.max))
            run(nc.vector.tensor_copy(per_hi[:, HEADS:8, :], e_max[:, :, :].rearrange("p t h -> p h t")))
            dve.sem_inc(idx2_ready, 1)
            dve.sem_inc(used2, 2)
            M3 = 2 * (1 + 2 + 2 + 1)
            with dve.Fori(0, kept_n) as r:
                step, n = chained(m3_chain, r * M3, True)
                for half in range(2):
                    v = 2 * r + half
                    dve.wait_ge(spread2_b, v + 1)
                    dve.sem_inc(passed, 1)
                    step(one_hot_hi(half, kept_hi[:, bass.ds(r * ROUND + half * HALFR, HALFR)]))
                    pick(step, half, HEADS, got[:, :, HEADS:8])
                    step(nc.vector.tensor_tensor(z2[:, half, :, :], kept_at(r, half)[:, :, HE:ROW], got[:, :, HEADS:8], ALU.subtract))
                    step(nc.vector.tensor_scalar(z2[:, half, :, :], z2[:, half, :, :], 0.0, None, ALU.min))
                    dve.sem_inc(got2, 1)
                    dve.wait_ge(exp2, v + 1)
                    dve.sem_inc(passed, 1)
                    step(nc.vector.tensor_tensor(
                        vals2[:, half, :, HEADS:ROW].rearrange("p k (h e) -> p k h e", h=HEADS),
                        kept_at(r, half)[:, :, 0:HE].rearrange("p k (h e) -> p k h e", h=HEADS),
                        vals2[:, half, :, 0:HEADS].unsqueeze(3).to_broadcast([P, HALFR, HEADS, EXPERTS]), ALU.mult))
                    dve.sem_inc(vals_ready, 1)
                    dve.wait_ge(summed2, v + 1)
                    spread(nc.vector, half, 0).then_inc(spread2, 1)
                assert n[0] == M3
            M2 = 4 + 2 * 8
            with dve.If(rest > 0):
                with dve.Fori(0, rest) as r:
                    step, n = chained(m2_chain, r * M2)
                    dve.wait_ge(key2_in, r * 16 + 16)
                    decode(step, idx2_ready)
                    for half in range(2):
                        v = 2 * (kept_n + r) + half
                        dve.wait_ge(spread2_b, v + 2)
                        dve.sem_inc(passed, 1)
                        step(one_hot_hi(half, g_hi[:, half * HALFR:(half + 1) * HALFR]))
                        pick(step, half, 0, got[:, :, :])
                        dve.wait_ge((rows2_in, rows2_b)[half], (r + 1) * 16 * HALFR)
                        zs, vs = z2[:, half, :, :], vals2[:, half, :, :]
                        step(nc.vector.tensor_tensor(zs, rows_g[:, half, :, HE:ROW], got[:, :, 0:HEADS], ALU.add))
                        step(nc.vector.scalar_tensor_tensor(zs, zs, 0.2, zs, ALU.mult, ALU.max))
                        step(nc.vector.tensor_tensor(zs, zs, got[:, :, HEADS:8], ALU.subtract))
                        step(nc.vector.tensor_scalar(zs, zs, 0.0, None, ALU.min))
                        dve.sem_inc(got2, 1)
                        dve.wait_ge(exp2, v + 1)
                        step(nc.vector.tensor_tensor(
                            vs[:, :, HEADS:ROW].rearrange("p k (h e) -> p k h e", h=HEADS),
                            rows_g[:, half, :, 0:HE].rearrange("p k (h e) -> p k h e", h=HEADS),
                            vs[:, :, 0:HEADS].unsqueeze(3).to_broadcast([P, HALFR, HEADS, EXPERTS]), ALU.mult))
                        dve.sem_inc(used2, 1)
                        dve.wait_ge(summed2, v + 1)
                        spread(nc.vector, half, 0).then_inc(spread2, 1)
                        dve.wait_ge(summed2_b, v + 1)
                        spread_pairs(nc.vector, half, lambda: dve.wait_ge(pair_chain, v + 1)).then_inc(spread2_b, 1)
                        dve.wait_ge(spread2, v + 1)
                    assert n[0] == M2
                dve.nop()
            run(nc.vector.tensor_tensor(cand[:, :, :], a_src, a_dst[:, :, :], ALU.add))
            run(nc.vector.scalar_tensor_tensor(cand[:, :, :], cand[:, :, :], 0.2, cand[:, :, :], ALU.mult, ALU.max))
            run(nc.vector.tensor_tensor(cand[:, :, :], cand[:, :, :], e_max[:, :, :], ALU.subtract))
            dve.sem_inc(f_ask, 1)
            run(nc.vector.tensor_tensor(s_max[:, :, :], a_dst[:, :, :],
                                        last_row[:, HE:ROW].unsqueeze(1).to_broadcast([P, HIS, HEADS]), ALU.add))
            run(nc.vector.scalar_tensor_tensor(s_max[:, :, :], s_max[:, :, :], 0.2, s_max[:, :, :], ALU.mult, ALU.max))
            run(nc.vector.tensor_tensor(s_max[:, :, :], s_max[:, :, :], e_max[:, :, :], ALU.subtract))
            run(nc.vector.tensor_scalar(s_max[:, :, :], s_max[:, :, :], 0.0, None, ALU.min))
            dve.sem_inc(f_ask, 1)
            dve.wait_ge(f_exp, 2)
            run(nc.vector.tensor_tensor(s_max[:, :, :], s_max[:, :, :], to_last[:, :].unsqueeze(2).to_broadcast([P, HIS, HEADS]), ALU.mult))
            acc = spread_v[0][0][:, 0, :].rearrange("p (t f) -> p t f", f=ROW)
            dve.wait_ge(summed2, total * 2 + 2)
            dve.sem_inc(passed, 1)
            dve.wait_ge(summed2_b, total * 2 + 2)
            for b in range(2):
                run(nc.vector.tensor_copy(acc[:, b * (HIS // 2):(b + 1) * (HIS // 2), :],
                                          ps[b][:, 0:HIS // 2 * ROW].rearrange("p (t f) -> p t f", f=ROW)))
            den, agg = acc[:, :, 0:HEADS], acc[:, :, HEADS:ROW]
            by_head = lambda t: t.rearrange("p t (h e) -> p t h e", h=HEADS)
            for w, f in ((cand, feats), (s_max, last_row[:, 0:HE].unsqueeze(1).to_broadcast([P, HIS, HE]))):
                run(nc.vector.tensor_tensor(den, den, w[:, :, :], ALU.add))
                run(nc.vector.tensor_tensor(by_head(prod[:, :, :]), by_head(f), w[:, :, :].unsqueeze(3).to_broadcast([P, HIS, HEADS, EXPERTS]), ALU.mult))
                run(nc.vector.tensor_tensor(agg, agg, prod[:, :, :], ALU.add))
            run(nc.vector.tensor_scalar(cand[:, :, :], den, 1e-16, None, ALU.add))
            run(nc.vector.reciprocal(cand[:, :, :], cand[:, :, :]))
            run(nc.vector.tensor_tensor(by_head(prod[:, :, :]), by_head(agg), cand[:, :, :].unsqueeze(3).to_broadcast([P, HIS, HEADS, EXPERTS]), ALU.mult))
            row = lambda k: gat_v[:, k:k + 1, :].to_broadcast([P, HIS, HE])
            wide = lambda k, w=HE: stat[:, k, :].unsqueeze(2).to_broadcast([P, HIS, w])
            run(nc.vector.tensor_tensor(prod[:, :, :], prod[:, :, :], row(0), ALU.add))
            run(nc.vector.tensor_reduce(stat[:, 0, :], prod[:, :, :], AX_X, ALU.add))
            run(nc.vector.tensor_scalar(stat[:, 0, :], stat[:, 0, :], 1.0 / HE, None, ALU.mult))
            run(nc.vector.tensor_tensor(prod[:, :, :], prod[:, :, :], wide(0), ALU.subtract))
            run(nc.vector.tensor_tensor(agg, prod[:, :, :], prod[:, :, :], ALU.mult))
            run(nc.vector.tensor_reduce(stat[:, 1, :], agg, AX_X, ALU.add))
            run(nc.vector.tensor_scalar(stat[:, 1, :], stat[:, 1, :], 1.0 / HE, None, ALU.mult))
            dve.sem_inc(f_ask, 1)
            dve.wait_ge(f_exp, 3)
            run(nc.vector.reciprocal(stat[:, 1, :], stat[:, 1, :]))
            run(nc.vector.tensor_tensor(prod[:, :, :], prod[:, :, :], wide(1), ALU.mult))
            run(nc.vector.tensor_tensor(prod[:, :, :], prod[:, :, :], row(1), ALU.mult))
            run(nc.vector.tensor_tensor(prod[:, :, :], prod[:, :, :], row(2), ALU.add))
            run(nc.vector.tensor_reduce(score[:, :, :], prod[:, :, :].rearrange("p t (h e) -> p t e h", h=HEADS), AX_X, ALU.add))
            run(nc.vector.tensor_scalar(score[:, :, :], score[:, :, :], 1.0 / HEADS, None, ALU.mult))
            square = lambda k: pair[:, k, :, :].rearrange("p t (i j) -> p t i j", i=EXPERTS)
            other = score[:, :, :].unsqueeze(2).to_broadcast([P, HIS, EXPERTS, EXPERTS])
            mine = score[:, :, :].unsqueeze(3).to_broadcast([P, HIS, EXPERTS, EXPERTS])
            run(nc.vector.tensor_tensor(square(0), other, mine, ALU.is_gt))
            run(nc.vector.tensor_tensor(square(1), other, mine, ALU.is_equal))
            run(nc.vector.tensor_tensor(pair[:, 1, :, :], pair[:, 1, :, :],
                                        below[:, :, :].rearrange("p i j -> p (i j)").unsqueeze(1).to_broadcast([P, HIS, EXPERTS * EXPERTS]), ALU.mult))
            run(nc.vector.tensor_tensor(pair[:, 0, :, :], pair[:, 0, :, :], pair[:, 1, :, :], ALU.add))
            run(nc.vector.tensor_reduce(cand[:, :, :], square(0), AX_X, ALU.add))
            run(nc.vector.tensor_reduce(stat[:, 2, :], score[:, :, :], AX_X, ALU.max))
            run(nc.vector.tensor_tensor(gate[:, :, :], score[:, :, :], wide(2, EXPERTS), ALU.subtract))
            dve.sem_inc(f_ask, 1)
            dve.wait_ge(f_exp, 4)
            run(nc.vector.scalar_tensor_tensor(gate[:, :, :], cand[:, :, :], 1.5, gate[:, :, :], ALU.is_lt, ALU.mult))
            run(nc.vector.tensor_reduce(stat[:, 3, :], gate[:, :, :], AX_X, ALU.add))
            run(nc.vector.reciprocal(stat[:, 3, :], stat[:, 3, :]))
            run(nc.vector.tensor_tensor(gate[:, :, :], gate[:, :, :], wide(3, EXPERTS), ALU.mult))
            dve.sem_inc(gates_known, 1)
            dve.wait_ge(my_done, 2 + CHUNKS * EXPERTS)
            dve.sem_inc(gated, 2)
            def gate_outputs(i):
                for e in range(EXPERTS):
                    v = EXPERTS * i + e
                    dve.wait_ge(gates_ready, v + 1)
                    nc.vector.tensor_tensor(y_exp[e][:, i, :], y_exp[e][:, i, :], ps[6 + e % 2][:, :], ALU.mult).then_inc(gated, 1)

            def add_outputs(i):
                dve.wait_ge(gated_b, 3 * i + 3)
                nc.vector.tensor_tensor(X[:, i, :], X[:, i, :], y_exp[0][:, i, :], ALU.add).then_inc(res4, 1)

            gate_outputs(0)
            with dve.Fori(1, CHUNKS) as i:
                gate_outputs(i)
                add_outputs(i - 1)
            add_outputs(CHUNKS - 1)

        @block.tensor
        def _(pe):
            def mm(o, l, r, start, stop, **kw):
                return nc.tensor.matmul(o, l, r, start=start, stop=stop, **kw)

            def norm(ln, res, credit):
                pe.sem_inc(ln.var_ready, 2)
                for i in range(CHUNKS + 2):
                    if i < CHUNKS:
                        if res is not None:
                            pe.wait_ge(res, i + credit + 1)
                        pe.wait_ge(ln.centred, i + 1)
                        mm(ps[i % 2][:, :], mean_w[:, :], X[:, i, :], True, True).then_inc(ln.mean_ready, 1)
                    if i >= 2:
                        pe.wait_ge(ln.squared, i - 1)
                        for j in range(CHUNK // P):
                            t = (i - 2) * (CHUNK // P) + j
                            last = mm(ps[2][:, t:t + 1], sq[:, i % 2, j * P:(j + 1) * P], mean_w[:, 0:1], True, True)
                        last.then_inc(ln.var_ready, 1)
                pe.wait_ge(ln.inv_ready, 1)
                for i in range(CHUNKS):
                    pe.wait_ge(ln.normed, i + 1)
                    for j in range(CHUNK // P):
                        t = i * (CHUNK // P) + j
                        last = mm(ps[6 + i % 2][:, j * P:(j + 1) * P], inv[:, t:t + 1].to_broadcast([P, P]), ident[:, :], True, True)
                    last.then_inc(ln.spread, 1)

            pe.wait_ge(x_in, 16 * IMGS)
            pe.wait_ge(made, 10)
            norm(ln0, None, 0)
            pe.wait_ge(wa_in, WA)
            pe.wait_ge(padded, CHUNKS)
            pe.wait_ge(made, 21)

            def conv(w, m, done):
                with pe.Fori(0, IMGS) as n:
                    for h in range(2):
                        for k in range(TAPS):
                            dy, dx = divmod(k, 3)
                            last = mm(bank_of(2 * n + h, slice(0, m)), w[:, k, :],
                                      XP[:, n, HROWS * h + dy:HROWS * h + dy + HROWS, dx:dx + SIDE], k == 0, k == TAPS - 1)
                        last.then_inc(done, 1)

            conv(w_off, 64, off_ready)

            def broadcast(n, k, h):
                u = (n * TAPS + k) * 2 + h
                pe.wait_ge(abs_done, 2 * u + 2)
                mm(ps[h][:, :], sel[:, 2 * k, :], OFS[:, 2 * n + h, :], True, True)
                pe.wait_ge(ax_done, u + 1)
                mm(ps[2][:, :], sel[:, 2 * k + 1, :], OFS[:, 2 * n + h, :], True, True)
                pe.wait_ge(txm_done, u + 2)
                mm(ps[3][:, :], sel[:, k, :], MSK[:, 2 * n + h, :], True, True).then_inc(bc_ready, 1)

            def sample(n, k, h):
                u = (n * TAPS + k) * 2 + h
                for g in range(2):
                    v = 2 * u + g
                    pe.wait_ge(ten_done, v + 5)
                    for j in range(GROUP):
                        last = mm(ps[4 + h][:, :], YT[:, GROUP * g + j, k * P:(k + 1) * P], TEN[:, 2 * h + g, j, :], False, False,
                                  skip_group_check=True)
                    last.then_inc(main_done, 1)

            pe.wait_ge(wb_in, WB_)
            pe.wait_ge(off_done, 2 + CHUNKS)
            pe.wait_ge(msk_done, 1 + CHUNKS)
            pe.wait_ge(far_chain, 2)
            pe.wait_ge(left_known, 1)
            lefts = pe.value_load(num[0:1, N_LEFT:N_LEFT + 1], min_val=1, max_val=(ECOLS - KEPT1) // 8)
            mm(ps[7][:, 0:HIS], zero_b[:, 0:P], zero_b[:, 0:HIS], True, False, skip_group_check=True)
            pe.sem_inc(left_added, 1)
            with pe.Fori(0, lefts) as r:
                pe.wait_ge(left_coded, r * 7 + 7)
                for c in range(8):
                    last = mm(ps[7][:, 0:HIS], oh_lo[:, 0, c, :], oh_hi[:, 0, c, :], False, False, skip_group_check=True)
                last.then_inc(left_added, 1)
            pe.wait_ge(batches_known, 1)
            pe.sem_inc(piece_added, 2)

            def add_piece(n, k, h):
                pe.wait_ge(piece_made, PIECES * n + 2 * k + h + 1)
                for c in range(PIECE):
                    last = mm(ps[7][:, 0:HIS], oh_lo[:, h, c, :], oh_hi[:, h, c, :], k + h + c == 0,
                              2 * k + h == PIECES - 1 and c == PIECE - 1)
                last.then_inc(piece_added, 1)

            is_far = pe.value_load(num[0:1, N_FAR:N_FAR + 1], min_val=0, max_val=1)
            with pe.If(is_far > 0):
                pe.sem_inc(main_done, 4)
                with pe.Fori(0, IMGS) as n:
                    broadcast(n, 0, 0)
                    pe.wait_ge(res1, 2 * n + 2)
                    for h in range(2):
                        mm(ps[4 + h][:, :], zero_b[:, 0:P], zero_b[:, :], True, False, skip_group_check=True)
                    pe.wait_ge(own_ready, n + 1)
                    pe.wait_ge(shares_added, n + 1)
                    for q in range(3 * SRC_T):
                        t, g = divmod(q, 3)
                        w = min(CHUNK, TAPS * P - g * CHUNK)
                        pe.wait_ge(yt_done, 3 * SRC_T * n + q + 1)
                        mm(ps[6 + q % 2][:, 0:w], own_img[:, t * P:(t + 1) * P], w_dcn[:, g * CHUNK:g * CHUNK + w],
                           True, True).then_inc(yt_ready, 1)
                    pe.wait_ge(yt_done, 3 * SRC_T * (n + 1) + 2)
                    for k in range(TAPS):
                        broadcast(n, k, 1)
                        sample(n, k, 0)
                        if 2 * k < PIECES:
                            add_piece(n, k, 0)
                        if k + 1 < TAPS:
                            broadcast(n, k + 1, 0)
                        sample(n, k, 1)
                        if 2 * k < PIECES:
                            add_piece(n, k, 1)
                pe.nop()

            def near_broadcast(n, k, h):
                u = (n * TAPS + k) * 2 + h
                pe.wait_ge(abs_done, u + 1)
                mm(ps[h][:, :], sel[:, 2 * k, :], OFS[:, 2 * n + h, :], True, True)
                pe.wait_ge(ax_done, u + 1)
                mm(ps[2][:, :], sel[:, 2 * k + 1, :], OFS[:, 2 * n + h, :], True, True).then_inc(bc_ready, 1)
                pe.wait_ge(txm_done, u + 2)
                mm(ps[3][:, :], sel[:, k, :], MSK[:, 2 * n + h, :], True, True).then_inc(mk_ready, 1)

            def make_tap(n, k, h):
                pe.wait_ge(yt_done, n * (2 * TAPS) + 2 * k + h + 1)
                for j in range(4):
                    t = 4 * h + j
                    last = mm(ps[6][:, j * P:(j + 1) * P], own_img[:, t * P:(t + 1) * P], w_dcn[:, k % TAPS * P:(k % TAPS + 1) * P], True, True)
                last.then_inc(yt_ready, 1)

            def near_sample(n, k, h):
                u = (n * TAPS + k) * 2 + h
                pe.wait_ge(yt_done, n * (2 * TAPS) + 2 * k + 3)
                pe.wait_ge(ten_done, u + 3)
                pe.wait_ge(ten_pool, u + 3)
                for t, j, c, slot in near_tiles(h):
                    last = mm(ps[4 + h][:, j * P:(j + c) * P], YTN[:, k % RING, t, :],
                              near_w[(2 * k + h) % RING][:, slot:slot + 2 * c - 1:2, :], False, False, skip_group_check=True)
                last.then_inc(main_done, 1)

            with pe.If(is_far < 1):
                pe.sem_inc(main_done, RING)
                pe.wait_ge(own_ready, 1)
                for h in range(2):
                    make_tap(0, 0, h)
                with pe.Fori(0, IMGS) as n:
                    near_broadcast(n, 0, 0)
                    for k in range(TAPS):
                        for h in range(2):
                            u = 2 * k + h
                            if h == 0:
                                near_broadcast(n, k, 1)
                            elif k + 1 < TAPS:
                                near_broadcast(n, k + 1, 0)
                            if u == 0:
                                pe.wait_ge(res1, 2 * n + 2)
                                for b in range(2):
                                    mm(ps[4 + b][:, :], zero_b[:, 0:P], zero_b[:, :], True, False, skip_group_check=True)
                            if u == 1:
                                pe.wait_ge(shares_added, n + 1)
                            if u == 2 * TAPS - 2:
                                pe.wait_ge(own_ready, n + 2)
                            make_tap(n, k + 1, h)
                            if 0 < u <= PIECES:
                                add_piece(n, *divmod(u - 1, 2))
                            near_sample(n, k, h)
                pe.nop()
            norm(ln1, res1, 2)
            pe.wait_ge(wrb_done, 1)
            with pe.Fori(0, IMGS) as n:
                for h in range(2):
                    i = 2 * n + h
                    pe.wait_ge(ln1.normed, i + 3)
                    pe.wait_ge(rw_done, i + 1)
                    mm(ps[h][:, :], wr_b[:, :], T[:, i, :], True, True).then_inc(rw_ready, 1)
            with pe.Fori(0, IMGS) as n:
                for h in range(2):
                    i = 2 * n + h
                    for c in range(HID):
                        pe.wait_ge(gelu_done, HID * i + c + 1)
                        mm(ps[4 + c % 2][:, :], f_w1[:, c * P:(c + 1) * P], T[:, i, :], True, True).then_inc(h_ready, 1)
                    pe.wait_ge(gelu_done, HID * (i + 1) + 2)
                    pe.wait_ge(yf_done, i + 1)
                    for c in range(HID):
                        last = mm(ps[6 + h][:, :], f_w2[:, c, :], hid[h][:, c, :], c == 0, c == HID - 1)
                    last.then_inc(y_ready, 1)
                pe.wait_ge(cmp_done, SRC_T * (n + 1))
                pe.wait_ge(kept_done, 2 * n + 2)
                for h in range(2):
                    for t in range(SRC_T):
                        last = mm(ps[2 + h][:, :], ones_b[:, :], cmp_b[:, t, h * CHUNK:(h + 1) * CHUNK],
                                  t == 0, t == SRC_T - 1)
                last.then_inc(rank_ready, 1)
            norm(ln2, res2, 0)
            batches = pe.value_load(num[0:1, N_BATCH:N_BATCH + 1], min_val=1, max_val=MAX_BATCHES)
            pe.sem_inc(turned, 1)
            with pe.Fori(0, batches) as b:
                pe.wait_ge(batch_in, b * 16 + 16)
                for q in range(BATCH // 4):
                    pe.wait_ge(turned_out, b * (BATCH // 4) + q + 1)
                    for j in range(4):
                        last = nc.tensor.transpose(ps[4 + q % 2][:, j * P:(j + 1) * P],
                                                   batch_k[:, 4 * q + j:4 * q + j + 1].to_broadcast([P, P]), ident[:, :])
                    last.then_inc(turned, 1)
            pe.wait_ge(turned_out, batches * (BATCH // 4) + 2)
            pe.sem_inc(passed, 1)
            pe.wait_ge(padded, 2 * CHUNKS)
            conv(w_conv, P, cv_ready)
            pe.wait_ge(rounds_known, 1)
            pe.wait_ge(res3, 2 + 3)
            norm(ln3, res3, 2)
            pe.wait_ge(wc_in, WC)
            pe.wait_ge(ln3.normed, 2 + CHUNKS)
            for t in range(TILES):
                i, j = divmod(t, CHUNK // P)
                last = mm(ps[0][:, t * HE:(t + 1) * HE], T[:, i, j * P:(j + 1) * P], w_gat[:, :], True, True)
            last.then_inc(feat_ready, 1)
            def hidden(i, e):
                v = EXPERTS * i + e
                for c in range(2):
                    pe.wait_ge(mid_done, 2 * v + c + 1)
                    mm(ps[2 + c][:, :], m_w1[:, e, c * P:(c + 1) * P], T[:, i, :], True, True).then_inc(mid_ready, 1)

            def expert_out(i, e):
                v = EXPERTS * i + e
                pe.wait_ge(mid_done, 2 * v + 4)
                pe.wait_ge(my_done, v + 1)
                for c in range(2):
                    last = mm(ps[4 + e % 2][:, :], m_w2[:, e, c, :], mid[:, e % 2, c, :], c == 0, c == 1)
                last.then_inc(my_ready, 1)

            pe.wait_ge(wd_in, 32)
            pe.sem_inc(my_ready, 2)
            with pe.Fori(0, CHUNKS) as i:
                hidden(i, 0)
                for e in range(1, EXPERTS):
                    hidden(i, e)
                    expert_out(i, e - 1)
                expert_out(i, EXPERTS - 1)
            pe.wait_ge(t_chain, 3)
            wide_hi = HIS // 2 * ROW
            for b in range(2):
                mm(ps[b][:, 0:wide_hi], zero_b[:, 0:P], zero_b[:, 0:wide_hi], True, False, skip_group_check=True)
            pe.sem_inc(summed2, 2)
            pe.sem_inc(summed2_b, 2)
            total = pe.value_load(num[0:1, N_ALL:N_ALL + 1], min_val=1, max_val=MAX_ROUNDS)
            with pe.Fori(0, total) as r:
                for g in range(2):
                    for half in range(2):
                        pe.wait_ge((spread2, spread2_b)[g], 2 * r + half + 1 + 2 * g)
                        for k in range((GROUP, GROUP // 2)[g]):
                            for b in range(2):
                                last = mm(ps[b][:, 0:wide_hi], ident[:, :], spread_v[g][half][:, k, b * wide_hi:(b + 1) * wide_hi],
                                          False, False, skip_group_check=True)
                        last.then_inc((summed2, summed2_b)[g], 1)
            pe.wait_ge(gates_known, 1)
            for i in range(CHUNKS):
                for e in range(EXPERTS):
                    pe.wait_ge(gated, EXPERTS * i + e + 1)
                    for j in range(CHUNK // P):
                        t = i * (CHUNK // P) + j
                        last = nc.tensor.transpose(ps[6 + e % 2][:, j * P:(j + 1) * P],
                                                   gate[:, t, e:e + 1].to_broadcast([P, P]), ident[:, :])
                    last.then_inc(gates_ready, 1)

_WEIGHTS = {
    "w_off": ("L0_conv_offset_w", (P, TAPS, 3 * TAPS)), "b_off": ("L0_conv_offset_b", (3 * TAPS,)),
    "w_dcn": ("L0_conv_dcn_w", (P, TAPS * P)), "wr": ("L0_ffn_wr", (P, 1)), "br": ("L0_ffn_br", (1,)),
    "f_w1": ("L0_ffn_w1", (P, HID * P)), "f_b1": ("L0_ffn_b1", (P, HID)),
    "edges": ("L1_ffn_edge_index", (2, EDGES)), "w_gat": ("L1_ffn_W_gat", (P, HE)),
    "att_src": ("L1_ffn_att_src", (HE,)), "att_dst": ("L1_ffn_att_dst", (HE,)), "b_gat": ("L1_ffn_b_gat", (HE,)),
    "ln_gamma": ("L1_ffn_ln_gamma", (HE,)), "ln_beta": ("L1_ffn_ln_beta", (HE,)),
    "m_w1": ("L1_ffn_W1", (EXPERTS, P, 2 * P)), "m_b1": ("L1_ffn_b1", (P, EXPERTS, 2)),
    "m_w2": ("L1_ffn_W2", (EXPERTS, 2 * P, P)), "m_b2": ("L1_ffn_b2", (P, EXPERTS)),
    "f_w2": ("L0_ffn_w2", (HID * P, P)), "f_b2": ("L0_ffn_b2", (P,)), "w_conv": ("L1_conv_weight", (P, TAPS, P)),
}


def kernel(**inputs):
    import concourse.bacc as _bacc
    from concourse.bass_utils import run_bass_kernel_spmd as _run

    nc = _bacc.Bacc("TRN2", target_bir_lowering=False, num_devices=1)
    y, x = np.divmod(np.arange(POS), SIDE)
    ky, kx = np.divmod(np.arange(TAPS), 3)
    base = np.stack([y[None] - 1 + ky[:, None], x[None] - 1 + kx[:, None]], 1).reshape(2 * TAPS, POS)
    rows = np.arange(P)[:, None] // SIDE + np.arange(SRC_T)[None] * (P // SIDE)
    arrays = {"base": base.astype(np.float32), "neg_y": -rows.astype(np.float32),
              "neg_x": -(np.arange(P)[:, None] % SIDE).astype(np.float32), "x": np.asarray(inputs["x"])}
    for name, (source, shape) in _WEIGHTS.items():
        w = np.asarray(inputs[source])
        if w.ndim == 4:
            w = w.reshape(w.shape[0], P, TAPS).transpose(1, 2, 0)
        elif name == "f_b1":
            w = w.reshape(HID, P).T
        elif name == "m_b1":
            w = w.reshape(EXPERTS, 2, P).transpose(2, 0, 1)
        elif name == "m_b2":
            w = w.T
        arrays[name] = np.ascontiguousarray(w).reshape(shape)
    a = {k: nc.dram_tensor(f"in_{k}", v.shape, mybir.dt.from_np(v.dtype), kind="ExternalInput").ap()
         for k, v in arrays.items()}
    out = nc.dram_tensor("out_x", (IMGS, P, SIDE, SIDE), F32, kind="ExternalOutput").ap()
    metaformer_kernel(nc, a, out)
    r = _run(nc, [{f"in_{k}": v for k, v in arrays.items()}], core_ids=[0])
    return r.results[0]["out_x"]
```
